# Optimizing a Trainium2 kernel written in Bass

```python
import numpy as np
import jax
import jax.numpy as jnp

def _softmax(x, axis=-1):
    return jax.nn.softmax(x, axis=axis)

def _gelu(x):
    return jax.nn.gelu(x, approximate=True)

def _silu(x):
    return jax.nn.silu(x)

def _sigmoid(x):
    return jax.nn.sigmoid(x)

def _layernorm(x, axis=-1, eps=1e-05):
    m = jnp.mean(x, axis=axis, keepdims=True)
    v = jnp.var(x, axis=axis, keepdims=True)
    return (x - m) / jnp.sqrt(v + eps)

def _scatter_add(tgt, idx, src, axis=0):
    return tgt.at[idx].add(src)

def _segment_sum(src, seg, n):
    return jax.ops.segment_sum(src, seg, n)
kernel_name = 'mk_xattn_ffn_d1_seqx_r4_3fc444'

def setup_inputs(seed: int=0):
    np.random.seed(seed)
    _w = jnp.asarray

    def _rec_inputs():
        import jax
        import jax.numpy as jnp
        _rk = jax.random.key(seed)
        x = -1.394e-06 + 0.9999 * jax.random.normal(jax.random.fold_in(_rk, 1), (128, 128, 256), jnp.float32)
        _lenS = 128 - jax.random.randint(jax.random.fold_in(_rk, 7), (128,), 0, max(1, 128 // 4) + 1, jnp.int32)
        _lenS2 = 128 - jax.random.randint(jax.random.fold_in(_rk, 8), (128,), 0, max(1, 128 // 4) + 1, jnp.int32)
        _ctx_1024P = jax.random.normal(jax.random.fold_in(_rk, 11), (128, 16, 256), jnp.float32)
        _ctx_1024c = jax.random.dirichlet(jax.random.fold_in(_rk, 511), 0.3 * jnp.ones((16,), jnp.float32), (128, 128))
        _ctx_1024t = jnp.einsum('bsk,bkd->bsd', _ctx_1024c, _ctx_1024P)
        _ctx_1024t = _ctx_1024t * jax.lax.rsqrt(jnp.mean(jnp.square(_ctx_1024t)) + 1e-12) * 0.953939
        ctx_1024 = -0.000292821 + 1.00034 * (_ctx_1024t + 0.3 * jax.random.normal(jax.random.fold_in(_rk, 611), (128, 128, 256), jnp.float32))
        return (x, ctx_1024)
    x, ctx_1024 = _rec_inputs()

    def _L0_xattn_setup():
        import jax, jax.numpy as jnp
        import numpy as np
        B, N, T = (2, 512, 512)
        ENC, DEC, HID = (256, 256, 256)
        HEADS = 16
        DH = HID // HEADS
        HALF = DH // 2
        LAMBDA_INIT = 0.8
        key = jax.random.key(seed)
        ks = jax.random.split(key, 9)
        s = 0.02
        return {'encoder_feature': jax.random.normal(ks[0], (B, N, ENC), jnp.float32), 'decoder_feature': jax.random.normal(ks[1], (B, T, DEC), jnp.float32), 'Wq': jax.random.normal(ks[2], (HID, DEC), jnp.float32) * s, 'Wk': jax.random.normal(ks[3], (HID, ENC), jnp.float32) * s, 'Wv': jax.random.normal(ks[4], (HID, ENC), jnp.float32) * s, 'lambda_q1': jax.random.normal(ks[5], (HALF,), jnp.float32) * 0.1, 'lambda_q2': jax.random.normal(ks[6], (HALF,), jnp.float32) * 0.1, 'lambda_k1': jax.random.normal(ks[7], (HALF,), jnp.float32) * 0.1, 'lambda_k2': jax.random.normal(ks[8], (HALF,), jnp.float32) * 0.1}
    _L0_xattn_all = _L0_xattn_setup()
    _L0_xattn_in = {k: v for k, v in _L0_xattn_all.items() if k in ('Wq', 'Wk', 'Wv', 'lambda_q1', 'lambda_q2', 'lambda_k1', 'lambda_k2')}
    del _L0_xattn_all

    def _L0_ffn_setup():
        import jax, jax.numpy as jnp
        import numpy as np
        H = 256
        M = 128
        E = 16
        TOP_K = 2
        SCALE = 2.5
        NORM_TOPK = True
        B, S = (1, 256)

        def _moe(x, gate_w, w_gate, w_up, w_down, ws_gate, ws_up, ws_down):
            T = x.shape[0]
            shared = jax.nn.silu(x @ ws_gate) * (x @ ws_up) @ ws_down
            scores = jax.nn.sigmoid(x.astype(jnp.float32) @ gate_w.T.astype(jnp.float32))
            topk_w, topk_idx = jax.lax.top_k(scores, TOP_K)
            if NORM_TOPK and TOP_K > 1:
                topk_w = topk_w / (topk_w.sum(-1, keepdims=True) + 1e-20)
            topk_w = topk_w * SCALE
            route = jnp.zeros((T, E), topk_w.dtype).at[jnp.arange(T)[:, None], topk_idx].set(topk_w)
            g = jnp.einsum('th,ehm->etm', x, w_gate)
            u = jnp.einsum('th,ehm->etm', x, w_up)
            eo = jnp.einsum('etm,emh->eth', jax.nn.silu(g) * u, w_down)
            routed = jnp.einsum('te,eth->th', route.astype(x.dtype), eo)
            return routed + shared
        key = jax.random.key(seed)
        ks = jax.random.split(key, 8)
        std = 0.02
        return {'hidden_states': jax.random.normal(ks[0], (B, S, H), jnp.float32), 'gate_w': jax.random.normal(ks[1], (E, H), jnp.float32) * std, 'w_gate': jax.random.normal(ks[2], (E, H, M), jnp.float32) * std, 'w_up': jax.random.normal(ks[3], (E, H, M), jnp.float32) * std, 'w_down': jax.random.normal(ks[4], (E, M, H), jnp.float32) * std, 'ws_gate': jax.random.normal(ks[5], (H, M), jnp.float32) * std, 'ws_up': jax.random.normal(ks[6], (H, M), jnp.float32) * std, 'ws_down': jax.random.normal(ks[7], (M, H), jnp.float32) * std}
    _L0_ffn_all = _L0_ffn_setup()
    _L0_ffn_in = {k: v for k, v in _L0_ffn_all.items() if k in ('gate_w', 'w_gate', 'w_up', 'w_down', 'ws_gate', 'ws_up', 'ws_down')}
    del _L0_ffn_all
    return {'x': x, 'ctx_1024': ctx_1024, 'L0_xattn_Wq': _L0_xattn_in['Wq'], 'L0_xattn_Wk': _L0_xattn_in['Wk'], 'L0_xattn_Wv': _L0_xattn_in['Wv'], 'L0_xattn_lambda_q1': _L0_xattn_in['lambda_q1'], 'L0_xattn_lambda_q2': _L0_xattn_in['lambda_q2'], 'L0_xattn_lambda_k1': _L0_xattn_in['lambda_k1'], 'L0_xattn_lambda_k2': _L0_xattn_in['lambda_k2'], 'L0_ffn_gate_w': _L0_ffn_in['gate_w'], 'L0_ffn_w_gate': _L0_ffn_in['w_gate'], 'L0_ffn_w_up': _L0_ffn_in['w_up'], 'L0_ffn_w_down': _L0_ffn_in['w_down'], 'L0_ffn_ws_gate': _L0_ffn_in['ws_gate'], 'L0_ffn_ws_up': _L0_ffn_in['ws_up'], 'L0_ffn_ws_down': _L0_ffn_in['ws_down']}

def reference(x, ctx_1024, L0_xattn_Wq, L0_xattn_Wk, L0_xattn_Wv, L0_xattn_lambda_q1, L0_xattn_lambda_q2, L0_xattn_lambda_k1, L0_xattn_lambda_k2, L0_ffn_gate_w, L0_ffn_w_gate, L0_ffn_w_up, L0_ffn_w_down, L0_ffn_ws_gate, L0_ffn_ws_up, L0_ffn_ws_down):
    import jax
    import jax.numpy as jnp

    def _L0_xattn_ref(encoder_feature, decoder_feature, Wq, Wk, Wv, lambda_q1, lambda_q2, lambda_k1, lambda_k2):
        import jax, jax.numpy as jnp
        import numpy as np
        B, N, T = (2, 512, 512)
        ENC, DEC, HID = (256, 256, 256)
        HEADS = 16
        DH = HID // HEADS
        HALF = DH // 2
        LAMBDA_INIT = 0.8
        b, n, _ = encoder_feature.shape
        _, t, _ = decoder_feature.shape
        hid = Wq.shape[0]
        dh = hid // HEADS
        half = dh // 2
        q = decoder_feature @ Wq.T
        k = encoder_feature @ Wk.T
        v = encoder_feature @ Wv.T
        q = q.reshape(b, t, 2 * HEADS, half).transpose(0, 2, 1, 3)
        k = k.reshape(b, n, 2 * HEADS, half).transpose(0, 2, 1, 3)
        v = v.reshape(b, n, HEADS, dh).transpose(0, 2, 1, 3)
        lam = jnp.exp(jnp.sum(lambda_q1 * lambda_k1)) - jnp.exp(jnp.sum(lambda_q2 * lambda_k2)) + LAMBDA_INIT
        scale = 1.0 / jnp.sqrt(jnp.float32(half))
        att = jax.nn.softmax(jnp.einsum('bhtd,bhnd->bhtn', q, k) * scale, axis=-1)
        att = att.reshape(b, HEADS, 2, t, n)
        att = att[:, :, 0] - lam * att[:, :, 1]
        out = jnp.einsum('bhtn,bhnd->bhtd', att, v)
        return out.transpose(0, 2, 1, 3).reshape(b, t, hid)

    def _L0_ffn_ref(hidden_states, gate_w, w_gate, w_up, w_down, ws_gate, ws_up, ws_down):
        import jax, jax.numpy as jnp
        import numpy as np
        H = 256
        M = 128
        E = 16
        TOP_K = 2
        SCALE = 2.5
        NORM_TOPK = True
        B, S = (1, 256)

        def _moe(x, gate_w, w_gate, w_up, w_down, ws_gate, ws_up, ws_down):
            T = x.shape[0]
            shared = jax.nn.silu(x @ ws_gate) * (x @ ws_up) @ ws_down
            scores = jax.nn.sigmoid(x.astype(jnp.float32) @ gate_w.T.astype(jnp.float32))
            topk_w, topk_idx = jax.lax.top_k(scores, TOP_K)
            if NORM_TOPK and TOP_K > 1:
                topk_w = topk_w / (topk_w.sum(-1, keepdims=True) + 1e-20)
            topk_w = topk_w * SCALE
            route = jnp.zeros((T, E), topk_w.dtype).at[jnp.arange(T)[:, None], topk_idx].set(topk_w)
            g = jnp.einsum('th,ehm->etm', x, w_gate)
            u = jnp.einsum('th,ehm->etm', x, w_up)
            eo = jnp.einsum('etm,emh->eth', jax.nn.silu(g) * u, w_down)
            routed = jnp.einsum('te,eth->th', route.astype(x.dtype), eo)
            return routed + shared
        b, s, h = hidden_states.shape
        x = hidden_states.reshape(-1, h)
        out = _moe(x, gate_w, w_gate, w_up, w_down, ws_gate, ws_up, ws_down)
        return out.reshape(b, s, h)
    x = x + _L0_xattn_ref(ctx_1024, _layernorm(x, axis=-1), L0_xattn_Wq, L0_xattn_Wk, L0_xattn_Wv, L0_xattn_lambda_q1, L0_xattn_lambda_q2, L0_xattn_lambda_k1, L0_xattn_lambda_k2)
    x = x + _L0_ffn_ref(_layernorm(x, axis=-1), L0_ffn_gate_w, L0_ffn_w_gate, L0_ffn_w_up, L0_ffn_w_down, L0_ffn_ws_gate, L0_ffn_ws_up, L0_ffn_ws_down)
    return x

_drawn_inputs = setup_inputs


def setup_inputs(seed=0):
    import zlib

    import numpy as np

    out = dict(_drawn_inputs(seed))
    spreads = {}
    factors = {'L0_xattn_Wq': 6.906,
     'L0_xattn_Wk': 6.917,
     'L0_xattn_lambda_q1': 8.0,
     'L0_xattn_lambda_q2': 8.0,
     'L0_xattn_lambda_k1': 8.0,
     'L0_xattn_lambda_k2': 6.544,
     'L0_ffn_gate_w': 2.865,
     'L0_ffn_w_gate': 2.703,
     'L0_ffn_w_up': 2.671,
     'L0_ffn_w_down': 2.67,
     'L0_ffn_ws_gate': 4.845,
     'L0_ffn_ws_up': 4.754,
     'L0_ffn_ws_down': 4.774}
    for name, (base, spread) in spreads.items():
        noise = np.random.default_rng([zlib.crc32(name.encode()), seed]).standard_normal(out[name].shape)
        drawn = base * np.exp(spread * noise) if base else spread * noise
        out[name] = jnp.asarray(drawn.astype(out[name].dtype))
    for name, factor in factors.items():
        out[name] = (out[name] * factor).astype(out[name].dtype)
    return out
```

```python
from contextlib import ExitStack

import concourse.bass as bass
from concourse import mybir

ALU = mybir.AluOpType
ACT = mybir.ActivationFunctionType
AX = mybir.AxisListType
F32 = mybir.dt.float32
BF16 = mybir.dt.bfloat16
U32 = mybir.dt.uint32
I32 = mybir.dt.int32

P = 128
HEADS = 16
SUB = 2 * HEADS
PARTS = 3
ROWS = 48
KROWS = ROWS + 2
CHUNK = 4
NCH = 2 * SUB // CHUNK
WIDE_HEADS = 7
LAMBDA_INIT = 0.8
EPS = 1e-5
ROUTE_SCALE = 2.5
TOPK = 2

MAX_SLOTS = {5: [0], 6: [1], 7: [2], 8: [3, 4], 9: [5], 10: [6, 7], 11: [8], 12: [9, 10], 13: [11], 14: [12, 13],
             15: [14, 15]}


class Step:

    def __init__(self, k, off, unroll=2):
        self.k, self.off, self.unroll = k, off, unroll

    def plus(self, n):
        return Step(self.k, self.off + n, self.unroll)

    def idx(self):
        return self.off if self.k is None else self.k * self.unroll + self.off

    def par(self):
        return self.off % 2

    def is_in(self, lo, hi):
        return self.k is not None or lo <= self.off < hi


def program(nc, x, ctx, lq1, lk1, lq2, lk2, wqT, wkT, wvT, gate_wT, w_gu, w_dn, ws_gu, ws_dn, out):
    NB, _, D = x.shape
    NS = NB // 2
    T = NB * P
    NT = TOPK * T // P + gate_wT.shape[-1]
    E = gate_wT.shape[-1]
    CAP = T
    DK = D // P
    SHH = SUB // 2
    DH = D // HEADS
    HALF = DH // 2
    SW = 2 * P
    HID = w_dn.shape[0]
    VW = 2 * HEADS * (DH + 1)
    WIDE = WIDE_HEADS * (DH + 1)
    assert NS % 2 == 0 and NB >= 28 and CAP < 32768 and DK == 2 and HALF * SHH == P and HID == P and NT <= 512

    x_g = x.rearrange("(g u) p d -> g p u d", u=2)
    c_g = ctx.rearrange("(g u) p d -> g p u d", u=2)
    x2_dram = nc.dram_tensor("x2_dram", (NB, P, D), F32, kind="Internal").ap()
    x2_g = x2_dram.rearrange("(g u) p d -> g p u d", u=2)
    parts_dram = nc.dram_tensor("parts_dram", (2, 2, 2, PARTS, P, SW), BF16, kind="Internal").ap()
    max_dram = nc.dram_tensor("max_dram", (2, 2, 2, 2, SHH, P), BF16, kind="Internal").ap()
    N_ROWS = E * CAP
    rows_dram = nc.dram_tensor("rows_dram", (N_ROWS, D), F32, kind="Internal").ap()
    routed_dram = nc.dram_tensor("routed_dram", (NT * P, D), F32, kind="Internal").ap()

    with ExitStack() as st:
        def sb(name, shape, dt=F32):
            return st.enter_context(nc.sbuf_tensor(name, shape, dt))

        def ps(name):
            return st.enter_context(nc.psum_tensor(name, [P, 512], F32))

        def sem(name):
            return st.enter_context(nc.semaphore(name))

        st_ps = [ps(f"st_ps{i}") for i in range(2)]
        mx_ps = [ps(f"mx_ps{i}") for i in range(2)]
        o_ps = [ps(f"o_ps{i}") for i in range(2)]
        ms_ps = [ps(f"ms_ps{i}") for i in range(2)]
        tp_ps, gu_ps, hp_ps, eo_ps = st_ps, mx_ps, o_ps, ms_ps

        wq_sb = sb("wq_sb", [P, DK, D])
        wk_sb = sb("wk_sb", [P, DK, D])
        wv_sb = sb("wv_sb", [P, DK, D])
        gw_sb = sb("gw_sb", [P, DK, E])
        lam_in = sb("lam_in", [P, 4, HALF])
        lam_p = sb("lam_p", [P, 2, HALF])
        lam_s = sb("lam_s", [P, 2])
        lam_e = sb("lam_e", [P, 2])
        coef = sb("coef", [P, SHH])
        ident = sb("ident", [P, P])
        identb = sb("identb", [P, P], BF16)
        upper = sb("upper", [P, P], BF16)
        onesb = sb("onesb", [P, P], BF16)
        iota_e = sb("iota_e", [P, E])
        neghalf = sb("neghalf", [P, 2])

        x_in = sb("x_in", [P, 2, D])
        c_in = sb("c_in", [P, 2, D])
        x_res = [sb(f"x_res{i}", [P, 2, D]) for i in range(2)]
        xn = sb("xn", [P, 2, D])
        xnT = sb("xnT", [P, DK, SW])
        cT = [sb(f"cT{i}", [P, DK, SW]) for i in range(2)]
        qp = sb("qp", [P, PARTS, 512], BF16)
        kp = sb("kp", [P, PARTS, 512], BF16)
        q_rest = sb("q_rest", [P, 512])
        k_rest = sb("k_rest", [P, 512])
        q_st = [sb(f"q_st{i}", [P, SHH, SW], BF16) for i in range(2)]
        k_st = [sb(f"k_st{i}", [P, SHH, SW], BF16) for i in range(2)]
        v_sb = [sb(f"v_sb{i}", [P, VW + WIDE]) for i in range(2)]
        prob = [sb(f"prob{i}", [P, 512]) for i in range(4)]
        mx = sb("mx", [P, 2, SUB])
        mxp = sb("mxp", [P, 2, 2 * SUB], BF16)
        mxT = [sb(f"mxT{i}", [2 * SUB, P], BF16) for i in range(2)]
        rl = sb("rl", [P, SHH])
        rlc = sb("rlc", [P, SHH])
        o_sc = [sb(f"o_sc{i}", [P, SHH, DH]) for i in range(2)]
        att = sb("att", [P, SHH // 2, DH])
        x2 = [sb(f"x2_{i}", [P, 2, D]) for i in range(2)]
        h2 = [sb(f"h2_{i}", [P, 2, D]) for i in range(2)]
        h2T = sb("h2T", [P, DK, SW])
        bs1 = sb("bs1", [P, 2, 6])
        mv1 = sb("mv1", [P, 2, 2])
        ve1 = sb("ve1", [P, 2])
        rs1 = sb("rs1", [P, 2])
        bs2 = sb("bs2", [P, 2, 6])
        mv2 = sb("mv2", [P, 2, 2])
        ve2 = sb("ve2", [P, 2])
        rs2 = sb("rs2", [P, 2])
        ez = sb("ez", [P, 2 * E])
        ez1 = sb("ez1", [P, 2 * E])
        score = sb("score", [P, 2, E])
        top = sb("top", [P, 2, 8])
        topi = sb("topi", [P, 2, 8], U32)
        topf = sb("topf", [P, 2, TOPK])
        hot = sb("hot", [P, 2, TOPK, E])
        hots = sb("hots", [P, 2, E], BF16)
        den = sb("den", [P, 2])
        den1 = sb("den1", [P, 2])
        rden = sb("rden", [P, 2])
        route_w = sb("route_w", [P, NS, 2 * TOPK])
        base = sb("base", [P, 2, E])
        pb = sb("pb", [P, 2, E])
        hotp = sb("hotp", [P, 2, TOPK, E])
        posf = sb("posf", [P, 2 * TOPK])
        posi = [sb(f"posi{i}", [P, 2 * TOPK], U32) for i in range(2)]
        pos_f = sb("pos_f", [P, NS, 2 * TOPK])

        w_gu_sb = sb("w_gu_sb", [P, E, DK, 2 * HID])
        w_dn_sb = sb("w_dn_sb", [P, E, D])
        ws_gu_sb = sb("ws_gu_sb", [P, DK, 2 * HID])
        ws_dn_sb = sb("ws_dn_sb", [P, D])
        zeros = sb("zeros", [P, D])
        cap_e = sb("cap_e", [P, E])
        count = sb("count", [P, E])
        upto = sb("upto", [E, E])
        tiles_i = sb("tiles_i", [E, 1], I32)
        tiles_s = sb("tiles_s", [E, 1], I32)
        tiles_n = sb("tiles_n", [E, 1])
        last_t = sb("last_t", [E, 1])
        one_skip = sb("one_skip", [E, 2])
        tile_i = sb("tile_i", [P, E], I32)
        tile_s = sb("tile_s", [P, E], I32)
        tile_f = sb("tile_f", [P, E])
        skip = sb("skip", [P, E])
        shift = sb("shift", [P, NS * 2 * TOPK])
        cut = sb("cut", [P, NS * 2 * TOPK])
        pos_all = sb("pos_all", [P, NS, 2 * TOPK], U32)
        iota_t = sb("iota_t", [E, NT])
        past = sb("past", [E, NT])
        expert_f = sb("expert_f", [1, NT])
        expert_tab = sb("expert_tab", [1, NT], I32)
        full = sb("full", [1, E])
        room = sb("room", [1, E])
        least = sb("least", [1, 1])
        row_f = sb("row_f", [1, NT])
        row_d = sb("row_d", [1, NT])
        row_tab = sb("row_tab", [1, NT], I32)
        pad_tab = sb("pad_tab", [1, E], I32)
        tok_in = [sb(f"tok_in{i}", [P, D]) for i in range(8)]
        rows_T = [sb(f"rows_T{i}", [P, DK, P]) for i in range(2)]
        gate = [sb(f"gate{i}", [P, HID]) for i in range(2)]
        hid = [sb(f"hid{i}", [P, HID]) for i in range(2)]
        hid_T = [sb(f"hid_T{i}", [P, P]) for i in range(2)]
        res = [sb(f"res{i}", [P, D]) for i in range(4)]
        bs3 = [sb(f"bs3_{i}", [P, 6]) for i in range(2)]
        mv3 = [sb(f"mv3_{i}", [P, 2]) for i in range(2)]
        ve3 = [sb(f"ve3_{i}", [P, 1]) for i in range(2)]
        rs3 = [sb(f"rs3_{i}", [P, 1]) for i in range(2)]
        h3 = [sb(f"h3_{i}", [P, D]) for i in range(2)]
        pos_r = [sb(f"pos_r{i}", [P, TOPK], U32) for i in range(2)]
        w_r = [sb(f"w_r{i}", [P, TOPK]) for i in range(2)]
        got = [sb(f"got{i}", [P, TOPK, D]) for i in range(4)]
        acc0 = [sb(f"acc0_{i}", [P, D]) for i in range(2)]
        acc1 = [sb(f"acc1_{i}", [P, D]) for i in range(2)]

        d_w, d_x, d_c = sem("d_w"), sem("d_x"), sem("d_c")
        d_res = [sem(f"d_res{i}") for i in range(2)]
        d_qw, d_kw, d_stk = sem("d_qw"), sem("d_kw"), sem("d_stk")
        d_m = [sem(f"d_m{i}") for i in range(2)]
        d_mw = [sem(f"d_mw{i}") for i in range(2)]
        d_x2 = [sem(f"d_x2_{i}") for i in range(2)]
        d_scat = [sem(f"d_scat{i}") for i in range(2)]
        d_we, d_zero, d_pad = sem("d_we"), sem("d_zero"), sem("d_pad")
        d_row = [sem(f"d_row{i}") for i in range(4)]
        d_eo = [sem(f"d_eo{i}") for i in range(4)]
        d_tok = [sem(f"d_tok{i}") for i in range(8)]
        d_got = [sem(f"d_got{i}") for i in range(4)]
        d_out = [sem(f"d_out{i}") for i in range(4)]
        v_tab, p_tab, v_row = sem("v_tab"), sem("p_tab"), sem("v_row")
        p_tp, a_tp = [sem("p_tp2"), sem("p_tp3")], [sem("a_tp2"), sem("a_tp3")]
        p_gu, a_gate = [sem("p_gu2"), sem("p_gu3")], [sem("a_gate2"), sem("a_gate3")]
        v_hid, p_hp = [sem("v_hid2"), sem("v_hid3")], [sem("p_hp2"), sem("p_hp3")]
        a_hT, p_eo = [sem("a_hT2"), sem("a_hT3")], [sem("p_eo2"), sem("p_eo3")]
        v_res = [sem("v_res2"), sem("v_res3")]
        v_b3, v_s3, g_v3, g_rs3, v_h3 = sem("v_b3"), sem("v_s3"), sem("g_v3"), sem("g_rs3"), sem("v_h3")
        g_pos, v_wr, v_a0, v_a1 = sem("g_pos"), sem("v_wr"), sem("v_a0"), sem("v_a1")
        p_xT, p_cT, p_v, p_q, p_k = sem("p_xT"), sem("p_cT"), sem("p_v"), sem("p_q"), sem("p_k")
        p_hT, p_lg, p_pf, p_mT = sem("p_hT"), sem("p_lg"), sem("p_pf"), sem("p_mT")
        p_st, p_pv, p_mx = sem("p_st"), sem("p_pv"), sem("p_mx")
        a_x, a_c, a_v, a_q, a_k = sem("a_x"), sem("a_c"), sem("a_v"), sem("a_q"), sem("a_k")
        a_h, a_e, a_mT, a_exp, a_lam = sem("a_h"), sem("a_e"), sem("a_mT"), sem("a_exp"), sem("a_lam")
        v_q, v_k, v_red, v_mx, v_s1, v_s2 = (sem("v_q"), sem("v_k"), sem("v_red"), sem("v_mx"), sem("v_s1"),
                                             sem("v_s2"))
        v_mxa, v_ps = sem("v_mxa"), sem("v_ps")
        v_rl, v_rlc, v_cb, v_b1, v_b2, v_lam = (sem("v_rl"), sem("v_rlc"), sem("v_cb"), sem("v_b1"), sem("v_b2"),
                                                sem("v_lam"))
        v_rt, v_hot, v_pf, v_pos, v_w = sem("v_rt"), sem("v_hot"), sem("v_pf"), sem("v_pos"), sem("v_w")
        g_set, v_xn, g_qb, g_qs, g_kb, g_ks = (sem("g_set"), sem("v_xn"), sem("g_qb"), sem("g_qs"),
                                               sem("g_kb"), sem("g_ks"))
        g_att, g_x2, v_h2, g_r1, g_r2 = sem("g_att"), sem("g_x2"), sem("v_h2"), sem("g_r1"), sem("g_r2")
        passed = sem("passed")
        SETUP = 18
        N_W = 8
        STK = 18 * 16
        MR = 2 * 16
        RT = 12

        first, lo, hi, end = -3, 4, NS - 4, NS + 2

        def wait(eng, sem, inc, s, j=0, last=None, plain=False):
            if s.k is None:
                v = inc * s.off + j
                if last is not None:
                    v = min(v, inc * last)
                if v > 0:
                    eng.wait_ge(sem, v)
            else:
                eng.wait_ge(sem, s.k * (s.unroll * inc) + (inc * s.off + j))
                if plain or eng.engine in (mybir.EngineType.SP, mybir.EngineType.Pool):
                    eng.sem_inc(passed, 1)

        def wait_par(eng, sems, inc, s):
            ring = len(sems)
            v = inc * (s.off // ring + 1)
            if s.k is None:
                if v > 0:
                    eng.wait_ge(sems[s.off % ring], v)
            else:
                eng.wait_ge(sems[s.off % ring], s.k * (inc * s.unroll // ring) + v)
                if eng.engine in (mybir.EngineType.SP, mybir.EngineType.Pool):
                    eng.sem_inc(passed, 1)

        def pipeline(eng, body, first, lo, hi, end, unroll):
            for it in range(first, lo):
                body(Step(None, it))
            with eng.Fori(0, (hi - lo) // unroll) as k:
                for off in range(unroll):
                    body(Step(k, lo + off, unroll))
            for it in range(hi, end):
                body(Step(None, it))

        def steps(eng, body):
            pipeline(eng, body, first, lo, hi, end, 2)

        NT_HI = (NT - 4) // 4 * 4
        TT_HI = (NB - 7) // 8 * 8

        def expert_steps(eng, body):
            pipeline(eng, body, -4, 8, NT_HI, NT + 2, 4)

        def token_steps(eng, body):
            pipeline(eng, body, -6, 8, TT_HI, NB + 2, 8)

        block = st.enter_context(nc.Block())

        @block.sync
        def _(sp):
            for dst, src in ((wq_sb, wqT), (wk_sb, wkT), (wv_sb, wvT), (gw_sb, gate_wT)):
                sp.dma_start(dst[:, :, :], src).then_inc(d_w, 16)
            for n, src in enumerate((lq1, lq2, lk1, lk2)):
                sp.dma_start(lam_in[:, n, :], src.partition_broadcast(P)).then_inc(d_w, 16)
            sp.dma_start(x_in[:, :, :], x_g[0]).then_inc(d_x, 16)

            def step(it):
                a, b, d, ln = it.plus(2), it.plus(1), it.plus(-1), it.plus(3)
                p = it.par()
                if it.k is None and it.off == 0:
                    sp.wait_ge(g_set, SETUP)
                    for n in range(4):
                        e = slice(n * E // 4, (n + 1) * E // 4)
                        sp.dma_start(w_gu_sb[:, e], w_gu[:, e]).then_inc(d_we, 16)
                    sp.dma_start(w_dn_sb[:, :, :], w_dn).then_inc(d_we, 16)
                    sp.dma_start(ws_gu_sb[:, :, :], ws_gu).then_inc(d_we, 16)
                    sp.dma_start(ws_dn_sb[:, :], ws_dn).then_inc(d_we, 16)
                    sp.dma_start(rows_dram.rearrange("(e n) d -> n e d", e=E)[CAP - P:CAP],
                                 zeros[:, :].unsqueeze(1).to_broadcast([P, E, D])).then_inc(d_zero, 16)
                if it.is_in(0, NS):
                    wait(sp, a_mT, 2, it, 2)
                    max_rows(it, 1)
                if d.is_in(0, NS):
                    wait(sp, g_x2, 4, d, 4)
                    sp.dma_start(x2_g[bass.ds(d.idx(), 1)].rearrange("g p u d -> (g p) u d"),
                                 x2[1 - p][:, :, :]).then_inc(d_x2[1 - p], 16)
                if b.is_in(0, NS):
                    wait(sp, g_x2, 4, it, 0)
                    sp.dma_start(x_res[1 - p][:, :, :],
                                 x_g[bass.ds(b.idx(), 1)].rearrange("g p u d -> (g p) u d")).then_inc(d_res[1 - p], 16)
                if ln.is_in(0, NS):
                    wait(sp, p_cT, 1, ln)
                    sp.dma_start(c_in[:, :, :],
                                 c_g[bass.ds(ln.idx(), 1)].rearrange("g p u d -> (g p) u d")).then_inc(d_c, 16)
                if a.is_in(0, NS):
                    for n, (done, buf, landed) in enumerate(((g_qs, qp, d_qw), (g_ks, kp, d_kw))):
                        wait(sp, done, 1, a, 1)
                        if n == 0:
                            wait(sp, d_stk, STK, a, -STK)
                        for h in range(2):
                            sp.dma_start(parts_dram[p, n, h].rearrange("r p t -> p r t"),
                                         buf[:, :, h * SW:(h + 1) * SW]).then_inc(landed, 16)
                nxt = it.plus(4)
                if nxt.is_in(1, NS):
                    wait(sp, v_xn, 2, nxt)
                    sp.dma_start(x_in[:, :, :],
                                 x_g[bass.ds(nxt.idx(), 1)].rearrange("g p u d -> (g p) u d")).then_inc(d_x, 16)
                if b.is_in(0, NS):
                    wait(sp, a_mT, 2, b, 1)
                    max_rows(b, 0)
                if a.is_in(0, NS):
                    wait(sp, p_st, NCH, it, NCH)
                    wait(sp, d_qw, 32, a, 32)
                    wait(sp, d_kw, 32, a, 32)
                    if a.k is None and a.off < 2:
                        sp.wait_ge(g_set, SETUP)
                    for h in range(2):
                        q, k = parts_dram[p, 0, h], parts_dram[p, 1, h]
                        for r, n in ((0, 3), (3, 2), (5, 1)):
                            lo_p = 64 * h + HALF * r
                            sp.dma_start(q_st[p][lo_p:lo_p + HALF * n, :, :],
                                         q[0:n].rearrange("r (d j) t -> (r d) j t", d=HALF)).then_inc(d_stk, 16)
                        for r, n in enumerate((0, 0, 0, 1, 1, 2)):
                            lo_p = 64 * h + HALF * r
                            sp.dma_start(k_st[p][lo_p:lo_p + HALF, :, :],
                                         k[n].rearrange("(d j) t -> d j t", d=HALF)).then_inc(d_stk, 16)

            def max_rows(s, u):
                p = s.par()
                wait(sp, d_m[u], MR, s, -MR)
                sp.dma_start(max_dram[p, u].rearrange("r h j t -> (r h j) t"), mxT[u][:, :]).then_inc(d_mw[u], 16)
                wait(sp, d_mw[u], 16, s, 16)
                for h in range(2):
                    row = 64 * h + ROWS
                    sp.dma_start(q_st[p][row:row + 2, :, u * P:(u + 1) * P], max_dram[p, u, :, h]
                                 ).then_inc(d_m[u], 16)

            steps(sp, step)
            for i in range(2):
                sp.wait_ge(d_x2[i], 16 * (NS // 2))

            sp.wait_ge(v_row, 1)
            for i in range(2):
                sp.wait_ge(d_scat[i], 64 * (NS // 2))
            for e in range(E):
                r = sp.value_load(pad_tab[0:1, e:e + 1], min_val=0, max_val=E * CAP - P)
                sp.dma_start(rows_dram[bass.ds(r, P), :], zeros[:, :]).then_inc(d_pad, 16)
            sp.wait_ge(d_pad, 16 * E)
            sp.wait_ge(v_row, 3)

            def expert_step(j):
                t = j.plus(4)
                if t.is_in(0, NT):
                    wait(sp, p_tp[0], 1, t, -3)
                    r = sp.value_load(row_tab[0:1, bass.ds(t.idx(), 1)], min_val=0, max_val=N_ROWS - P)
                    sp.dma_start(tok_in[t.off % 4][:, :], rows_dram[bass.ds(r, P), :]).then_inc(d_row[t.off % 4], 16)
                t = j.plus(-1)
                if t.is_in(0, NT):
                    wait(sp, v_res[0], 1, t, 1)
                    sp.dma_start(routed_dram[bass.ds(t.idx() * P, P), :], res[t.off % 4][:, :]).then_inc(d_eo[t.off % 4], 16)

            expert_steps(sp, expert_step)

            sp.wait_ge(p_tp[0], NT)

            def token_step(j):
                t = j.plus(6)
                if t.is_in(0, NB):
                    wait(sp, v_a0, 1, t, -7)
                    sp.dma_start(tok_in[t.off % 8][:, :], x2_dram[bass.ds(t.idx(), 1)].rearrange("g p d -> (g p) d")
                                 ).then_inc(d_tok[t.off % 8], 16)
                t = j.plus(-1)
                if t.is_in(0, NB):
                    wait(sp, v_res[1], 1, t, 1)
                    sp.dma_start(out[bass.ds(t.idx(), 1)].rearrange("g p d -> (g p) d"), res[t.off % 4][:, :]
                                 ).then_inc(d_out[t.off % 4], 16)

            token_steps(sp, token_step)
            for i in range(4):
                sp.wait_ge(d_out[i], 16 * (NB // 4))

        @block.tensor
        def _(pe):
            pe.wait_ge(d_w, 16 * N_W)
            pe.wait_ge(g_set, SETUP)
            M0, M1 = ms_ps

            def scores(s, k):
                u, c = divmod(k, NCH // 2)
                h, p = c // 4, s.par()
                if c == 0:
                    wait(pe, d_m[u], MR, s, MR)
                for i in range(CHUNK):
                    j = CHUNK * (c % 4) + i
                    mm = pe.matmul(st_ps[k % 2][:, i * P:(i + 1) * P],
                                   k_st[p][64 * h:64 * h + KROWS, j, u * P:(u + 1) * P],
                                   q_st[p][64 * h:64 * h + KROWS, j, u * P:(u + 1) * P], start=True, stop=True)
                mm.then_inc(p_st, 1)

            def attend(s, k):
                u, c = divmod(k, NCH // 2)
                if k == 0:
                    wait(pe, a_v, 1, s, 1)
                if c % 4 == 0:
                    wait(pe, v_cb, 4, s, k // 4 - 1)
                for i in range(CHUNK):
                    sub = CHUNK * c + i
                    at = (sub % SHH) * (DH + 1)
                    own = (u * HEADS + sub // 2) * (DH + 1)
                    mm = pe.matmul(o_ps[(k // 4) % 2][:, at:at + WIDE], prob[k % 4][:, i * P:(i + 1) * P],
                                   v_sb[s.par()][:, own:own + WIDE], start=True, stop=True)
                mm.then_inc(p_pv, 1)

            def maxima(s, k):
                u, c = divmod(k, NCH // 2)
                h, p = c // 4, s.par()
                if k == 0:
                    wait(pe, d_stk, STK, s, STK)
                wait(pe, v_red, NCH, s, k - 1)
                for i in range(CHUNK):
                    j = CHUNK * (c % 4) + i
                    mm = pe.matmul(mx_ps[k % 2][:, i * P:(i + 1) * P],
                                   q_st[p][64 * h:64 * h + ROWS, j, u * P:(u + 1) * P],
                                   k_st[p][64 * h:64 * h + ROWS, j, u * P:(u + 1) * P], start=True, stop=True)
                mm.then_inc(p_mx, 1)

            def turn_max(s, u, bank):
                wait(pe, v_mx, 2, s, u + 1, plain=True)
                pe.transpose(bank.bitcast(BF16)[0:2 * SUB, 0:P], mxp[:, u, :], identb[:, :]).then_inc(p_mT, 1)

            def turn(src, bank, done):
                for u in range(2):
                    for h in range(DK):
                        mm = pe.transpose(bank[:, h * SW + u * P:h * SW + (u + 1) * P], src[:, u, h * P:(h + 1) * P],
                                          ident[:, :])
                mm.then_inc(done, 1)

            def project(w, src, bank, done):
                for m in range(2):
                    for h in range(DK):
                        mm = pe.matmul(bank[:, m * SW:(m + 1) * SW], w[:, h, m * P:(m + 1) * P], src[:, h, :],
                                       start=(h == 0), stop=(h == DK - 1))
                mm.then_inc(done, 1)

            def side(it, k):
                a, b, d, r = it.plus(2), it.plus(1), it.plus(-1), it.plus(-2)
                do_a, do_b, do_d = a.is_in(0, NS), b.is_in(0, NS), d.is_in(0, NS)
                if k == 1 and it.is_in(0, NS):
                    turn_max(it, 1, M0)
                if k == 0 and do_a:
                    wait(pe, v_pf, 1, r)
                    wait(pe, a_mT, 2, it, 1, last=NS)
                    wait(pe, v_xn, 2, a, 2)
                    turn(xn, M1, p_xT)
                if k == 2 and do_a:
                    wait(pe, a_mT, 2, it, 2, last=NS)
                    wait(pe, d_c, 16, a, 16)
                    turn(c_in, M0, p_cT)
                if k == 3 and do_b:
                    if do_a:
                        wait(pe, a_x, 1, a, 1)
                    else:
                        wait(pe, a_mT, 2, it, 1, last=NS)
                    wait(pe, a_c, 1, b, 1)
                    for u in range(2):
                        for h in range(DK):
                            mm = pe.matmul(M1[:, u * SW:(u + 1) * SW], cT[b.par()][:, h, u * P:(u + 1) * P],
                                           wv_sb[:, h, :], start=(h == 0), stop=(h == DK - 1))
                    mm.then_inc(p_v, 1)
                if k == 4 and do_a:
                    wait(pe, a_x, 1, a, 1)
                    wait(pe, a_c, 1, a, 1)
                    project(wq_sb, xnT, M0, p_q)
                if k == 5 and do_a:
                    wait(pe, a_v, 1, b, 1)
                    wait(pe, a_c, 1, a, 1)
                    project(wk_sb, cT[a.par()], M1, p_k)
                if k == 6 and do_d:
                    if do_a:
                        wait(pe, v_q, 1, a, 1)
                    else:
                        wait(pe, a_mT, 2, it, 2, last=NS)
                    wait(pe, v_h2, 2, d, 2)
                    turn(h2[d.par()], M0, p_hT)
                if k == 7 and r.is_in(0, NS):
                    if not do_d:
                        wait(pe, a_e, 1, d)
                    if do_a:
                        wait(pe, v_k, 1, a, 1)
                    wait(pe, v_hot, 1, r, 1)
                    pe.matmul(M1[:, 2 * E:4 * E], upper[:, :], hots[:, :, :], start=True, stop=True)
                    pe.matmul(M1[:, 4 * E:6 * E], onesb[:, :], hots[:, :, :], start=True, stop=True).then_inc(p_pf, 1)
                if k == 7 and do_d:
                    if do_a:
                        wait(pe, v_k, 1, a, 1)
                    else:
                        wait(pe, a_v, 1, b, 1, last=NS)
                        wait(pe, a_mT, 2, it, 1, last=NS)
                    wait(pe, a_h, 1, d, 1)
                    for u in range(2):
                        for h in range(DK):
                            mm = pe.matmul(M1[:, u * E:(u + 1) * E], h2T[:, h, u * P:(u + 1) * P], gw_sb[:, h, :],
                                           start=(h == 0), stop=(h == DK - 1))
                    mm.then_inc(p_lg, 1)
                if k == 12 and do_b:
                    wait(pe, v_pf, 1, r, 1)
                    wait(pe, a_e, 1, d, 1, last=NS)
                    if d.k is None and d.off < 0 and do_a:
                        wait(pe, v_k, 1, a, 1)
                    turn_max(b, 0, M1)
                if do_b:
                    for n in MAX_SLOTS.get(k, ()):
                        maxima(b, n)

            def step(it):
                d = it.plus(-1)
                for k in range(NCH):
                    cur, prev = it.is_in(0, NS), k < 2 and d.is_in(0, NS)
                    if cur or prev or k >= 2:
                        if it.is_in(0, NS + (1 if k < 2 else 0)):
                            wait(pe, a_exp, NCH, it, k - 1)
                    if cur:
                        scores(it, k)
                    if prev:
                        attend(d, NCH + k - 2)
                    elif cur and k >= 2:
                        attend(it, k - 2)
                    side(it, k)

            steps(pe, step)

            pe.wait_ge(v_tab, 1)
            pe.wait_ge(a_e, NS)
            pe.wait_ge(v_pf, NS)
            pe.transpose(M0[0:E, 0:P], count[:, :], ident[:, :]).then_inc(p_tab, 1)
            pe.wait_ge(v_tab, 9)
            pe.matmul(M1[0:E, 0:1], upto[:, :], tiles_n[:, :], start=True, stop=True).then_inc(p_tab, 1)
            pe.wait_ge(v_tab, 12)
            pe.matmul(M0[0:1, 0:NT], one_skip[:, 0:1], past[:, :], start=True, stop=True)
            pe.matmul(M1[0:1, 0:NT], one_skip[:, 1:2], past[:, :], start=True, stop=True).then_inc(p_tab, 1)

            pe.wait_ge(a_exp, NCH * NS)
            pe.wait_ge(v_red, NCH * NS)
            pe.wait_ge(v_cb, 4 * NS)
            pe.wait_ge(v_row, 3)
            pe.wait_ge(d_we, 16 * 7)

            def ffn(ph, n, j, turned, free_in, w_up, w_down):
                t = j.plus(2)
                if t.is_in(0, n):
                    turned(t)
                    wait(pe, a_tp[ph], 1, t, -1)
                    for h in range(DK):
                        mm = pe.transpose(tp_ps[t.off % 2][:, h * P:(h + 1) * P],
                                          free_in(t)[:, h * P:(h + 1) * P], ident[:, :])
                    mm.then_inc(p_tp[ph], 1)
                t = j.plus(1)
                if t.is_in(0, n):
                    w = w_up(t)
                    wait(pe, a_tp[ph], 1, t, 1)
                    wait(pe, v_hid[ph], 1, t, -1)
                    for h in range(DK):
                        mm = pe.matmul(gu_ps[t.off % 2][:, 0:2 * HID], rows_T[t.off % 2][:, h, :], w(h),
                                       start=(h == 0), stop=(h == DK - 1))
                    mm.then_inc(p_gu[ph], 1)
                t = j
                if t.is_in(0, n):
                    wait(pe, v_hid[ph], 1, t, 1)
                    wait(pe, a_hT[ph], 1, t, -1)
                    pe.transpose(hp_ps[t.off % 2][:, 0:P], hid[t.off % 2][:, :], ident[:, :]).then_inc(p_hp[ph], 1)
                t = j.plus(-1)
                if t.is_in(0, n):
                    w = w_down(t)
                    wait(pe, a_hT[ph], 1, t, 1)
                    wait(pe, v_res[ph], 1, t, -1)
                    pe.matmul(eo_ps[t.off % 2][:, 0:D], hid_T[t.off % 2][:, :], w, start=True,
                              stop=True).then_inc(p_eo[ph], 1)

            def expert_of(t):
                return pe.value_load(expert_tab[0:1, bass.ds(t.idx(), 1)], min_val=0, max_val=E - 1)

            def routed_up(t):
                e = expert_of(t)
                return lambda h: w_gu_sb[:, bass.ds(e, 1), h, :].rearrange("p e n -> p (e n)")

            def routed_down(t):
                return w_dn_sb[:, bass.ds(expert_of(t), 1), :].rearrange("p e n -> p (e n)")

            expert_steps(pe, lambda j: ffn(0, NT, j, lambda t: wait_par(pe, d_row, 16, t),
                                           lambda t: tok_in[t.off % 4], routed_up, routed_down))
            pe.wait_ge(v_res[0], NT)
            token_steps(pe, lambda j: ffn(1, NB, j, lambda t: wait(pe, v_h3, 1, t, 1),
                                          lambda t: h3[t.off % 2], lambda t: lambda h: ws_gu_sb[:, h, :],
                                          lambda t: ws_dn_sb[:, :]))

        @block.scalar
        def _(act):
            M0, M1 = ms_ps
            act.wait_ge(v_lam, 2)
            nc.scalar.activation(lam_e[:, :], lam_s[:, :], ACT.Exp).then_inc(a_lam, 1)

            def copy_max(s, u, bank):
                wait(act, p_mT, 2, s, u + 1)
                wait(act, d_mw[u], 16, s)
                nc.scalar.activation(mxT[u][:, :], bank.bitcast(BF16)[0:2 * SUB, 0:P], ACT.Copy).then_inc(a_mT, 1)

            def step(it):
                a, b, d = it.plus(2), it.plus(1), it.plus(-1)
                do_a, do_b, do_c, do_d = a.is_in(0, NS), b.is_in(0, NS), it.is_in(0, NS), d.is_in(0, NS)
                for k in range(NCH):
                    if do_c:
                        wait(act, p_st, NCH, it, k + 1)
                        wait(act, p_pv, NCH, it, k - 3)
                        nc.scalar.activation(prob[k % 4][:, :], st_ps[k % 2][:, :], ACT.Exp,
                                             scale=float(HALF) ** -0.5).then_inc(a_exp, 1)
                    if k == 1 and do_c:
                        copy_max(it, 1, M0)
                    if k == 0 and do_a:
                        wait(act, p_xT, 1, a, 1)
                        wait(act, p_q, 1, a)
                        nc.scalar.activation(xnT[:, :, :], M1[:, :], ACT.Copy).then_inc(a_x, 1)
                    if k == 2 and do_a:
                        wait(act, p_cT, 1, a, 1)
                        wait(act, p_v, 1, it, 1)
                        wait(act, p_k, 1, it, 1)
                        nc.scalar.activation(cT[a.par()][:, :, :], M0[:, :], ACT.Copy).then_inc(a_c, 1)
                    if k == 3 and do_b:
                        wait(act, p_v, 1, b, 1)
                        wait(act, p_pv, NCH, it)
                        nc.scalar.activation(v_sb[b.par()][:, 0:VW].rearrange("p (u h d) -> p u h d", u=2,
                                                                              h=HEADS)[:, :, :, 0:DH],
                                             M1[:, :].rearrange("p (u h d) -> p u h d", u=2, h=HEADS),
                                             ACT.Copy).then_inc(a_v, 1)
                    if k == 4 and do_a:
                        wait(act, p_q, 1, a, 1)
                        wait(act, d_qw, 32, a)
                        nc.scalar.activation(qp[:, 0, :], M0[:, :], ACT.Copy).then_inc(a_q, 1)
                    if k == 5 and do_a:
                        wait(act, p_k, 1, a, 1)
                        wait(act, d_kw, 32, a)
                        nc.scalar.activation(kp[:, 0, :], M1[:, :], ACT.Copy).then_inc(a_k, 1)
                    if k == 6 and do_d:
                        wait(act, p_hT, 1, d, 1)
                        wait(act, p_lg, 1, d)
                        nc.scalar.activation(h2T[:, :, :], M0[:, :], ACT.Copy).then_inc(a_h, 1)
                    if k == 7 and do_d:
                        wait(act, p_lg, 1, d, 1)
                        wait(act, v_rt, RT, d)
                        nc.scalar.activation(ez[:, :], M1[:, 0:2 * E], ACT.Exp, scale=-1.0).then_inc(a_e, 1)
                    if k == 12 and do_b:
                        copy_max(b, 0, M1)

            steps(act, step)

            def ffn(ph, n, j):
                t = j.plus(2)
                if t.is_in(0, n):
                    wait(act, p_tp[ph], 1, t, 1)
                    wait(act, p_gu[ph], 1, t, -1)
                    nc.scalar.activation(rows_T[t.off % 2][:, :, :], tp_ps[t.off % 2][:, 0:D],
                                         ACT.Copy).then_inc(a_tp[ph], 1)
                t = j.plus(1)
                if t.is_in(0, n):
                    wait(act, p_gu[ph], 1, t, 1)
                    wait(act, v_hid[ph], 1, t, -1)
                    nc.scalar.activation(gate[t.off % 2][:, :], gu_ps[t.off % 2][:, 0:HID],
                                         ACT.Silu).then_inc(a_gate[ph], 1)
                t = j
                if t.is_in(0, n):
                    wait(act, p_hp[ph], 1, t, 1)
                    wait(act, p_eo[ph], 1, t, -1)
                    nc.scalar.activation(hid_T[t.off % 2][:, :], hp_ps[t.off % 2][:, 0:P],
                                         ACT.Copy).then_inc(a_hT[ph], 1)

            expert_steps(act, lambda j: ffn(0, NT, j))
            token_steps(act, lambda j: ffn(1, NB, j))

        @block.vector
        def _(dve):
            v = nc.vector
            M0, M1 = ms_ps
            dve.wait_ge(d_w, 16 * N_W)
            v.tensor_tensor(lam_p[:, :, :], lam_in[:, 0:2, :], lam_in[:, 2:4, :], ALU.mult).then_inc(v_lam, 1)
            dve.wait_ge(v_lam, 1)
            v.tensor_reduce(lam_s[:, :], lam_p[:, :, :], AX.X, ALU.add).then_inc(v_lam, 1)
            dve.wait_ge(a_lam, 1)
            dve.wait_ge(g_set, SETUP)
            cf = coef[:, :].rearrange("p (h two) -> p h two", two=2)
            v.tensor_scalar(lam_p[:, 0, 0:1], lam_e[:, 1:2], lam_e[:, 0:1], -LAMBDA_INIT, ALU.subtract,
                            ALU.add).then_inc(v_lam, 1)
            dve.wait_ge(v_lam, 3)
            v.tensor_copy(cf[:, :, 1], lam_p[:, 0, 0:1].to_broadcast([P, SHH // 2])).then_inc(v_lam, 1)
            dve.wait_ge(v_lam, 4)

            def rest(s, bank, a_done, part, tmp, g_done, v_done):
                wait(dve, a_done, 1, s, 1)
                wait(dve, g_done, 1, s)
                v.tensor_tensor(tmp[:, :], bank[:, :], part[:, 0, :], ALU.subtract).then_inc(v_done, 1)

            def reduce_max(s, k):
                u, c = divmod(k, NCH // 2)
                wait(dve, p_mx, NCH, s, k + 1)
                if c == 0:
                    wait(dve, v_mxa, 2, s, u - 1)
                v.tensor_reduce(mx[:, u, c * CHUNK:(c + 1) * CHUNK],
                                mx_ps[k % 2][:, :].rearrange("p (c n) -> p c n", c=CHUNK), AX.X,
                                ALU.max).then_inc(v_red, 1)
                if c == NCH // 2 - 1:
                    wait(dve, v_red, NCH, s, k + 1)
                    wait(dve, p_mT, 2, s, u - 1)
                    v.tensor_copy(mxp[:, u, 0:SUB], mx[:, u, :]).then_inc(v_mxa, 1)
                    wait(dve, v_mxa, 2, s, u + 1)
                    v.tensor_tensor(mxp[:, u, SUB:2 * SUB], mx[:, u, :], mxp[:, u, 0:SUB],
                                    ALU.subtract).then_inc(v_mx, 1)

            def combine(s, h):
                o = o_ps[h % 2][:, 0:SHH * (DH + 1)].rearrange("p (s d) -> p s d", s=SHH)
                wait(dve, p_pv, NCH, s, 4 * (h + 1))
                wait(dve, v_cb, 4, s, h)
                v.reciprocal(rl[:, :], o[:, :, DH]).then_inc(v_rl, 1)
                wait(dve, v_rl, 4, s, h + 1)
                v.tensor_tensor(rlc[:, :], rl[:, :], coef[:, :], ALU.mult).then_inc(v_rlc, 1)
                wait(dve, v_rlc, 4, s, h + 1)
                wait(dve, g_att, 4, s, h - 1)
                v.tensor_tensor(o_sc[h % 2][:, :, :], o[:, :, 0:DH],
                                rlc[:, :].unsqueeze(2).to_broadcast([P, SHH, DH]), ALU.mult).then_inc(v_cb, 1)

            def stats(s, src, st_b, mv, ve, v_b, v_s, v_done):
                wait(dve, v_done, 2, s)
                for u in range(2):
                    v.bn_stats(st_b[:, u, :], src[:, u, :]).then_inc(v_b, 1)
                for u in range(2):
                    wait(dve, v_b, 2, s, u + 1, plain=True)
                    v.bn_aggr(mv[:, u, :], st_b[:, u, :]).then_inc(v_s, 1)
                wait(dve, v_s, 3, s, 2)
                v.tensor_scalar(ve[:, :], mv[:, :, 1], EPS, None, ALU.add).then_inc(v_s, 1)

            def norm(s, src, mv, rs, dst, g_r, v_done):
                wait(dve, g_r, 1, s, 1)
                for u in range(2):
                    v.tensor_scalar(dst[:, u, :], src[:, u, :], mv[:, u, 0:1], rs[:, u:u + 1], ALU.subtract,
                                    ALU.mult).then_inc(v_done, 1)

            def best_two(s):
                wait(dve, a_e, 1, s, 1)
                v.tensor_scalar(ez1[:, :], ez[:, :], 1.0, None, ALU.add).then_inc(v_rt, 1)
                wait(dve, v_rt, RT, s, 1)
                v.reciprocal(score[:, :, :], ez1[:, :].rearrange("p (u e) -> p u e", u=2)).then_inc(v_rt, 1)
                wait(dve, v_rt, RT, s, 2, plain=True)
                for u in range(2):
                    v.max(top[:, u, :], score[:, u, :]).then_inc(v_rt, 1)
                wait(dve, v_rt, RT, s, 4, plain=True)
                for u in range(2):
                    v.max_index(topi[:, u, :], top[:, u, :], score[:, u, :]).then_inc(v_rt, 1)
                v.tensor_tensor(den[:, :], top[:, :, 0], top[:, :, 1], ALU.add).then_inc(v_rt, 1)

            def choice(s):
                wait(dve, v_rt, RT, s, 7)
                v.tensor_copy(topf[:, :, :], topi[:, :, 0:TOPK]).then_inc(v_rt, 1)
                v.tensor_scalar(den1[:, :], den[:, :], 1e-20, None, ALU.add).then_inc(v_rt, 1)
                wait(dve, v_rt, RT, s, 9)
                v.tensor_tensor(hot[:, :, :, :].rearrange("p u k e -> p (u k) e"),
                                iota_e[:, :].unsqueeze(1).to_broadcast([P, 2 * TOPK, E]),
                                topf[:, :, :].rearrange("p u k -> p (u k)").unsqueeze(2)
                                .to_broadcast([P, 2 * TOPK, E]), ALU.is_equal).then_inc(v_rt, 1)
                v.reciprocal(rden[:, :], den1[:, :]).then_inc(v_rt, 1)
                wait(dve, v_rt, RT, s, 11)
                v.tensor_tensor(hots[:, :, :], hot[:, :, 0, :], hot[:, :, 1, :], ALU.add).then_inc(v_hot, 1)
                v.scalar_tensor_tensor(
                    route_w[:, bass.ds(s.idx(), 1), :].rearrange("p g (u k) -> p (g u) k", u=2), top[:, :, 0:TOPK],
                    ROUTE_SCALE, rden[:, :].unsqueeze(2).to_broadcast([P, 2, TOPK]), ALU.mult,
                    ALU.mult).then_inc(v_rt, 1)

            def positions(s):
                tot = M1[:, 4 * E:6 * E].rearrange("p (u e) -> p u e", u=2)
                wait(dve, p_pf, 1, s, 1)
                wait(dve, a_e, 1, s.plus(1), 1, last=NS)
                v.tensor_tensor(base[:, 1, :], base[:, 0, :], tot[:, 0, :], ALU.add).then_inc(v_ps, 1)
                wait(dve, v_ps, 3, s, 1)
                v.tensor_tensor(pb[:, :, :], M1[:, 2 * E:4 * E].rearrange("p (u e) -> p u e", u=2), base[:, :, :],
                                ALU.add).then_inc(v_ps, 1)
                wait(dve, v_ps, 3, s, 2)
                v.tensor_tensor(base[:, 0, :], base[:, 1, :], tot[:, 1, :], ALU.add).then_inc(v_pf, 1)
                v.tensor_tensor(hotp[:, :, :, :], hot[:, :, :, :],
                                pb[:, :, :].unsqueeze(2).to_broadcast([P, 2, TOPK, E]), ALU.mult).then_inc(v_ps, 1)
                wait(dve, v_ps, 3, s, 3)
                v.tensor_reduce(posf[:, :], hotp[:, :, :, :].rearrange("p u k e -> p (u k) e"), AX.X,
                                ALU.add).then_inc(v_w, 1)
                wait(dve, v_w, 1, s, 1)
                wait(dve, v_pf, 1, s, 1)
                wait_par(dve, d_scat, 64, s.plus(-2))
                v.tensor_copy(posi[s.par()][:, :], posf[:, :]).then_inc(v_pos, 1)
                v.tensor_copy(pos_f[:, bass.ds(s.idx(), 1), :].rearrange("p g k -> p (g k)"),
                              posf[:, :]).then_inc(v_pos, 1)

            def step(it):
                a, b, d, ln, r = it.plus(2), it.plus(1), it.plus(-1), it.plus(3), it.plus(-2)
                do_a, do_b, do_d, do_ln, do_r = (a.is_in(0, NS), b.is_in(0, NS), d.is_in(0, NS), ln.is_in(0, NS),
                                                 r.is_in(0, NS))
                for k in range(NCH):
                    if k == 0 and do_r:
                        best_two(r)
                    if k == 1 and do_d:
                        combine(d, 3)
                    if k == 2 and do_r:
                        choice(r)
                    if k == 3 and do_d:
                        wait(dve, g_x2, 4, d, 4)
                        stats(d, x2[d.par()], bs2, mv2, ve2, v_b2, v_s2, v_h2)
                    if k == 4 and do_a:
                        rest(a, M0, a_q, qp, q_rest, g_qs, v_q)
                    if k == 5 and do_a:
                        rest(a, M1, a_k, kp, k_rest, g_ks, v_k)
                    if do_b:
                        for n in MAX_SLOTS.get(k, ()):
                            reduce_max(b, n)
                    if k == 4 and do_d:
                        wait_par(dve, d_scat, 64, d.plus(-2))
                        if d.k is not None or d.off >= 2:
                            wait(dve, p_hT, 1, d.plus(-1))
                        norm(d, x2[d.par()], mv2, rs2, h2[d.par()], g_r2, v_h2)
                    if k in (5, 9, 13) and it.is_in(0, NS):
                        combine(it, k // 4 - 1)
                    if k == 7 and do_ln:
                        wait(dve, d_x, 16, ln, 16)
                        stats(ln, x_in, bs1, mv1, ve1, v_b1, v_s1, v_xn)
                    if k == 8 and do_ln:
                        wait(dve, p_xT, 1, ln)
                        norm(ln, x_in, mv1, rs1, xn, g_r1, v_xn)
                    if k == 10 and do_r:
                        positions(r)

            steps(dve, step)

            n_tab = [0]

            def tab(ins):
                ins.then_inc(v_tab, 1)
                n_tab[0] += 1
                dve.wait_ge(v_tab, n_tab[0])

            dve.wait_ge(v_pf, NS)
            tab(v.tensor_tensor(count[:, :], base[:, 0, :], cap_e[:, :], ALU.subtract))
            tab(v.tensor_scalar(full[:, :], count[0:1, :], float(CAP - P), None, ALU.is_gt))
            tab(v.scalar_tensor_tensor(room[:, :], full[:, :], float(1 << 20), base[0:1, 0, :], ALU.mult, ALU.add))
            tab(v.tensor_reduce(least[:, :], room[:, :], AX.X, ALU.min))
            tab(v.scalar_tensor_tensor(room[:, :], base[0:1, 0, :], least[:, 0:1], full[:, :], ALU.subtract,
                                       ALU.mult))
            v.tensor_tensor(pad_tab[:, :], base[0:1, 0, :], room[:, :], ALU.subtract).then_inc(v_row, 1)
            dve.wait_ge(p_tab, 1)
            tab(v.tensor_scalar(tiles_n[:, :], M0[0:E, 0:1], float(P - 1), None, ALU.add))
            tab(v.tensor_copy(tiles_i[:, :], tiles_n[:, :]))
            tab(v.tensor_scalar(tiles_s[:, :], tiles_i[:, :], 7, None, ALU.logical_shift_right))
            tab(v.tensor_copy(tiles_n[:, :], tiles_s[:, :]))
            tab(v.tensor_scalar(one_skip[:, 1:2], tiles_n[:, :], float(-P), float(CAP), ALU.mult, ALU.add))
            dve.wait_ge(p_tab, 2)
            tab(v.tensor_copy(last_t[:, :], M1[0:E, 0:1]))
            tab(v.tensor_scalar(past[:, :], iota_t[:, :], last_t[:, 0:1], None, ALU.is_ge))
            dve.wait_ge(p_tab, 3)
            v.tensor_scalar(expert_tab[:, :], M0[0:1, 0:NT], float(E - 1), None, ALU.min).then_inc(v_row, 1)
            tab(v.scalar_tensor_tensor(row_f[:, :], iota_t[0:1, :], float(P), M1[0:1, 0:NT], ALU.mult, ALU.add))
            tab(v.tensor_scalar(past[0:1, :], row_f[:, :], float(E * CAP), None, ALU.is_ge))
            tab(v.scalar_tensor_tensor(row_d[:, :], row_f[:, :], row_f[:, 0:1], past[0:1, :], ALU.subtract,
                                       ALU.mult))
            v.tensor_tensor(row_tab[:, :], row_f[:, :], row_d[:, :], ALU.subtract).then_inc(v_row, 1)

            tab(v.tensor_scalar(tile_f[:, :], count[:, :], float(P - 1), None, ALU.add))
            tab(v.tensor_copy(tile_i[:, :], tile_f[:, :]))
            tab(v.tensor_scalar(tile_s[:, :], tile_i[:, :], 7, None, ALU.logical_shift_right))
            tab(v.tensor_copy(tile_f[:, :], tile_s[:, :]))
            tab(v.tensor_scalar(skip[:, :], tile_f[:, :], float(-P), float(CAP), ALU.mult, ALU.add))
            flat = pos_f[:, :, :].rearrange("p g k -> p (g k)")
            for e in range(E - 1, 0, -1):
                tab(v.tensor_scalar(cut[:, :], flat, float(e * CAP), skip[:, e - 1:e], ALU.is_ge, ALU.mult))
                tab(v.tensor_tensor(shift[:, :], shift[:, :] if e < E - 1 else cut[:, :],
                                    cut[:, :] if e < E - 1 else zeros[:, 0:NS * 2 * TOPK], ALU.add))
            tab(v.tensor_tensor(pos_all[:, :, :].rearrange("p g k -> p (g k)"), flat, shift[:, :], ALU.subtract))
            dve.sem_inc(v_row, 1)

            def hidden(ph, n, j):
                t = j.plus(1)
                if t.is_in(0, n):
                    wait(dve, a_gate[ph], 1, t, 1)
                    wait(dve, p_hp[ph], 1, t, -1)
                    v.tensor_tensor(hid[t.off % 2][:, :], gate[t.off % 2][:, :], gu_ps[t.off % 2][:, HID:2 * HID],
                                    ALU.mult).then_inc(v_hid[ph], 1)

            def expert_step(j):
                hidden(0, NT, j)
                t = j.plus(-1)
                if t.is_in(0, NT):
                    wait(dve, p_eo[0], 1, t, 1)
                    wait_par(dve, d_eo, 16, t.plus(-4))
                    v.tensor_copy(res[t.off % 4][:, :], eo_ps[t.off % 2][:, 0:D]).then_inc(v_res[0], 1)

            expert_steps(dve, expert_step)
            for i in range(4):
                dve.wait_ge(d_eo[i], 16 * (NT // 4))

            def token_step(j):
                t = j.plus(4)
                if t.is_in(0, NB):
                    wait_par(dve, d_tok, 16, t)
                    wait(dve, v_h3, 1, t, -1)
                    v.bn_stats(bs3[t.off % 2][:, :], tok_in[t.off % 8][:, :]).then_inc(v_b3, 1)
                    wait(dve, v_b3, 1, t, 1, plain=True)
                    v.bn_aggr(mv3[t.off % 2][:, :], bs3[t.off % 2][:, :]).then_inc(v_s3, 1)
                t = j.plus(3)
                if t.is_in(0, NB):
                    wait(dve, g_rs3, 1, t, 1)
                    wait(dve, p_tp[1], 1, t, -1)
                    v.tensor_scalar(h3[t.off % 2][:, :], tok_in[t.off % 8][:, :], mv3[t.off % 2][:, 0:1],
                                    rs3[t.off % 2][:, 0:1], ALU.subtract, ALU.mult).then_inc(v_h3, 1)
                hidden(1, NB, j)
                t = j.plus(-1)
                if t.is_in(0, NB):
                    c = TOPK * (t.off % 2)
                    g = t.off // 2 if t.k is None else t.k * (t.unroll // 2) + t.off // 2
                    p = t.off % 2
                    wait(dve, v_a1, 1, t, -1)
                    v.tensor_copy(w_r[p][:, :],
                                  route_w[:, bass.ds(g, 1), c:c + TOPK].rearrange("p g k -> p (g k)")
                                  ).then_inc(v_wr, 1)
                    wait_par(dve, d_got, 32, t)
                    wait(dve, v_wr, 1, t, 1)
                    v.scalar_tensor_tensor(acc0[p][:, :], got[t.off % 4][:, 0, :], w_r[p][:, 0:1],
                                           tok_in[t.off % 8][:, :], ALU.mult, ALU.add).then_inc(v_a0, 1)
                    wait(dve, v_a0, 1, t, 1)
                    v.scalar_tensor_tensor(acc1[p][:, :], got[t.off % 4][:, 1, :], w_r[p][:, 1:2],
                                           acc0[p][:, :], ALU.mult, ALU.add).then_inc(v_a1, 1)
                    wait(dve, v_a1, 1, t, 1)
                    wait(dve, p_eo[1], 1, t, 1)
                    wait_par(dve, d_out, 16, t.plus(-4))
                    v.tensor_tensor(res[t.off % 4][:, :], eo_ps[p][:, 0:D], acc1[p][:, :],
                                    ALU.add).then_inc(v_res[1], 1)

            token_steps(dve, token_step)

        @block.gpsimd
        def _(gp):
            g = nc.gpsimd
            n = 0
            for ins in ([g.memset(ident[:, :], 0.0), g.memset(identb[:, :], 0.0), g.memset(upper[:, :], 1.0),
                         g.memset(onesb[:, :], 1.0), g.memset(neghalf[:, :], -0.5), g.memset(coef[:, :], 1.0),
                         g.memset(zeros[:, :], 0.0), g.memset(upto[:, :], 1.0), g.memset(one_skip[:, :], 1.0)]
                        + [g.memset(k_st[i][:, :, :], -1.0) for i in range(2)]
                        + [g.memset(v_sb[i][:, :], 1.0) for i in range(2)]):
                ins.then_inc(g_set, 1)
                n += 1
            gp.wait_ge(g_set, n)
            for m in (ident, identb):
                g.affine_select(out=m[:, :], in_=m[:, :], compare_op=ALU.not_equal, fill=1.0, base=0,
                                pattern=[[-1, P]], channel_multiplier=1)
            g.affine_select(out=upper[:, :], in_=upper[:, :], compare_op=ALU.is_gt, fill=0.0, base=0,
                            pattern=[[1, P]], channel_multiplier=-1).then_inc(g_set, 1)
            g.iota(iota_e[:, :], pattern=[[1, E]], base=0, channel_multiplier=0,
                   allow_small_or_imprecise_dtypes=True).then_inc(g_set, 1)
            g.iota(base[:, 0, :], pattern=[[CAP, E]], base=0, channel_multiplier=0,
                   allow_small_or_imprecise_dtypes=True).then_inc(g_set, 1)
            g.iota(cap_e[:, :], pattern=[[CAP, E]], base=0, channel_multiplier=0,
                   allow_small_or_imprecise_dtypes=True).then_inc(g_set, 1)
            g.iota(iota_t[:, :], pattern=[[1, NT]], base=0, channel_multiplier=0,
                   allow_small_or_imprecise_dtypes=True)
            g.affine_select(out=upto[:, :], in_=upto[:, :], compare_op=ALU.is_ge, fill=0.0, base=0,
                            pattern=[[1, E]], channel_multiplier=-1).then_inc(g_set, 1)
            assert n + 5 == SETUP
            gp.wait_ge(g_set, SETUP)

            def deviation(s, ve, rs, v_s, g_r):
                wait(gp, v_s, 3, s, 3)
                g.tensor_tensor(rs[:, :], ve[:, :], neghalf[:, :], ALU.pow).then_inc(g_r, 1)

            def split(s, tmp, part, v_done, g_b, g_done, landed):
                wait(gp, v_done, 1, s, 1)
                wait(gp, landed, 32, s)
                g.tensor_copy(part[:, 1, :], tmp[:, :]).then_inc(g_b, 1)
                wait(gp, g_b, 1, s, 1)
                g.tensor_tensor(part[:, 2, :], tmp[:, :], part[:, 1, :], ALU.subtract).then_inc(g_done, 1)

            def residual(s, h):
                u, m = divmod(h, 2)
                p = s.par()
                wait(gp, v_cb, 4, s, h + 1)
                wait(gp, g_x2, 4, s, h)
                two = o_sc[h % 2][:, :, :].rearrange("p (h two) d -> p h two d", two=2)
                g.tensor_tensor(att[:, :, :], two[:, :, 0, :], two[:, :, 1, :], ALU.add).then_inc(g_att, 1)
                wait(gp, g_att, 4, s, h + 1)
                if h == 0:
                    wait_par(gp, d_res, 16, s)
                    wait_par(gp, d_x2, 16, s.plus(-2))
                    wait(gp, v_h2, 2, s.plus(-1))
                g.tensor_tensor(x2[p][:, u, m * P:(m + 1) * P].rearrange("p (h d) -> p h d", d=DH), att[:, :, :],
                                x_res[p][:, u, m * P:(m + 1) * P].rearrange("p (h d) -> p h d", d=DH),
                                ALU.add).then_inc(g_x2, 1)

            def scatter(s):
                p = s.par()
                if s.k is None and s.off == 0:
                    gp.wait_ge(d_zero, 16)
                wait(gp, v_pos, 2, s, 2)
                wait(gp, v_h2, 2, s, 2)
                for u in range(2):
                    for k in range(TOPK):
                        c = TOPK * u + k
                        g.indirect_dma_start(
                            rows_dram[:, :], bass.IndirectOffsetOnAxis(ap=posi[p][:, c:c + 1], axis=0),
                            h2[p][:, u, :], None).then_inc(d_scat[p], 16)

            def step(it):
                a, d, ln, r = it.plus(2), it.plus(-1), it.plus(3), it.plus(-2)
                do_c = it.is_in(0, NS)
                if d.is_in(0, NS):
                    residual(d, 3)
                    deviation(d, ve2, rs2, v_s2, g_r2)
                if a.is_in(0, NS):
                    split(a, q_rest, qp, v_q, g_qb, g_qs, d_qw)
                    split(a, k_rest, kp, v_k, g_kb, g_ks, d_kw)
                if do_c:
                    residual(it, 0)
                if ln.is_in(0, NS):
                    deviation(ln, ve1, rs1, v_s1, g_r1)
                if do_c:
                    residual(it, 1)
                if r.is_in(0, NS):
                    scatter(r)
                if do_c:
                    residual(it, 2)

            steps(gp, step)

            gp.wait_ge(v_row, 4)
            for i in range(4):
                gp.wait_ge(d_eo[i], 16 * (NT // 4))

            def token_step(j):
                t = j.plus(4)
                if t.is_in(0, NB):
                    q = t.off % 2
                    wait(gp, v_s3, 1, t, 1)
                    g.tensor_scalar(ve3[q][:, :], mv3[q][:, 1:2], EPS, None, ALU.add).then_inc(g_v3, 1)
                    wait(gp, g_v3, 1, t, 1)
                    g.tensor_tensor(rs3[q][:, :], ve3[q][:, :], neghalf[:, 0:1], ALU.pow).then_inc(g_rs3, 1)
                t = j.plus(2)
                if t.is_in(0, NB):
                    c = TOPK * (t.off % 2)
                    grp = t.off // 2 if t.k is None else t.k * (t.unroll // 2) + t.off // 2
                    wait_par(gp, d_got, 32, t.plus(-2))
                    g.tensor_copy(pos_r[t.off % 2][:, :],
                                  pos_all[:, bass.ds(grp, 1), c:c + TOPK].rearrange("p g k -> p (g k)")
                                  ).then_inc(g_pos, 1)
                    wait(gp, v_a1, 1, t, -3)
                    wait(gp, g_pos, 1, t, 1)
                    for k in range(TOPK):
                        g.indirect_dma_start(got[t.off % 4][:, k, :], None, routed_dram[:, :],
                                             bass.IndirectOffsetOnAxis(ap=pos_r[t.off % 2][:, k:k + 1], axis=0)
                                             ).then_inc(d_got[t.off % 4], 16)

            token_steps(gp, token_step)


def kernel(x, ctx_1024, L0_xattn_Wq, L0_xattn_Wk, L0_xattn_Wv, L0_xattn_lambda_q1, L0_xattn_lambda_q2,
           L0_xattn_lambda_k1, L0_xattn_lambda_k2, L0_ffn_gate_w, L0_ffn_w_gate, L0_ffn_w_up, L0_ffn_w_down,
           L0_ffn_ws_gate, L0_ffn_ws_up, L0_ffn_ws_down):
    import numpy as np
    import concourse.bacc as bacc
    from concourse.bass_utils import run_bass_kernel_spmd

    def contract_rows(w):
        w = np.asarray(w)
        return w.reshape(w.shape[0] // P, P, w.shape[1]).transpose(1, 0, 2)

    def dims_first(w):
        w = np.asarray(w).T
        return w.reshape(w.shape[0], 2, SUB // 2, -1).transpose(0, 1, 3, 2).reshape(w.shape)

    wg, wu = np.asarray(L0_ffn_w_gate), np.asarray(L0_ffn_w_up)
    n_e, dim, hid = wg.shape
    gate_up = np.concatenate([wg, wu], axis=2).reshape(n_e, dim // P, P, 2 * hid).transpose(2, 0, 1, 3)
    down = np.asarray(L0_ffn_w_down).transpose(1, 0, 2)
    laid = {
        "x": x, "ctx": ctx_1024, "lq1": L0_xattn_lambda_q1, "lk1": L0_xattn_lambda_k1, "lq2": L0_xattn_lambda_q2,
        "lk2": L0_xattn_lambda_k2, "wqT": contract_rows(dims_first(L0_xattn_Wq)),
        "wkT": contract_rows(dims_first(L0_xattn_Wk)), "wvT": contract_rows(np.asarray(L0_xattn_Wv).T),
        "gate_wT": contract_rows(np.asarray(L0_ffn_gate_w).T), "w_gu": gate_up, "w_dn": down,
        "ws_gu": contract_rows(np.concatenate([np.asarray(L0_ffn_ws_gate), np.asarray(L0_ffn_ws_up)], axis=1)),
        "ws_dn": L0_ffn_ws_down,
    }
    nc = bacc.Bacc("TRN2", target_bir_lowering=False, num_devices=1)
    arrays, args = {}, {}
    for name, a in laid.items():
        a = np.ascontiguousarray(a)
        arrays["in_" + name] = a
        args[name] = nc.dram_tensor("in_" + name, a.shape, mybir.dt.from_np(a.dtype), kind="ExternalInput").ap()
    out = nc.dram_tensor("out", x.shape, F32, kind="ExternalOutput").ap()
    program(nc, out=out, **args)
    r = run_bass_kernel_spmd(nc, [arrays], core_ids=[0])
    return r.results[0]["out"]
```

```python
from contextlib import ExitStack

import concourse.bass as bass
from concourse import mybir

ALU = mybir.AluOpType
ACT = mybir.ActivationFunctionType
AX = mybir.AxisListType
F32 = mybir.dt.float32
BF16 = mybir.dt.bfloat16
F32R = mybir.dt.float32r
U32 = mybir.dt.uint32
I32 = mybir.dt.int32

P = 128
HEADS = 16
SUB = 2 * HEADS
PARTS = 3
ROWS = 48
KROWS = ROWS + 2
CHUNK = 4
NCH = 2 * SUB // CHUNK
WIDE_HEADS = 7
LAMBDA_INIT = 0.8
EPS = 1e-5
ROUTE_SCALE = 2.5
TOPK = 2

MAX_SLOTS = {4: [0, 1], 5: [2, 3], 6: [4], 7: [5], 8: [6], 9: [7], 10: [8], 11: [9], 12: [10, 11], 13: [12],
             14: [13, 14], 15: [15]}


class Step:

    def __init__(self, k, off, unroll=2):
        self.k, self.off, self.unroll = k, off, unroll

    def plus(self, n):
        return Step(self.k, self.off + n, self.unroll)

    def idx(self):
        return self.off if self.k is None else self.k * self.unroll + self.off

    def par(self):
        return self.off % 2

    def is_in(self, lo, hi):
        return self.k is not None or lo <= self.off < hi


def program(nc, x, ctx, lq1, lk1, lq2, lk2, wqT, wkT, wvT, gate_wT, w_gu, w_dn, ws_gu, ws_dn, out):
    NB, _, D = x.shape
    NS = NB // 2
    T = NB * P
    NT = TOPK * T // P + gate_wT.shape[-1]
    E = gate_wT.shape[-1]
    CAP = T
    DK = D // P
    SHH = SUB // 2
    DH = D // HEADS
    HALF = DH // 2
    SW = 2 * P
    HID = w_dn.shape[0]
    VW = 2 * HEADS * (DH + 1)
    WIDE = WIDE_HEADS * (DH + 1)
    assert NS % 2 == 0 and NB >= 28 and E % 4 == 0 and CAP < 32768 and DK == 2 and HALF * SHH == P and HID == P and NT <= 512

    x_g = x.rearrange("(g u) p d -> g p u d", u=2)
    c_g = ctx.rearrange("(g u) p d -> g p u d", u=2)
    x2_dram = nc.dram_tensor("x2_dram", (NB, P, D), F32, kind="Internal").ap()
    x2_g = x2_dram.rearrange("(g u) p d -> g p u d", u=2)
    stack_dram = nc.dram_tensor("stack_dram", (2, 2, 2, ROWS, SHH, SW), BF16, kind="Internal").ap()
    max_dram = nc.dram_tensor("max_dram", (2, 2, 2, 2, SHH, P), BF16, kind="Internal").ap()
    N_ROWS = E * CAP
    rows_dram = nc.dram_tensor("rows_dram", (N_ROWS, D), F32, kind="Internal").ap()
    tags_dram = nc.dram_tensor("tags_dram", (N_ROWS, 2), F32, kind="Internal").ap()
    routed_dram = nc.dram_tensor("routed_dram", (T * TOPK, D), F32, kind="Internal").ap()

    routed_t = routed_dram.rearrange("(g p k) d -> g p k d", p=P, k=TOPK)

    with ExitStack() as st:
        def sb(name, shape, dt=F32):
            return st.enter_context(nc.sbuf_tensor(name, shape, dt))

        def ps(name):
            return st.enter_context(nc.psum_tensor(name, [P, 512], F32))

        def sem(name):
            return st.enter_context(nc.semaphore(name))

        st_ps = [ps(f"st_ps{i}") for i in range(2)]
        mx_ps = [ps(f"mx_ps{i}") for i in range(2)]
        o_ps = [ps(f"o_ps{i}") for i in range(2)]
        ms_ps = [ps(f"ms_ps{i}") for i in range(2)]
        tp_ps, gu_ps, hp_ps, eo_ps = st_ps, mx_ps, o_ps, ms_ps

        with ExitStack() as first_st:
            def first_sb(name, shape):
                return first_st.enter_context(nc.sbuf_tensor(name, shape, F32))

            w_gu_sb = first_sb("w_gu_sb", [P, E, DK, 2 * HID])
            w_dn_sb = first_sb("w_dn_sb", [P, E, D])
            ws_gu_sb = first_sb("ws_gu_sb", [P, DK, 2 * HID])
            ws_dn_sb = first_sb("ws_dn_sb", [P, D])
            stacks = first_sb("stacks", [P, 4 * SHH * SW // 2])
            spare = first_sb("spare", [P, E * D + DK * 2 * HID + D])
        w_gu_lo = sb("w_gu_lo", [P, E, DK, 2 * HID])
        w_dn_lo = sb("w_dn_lo", [P, E, D])
        ws_gu_lo = sb("ws_gu_lo", [P, DK, 2 * HID])
        ws_dn_lo = sb("ws_dn_lo", [P, D])
        w_gu_hi = sb("w_gu_hi", [P, E, DK, 2 * HID])
        w_dn_hi = sb("w_dn_hi", [P, E, D])
        ws_gu_hi = sb("ws_gu_hi", [P, DK, 2 * HID])
        ws_dn_hi = sb("ws_dn_hi", [P, D])

        wq_sb = sb("wq_sb", [P, DK, D])
        wk_sb = sb("wk_sb", [P, DK, D])
        wv_sb = sb("wv_sb", [P, DK, D])
        gw_sb = sb("gw_sb", [P, DK, E])
        lam_in = sb("lam_in", [P, 4, HALF])
        lam_p = sb("lam_p", [P, 2, HALF])
        lam_s = sb("lam_s", [P, 2])
        lam_e = sb("lam_e", [P, 2])
        coef = sb("coef", [P, SHH])
        ident = sb("ident", [P, P])
        identb = sb("identb", [P, P], BF16)
        upper = sb("upper", [P, P], BF16)
        onesb = sb("onesb", [P, P], BF16)
        iota_e = sb("iota_e", [P, E])
        neghalf = sb("neghalf", [P, 2])

        x_in = sb("x_in", [P, 2, D])
        c_in = sb("c_in", [P, 2, D])
        x_res = [sb(f"x_res{i}", [P, 2, D]) for i in range(2)]
        taken = [0]

        def carve(words, pattern, **sizes):
            taken[0] += words
            return spare[:, taken[0] - words:taken[0]].rearrange(pattern, **sizes)

        def carve_parts():
            taken[0] += PARTS * 256
            return spare.bitcast(BF16)[:, 2 * taken[0] - PARTS * 512:2 * taken[0]].rearrange("p (r n) -> p r n", r=PARTS)

        def stack(n):
            return stacks.bitcast(BF16)[:, n * SHH * SW:(n + 1) * SHH * SW].rearrange("p (j t) -> p j t", j=SHH)

        xnT = sb("xnT", [P, DK, SW])
        cT = [sb(f"cT{i}", [P, DK, SW]) for i in range(2)]
        q_st, k_st = [stack(0), stack(1)], [stack(2), stack(3)]
        prob = [carve(512, "p n -> p n") for _ in range(4)]
        qp, kp = carve_parts(), carve_parts()
        q_rest, k_rest = carve(512, "p n -> p n"), carve(512, "p n -> p n")
        assert taken[0] <= E * D + DK * 2 * HID + D
        xn = sb("xn", [P, 2, D])
        v_sb = [sb(f"v_sb{i}", [P, VW + WIDE]) for i in range(2)]
        mx = sb("mx", [P, 2, SUB])
        mxp = sb("mxp", [P, 2, 2 * SUB], BF16)
        mxT = [sb(f"mxT{i}", [2 * SUB, P], BF16) for i in range(2)]
        rl = sb("rl", [P, SHH])
        rlc = sb("rlc", [P, SHH])
        o_sc = [sb(f"o_sc{i}", [P, SHH, DH]) for i in range(2)]
        att = sb("att", [P, SHH // 2, DH])
        x2 = [sb(f"x2_{i}", [P, 2, D]) for i in range(2)]
        h2 = [sb(f"h2_{i}", [P, 2, D]) for i in range(2)]
        h2T = sb("h2T", [P, DK, SW])
        bs1 = sb("bs1", [P, 2, 6])
        mv1 = sb("mv1", [P, 2, 2])
        ve1 = sb("ve1", [P, 2])
        bs2 = sb("bs2", [P, 2, 6])
        mv2 = sb("mv2", [P, 2, 2])
        ve2 = sb("ve2", [P, 2])
        mv_all = sb("mv_all", [P, NS, 4])
        ez = sb("ez", [P, 2 * E])
        ez1 = sb("ez1", [P, 2 * E])
        score = sb("score", [P, 2, E])
        top = sb("top", [P, 2, 8])
        topi = sb("topi", [P, 2, 8], U32)
        topf = sb("topf", [P, 2, TOPK])
        hot = sb("hot", [P, 2, TOPK, E])
        hots = sb("hots", [P, 2, E], BF16)
        den = sb("den", [P, 2])
        den1 = sb("den1", [P, 2])
        rden = sb("rden", [P, 2])
        number = sb("number", [P, 2 * TOPK])
        tag = [sb(f"tag{i}", [P, 2 * TOPK, 2]) for i in range(2)]
        no_tag = sb("no_tag", [P, 2])
        base = sb("base", [P, 2, E])
        pb = sb("pb", [P, 2, E])
        hotp = sb("hotp", [P, 2, TOPK, E])
        posf = sb("posf", [P, 2 * TOPK])
        posi = [sb(f"posi{i}", [P, 2 * TOPK], U32) for i in range(2)]

        zeros = sb("zeros", [P, D])
        cap_e = sb("cap_e", [P, E])
        count = sb("count", [P, E])
        upto = sb("upto", [E, E])
        tiles_i = sb("tiles_i", [E, 1], I32)
        tiles_s = sb("tiles_s", [E, 1], I32)
        tiles_n = sb("tiles_n", [E, 1])
        last_t = sb("last_t", [E, 1])
        one_skip = sb("one_skip", [E, 2])
        iota_t = sb("iota_t", [E, NT])
        past = sb("past", [E, NT])
        expert_f = sb("expert_f", [1, NT])
        expert_tab = sb("expert_tab", [1, NT], I32)
        full = sb("full", [1, E])
        room = sb("room", [1, E])
        least = sb("least", [1, 1])
        row_f = sb("row_f", [1, NT])
        row_d = sb("row_d", [1, NT])
        row_tab = sb("row_tab", [1, NT], I32)
        pad_f = sb("pad_f", [1, E])
        pad_tab = sb("pad_tab", [1, E], I32)
        row_tag = [sb(f"row_tag{i}", [P, 2]) for i in range(16)]
        tok_in = [sb(f"tok_in{i}", [P, D]) for i in range(8)]
        rows_T = [sb(f"rows_T{i}", [P, 2, DK * P]) for i in range(2)]
        gate = [sb(f"gate{i}", [P, HID]) for i in range(2)]
        hid = [sb(f"hid{i}", [P, HID]) for i in range(2)]
        hid_T = [sb(f"hid_T{i}", [P, 2, P]) for i in range(2)]
        res = [sb(f"res{i}", [P, D]) for i in range(4)]
        mv3 = [sb(f"mv3_{i}", [P, 2]) for i in range(2)]
        h3 = [sb(f"h3_{i}", [P, D]) for i in range(2)]
        got = [sb(f"got{i}", [P, TOPK, D]) for i in range(4)]
        acc0 = [sb(f"acc0_{i}", [P, D]) for i in range(2)]
        acc1 = [sb(f"acc1_{i}", [P, D]) for i in range(2)]

        d_w, d_x, d_c = sem("d_w"), sem("d_x"), sem("d_c")
        d_res = [sem(f"d_res{i}") for i in range(2)]
        d_qw, d_kw, d_stk = sem("d_qw"), sem("d_kw"), sem("d_stk")
        d_m = [sem(f"d_m{i}") for i in range(2)]
        d_mw = [sem(f"d_mw{i}") for i in range(2)]
        d_x2 = [sem(f"d_x2_{i}") for i in range(2)]
        d_scat = [sem(f"d_scat{i}") for i in range(2)]
        d_we, d_zero, d_pad = sem("d_we"), sem("d_zero"), sem("d_pad")
        d_row = [sem(f"d_row{i}") for i in range(8)]
        d_tag = [sem(f"d_tag{i}") for i in range(16)]
        d_eo = [sem(f"d_eo{i}") for i in range(4)]
        d_tok = [sem(f"d_tok{i}") for i in range(8)]
        d_got = [sem(f"d_got{i}") for i in range(4)]
        d_out = [sem(f"d_out{i}") for i in range(4)]
        v_tab, p_tab, v_row = sem("v_tab"), sem("p_tab"), sem("v_row")
        p_tp, a_tp = [sem("p_tp2"), sem("p_tp3")], [sem("a_tp2"), sem("a_tp3")]
        p_gu, a_gate = [sem("p_gu2"), sem("p_gu3")], [sem("a_gate2"), sem("a_gate3")]
        v_hid, p_hp = [sem("v_hid2"), sem("v_hid3")], [sem("p_hp2"), sem("p_hp3")]
        a_hT, p_eo = [sem("a_hT2"), sem("a_hT3")], [sem("p_eo2"), sem("p_eo3")]
        v_tl, v_hl = [sem("v_tl2"), sem("v_tl3")], [sem("v_hl2"), sem("v_hl3")]
        a_wh, v_wl = sem("a_wh"), sem("v_wl")
        v_res = [sem("v_res2"), sem("v_res3")]
        v_s3, v_h3, g_a0, g_a1, v_all = sem("v_s3"), sem("v_h3"), sem("g_a0"), sem("g_a1"), sem("v_all")
        g_num, g_tag = sem("g_num"), sem("g_tag")
        p_xT, p_cT, p_v, p_q, p_k = sem("p_xT"), sem("p_cT"), sem("p_v"), sem("p_q"), sem("p_k")
        p_hT, p_lg, p_pf, p_mT = sem("p_hT"), sem("p_lg"), sem("p_pf"), sem("p_mT")
        p_st, p_pv, p_mx = sem("p_st"), sem("p_pv"), sem("p_mx")
        a_x, a_c, a_v, a_q, a_k = sem("a_x"), sem("a_c"), sem("a_v"), sem("a_q"), sem("a_k")
        a_h, a_e, a_mT, a_exp, a_lam = sem("a_h"), sem("a_e"), sem("a_mT"), sem("a_exp"), sem("a_lam")
        v_q, v_k, v_red, v_mx, v_s1, v_s2 = (sem("v_q"), sem("v_k"), sem("v_red"), sem("v_mx"), sem("v_s1"),
                                             sem("v_s2"))
        v_mxa, v_ps = sem("v_mxa"), sem("v_ps")
        v_rl, v_rlc, v_cb, v_b1, v_b2, v_lam = (sem("v_rl"), sem("v_rlc"), sem("v_cb"), sem("v_b1"), sem("v_b2"),
                                                sem("v_lam"))
        v_rt, v_hot, v_pf, v_pos, v_w = sem("v_rt"), sem("v_hot"), sem("v_pf"), sem("v_pos"), sem("v_w")
        g_set, v_xn, g_qb, g_qs, g_kb, g_ks = (sem("g_set"), sem("v_xn"), sem("g_qb"), sem("g_qs"),
                                               sem("g_kb"), sem("g_ks"))
        g_att, g_x2, v_h2, g_r1, g_r2 = sem("g_att"), sem("g_x2"), sem("v_h2"), sem("g_r1"), sem("g_r2")
        passed = sem("passed")
        SETUP = 21
        N_W = 8
        PW = 2 * 3 * 16
        STK = 4 * 16
        MR = 2 * 16
        SCAT = 2 * 2 * TOPK * 16
        RT = 12

        first, lo, hi, end = -3, 4, NS - 4, NS + 2

        def wait(eng, sem, inc, s, j=0, last=None, plain=False):
            if s.k is None:
                v = inc * s.off + j
                if last is not None:
                    v = min(v, inc * last)
                if v > 0:
                    eng.wait_ge(sem, v)
            else:
                eng.wait_ge(sem, s.k * (s.unroll * inc) + (inc * s.off + j))
                if plain or eng.engine in (mybir.EngineType.SP, mybir.EngineType.Pool):
                    eng.sem_inc(passed, 1)

        def wait_par(eng, sems, inc, s):
            ring = len(sems)
            v = inc * (s.off // ring + 1)
            if s.k is None:
                if v > 0:
                    eng.wait_ge(sems[s.off % ring], v)
            else:
                eng.wait_ge(sems[s.off % ring], s.k * (inc * s.unroll // ring) + v)
                if eng.engine in (mybir.EngineType.SP, mybir.EngineType.Pool):
                    eng.sem_inc(passed, 1)

        def pipeline(eng, body, first, lo, hi, end, unroll):
            for it in range(first, lo):
                body(Step(None, it))
            with eng.Fori(0, (hi - lo) // unroll) as k:
                for off in range(unroll):
                    body(Step(k, lo + off, unroll))
            for it in range(hi, end):
                body(Step(None, it))

        def steps(eng, body):
            pipeline(eng, body, first, lo, hi, end, 2)

        NT_HI = 16 + (NT - 23) // 16 * 16
        TT_HI = (NB - 7) // 8 * 8

        def expert_steps(eng, body):
            pipeline(eng, body, -6, 16, NT_HI, NT + 2, 16)

        def token_steps(eng, body):
            pipeline(eng, body, -6, 8, TT_HI, NB + 2, 8)

        def load(eng, entry, most):
            return nc.values_load(entry, engines=(eng.engine,), min_val=0, max_val=most,
                                  skip_runtime_bounds_check_because="VectorE clamps the tables' entries")

        def pad_rows(eng, i):
            eng.wait_ge(v_row, 1)
            for e in range(i, E, 2):
                r = load(eng, pad_tab[0:1, e:e + 1], E * CAP - P)
                eng.dma_start(rows_dram[bass.ds(r, P), :], zeros[:, :]).then_inc(d_pad, 16)
                eng.dma_start(tags_dram[bass.ds(r, P), :], no_tag[:, :]).then_inc(d_pad, 16)

        def rnd(ap):
            return ap.bitcast(F32R)

        def by_expert(w, e):
            return w[:, e:e + E // 4].rearrange("p e k n -> p (e k n)" if len(w.shape) == 4 else "p e n -> p (e n)")

        pieces = [tuple(by_expert(w, e) for w in ws) for e in range(0, E, E // 4)
                  for ws in ((w_gu_sb, w_gu_lo, w_gu_hi), (w_dn_sb, w_dn_lo, w_dn_hi))]
        pieces += [tuple(w[:, :, :].rearrange("p k n -> p (k n)") for w in (ws_gu_sb, ws_gu_lo, ws_gu_hi)),
                   tuple(w[:, :] for w in (ws_dn_sb, ws_dn_lo, ws_dn_hi))]

        block = st.enter_context(nc.Block())

        @block.sync
        def _(sp):
            sp.dma_start(x_in[:, :, :], x_g[0]).then_inc(d_x, 16)
            for dst, src in ((wq_sb, wqT), (wk_sb, wkT), (wv_sb, wvT), (gw_sb, gate_wT)):
                sp.dma_start(dst[:, :, :], src).then_inc(d_w, 16)
            for n, src in enumerate((lq1, lq2, lk1, lk2)):
                sp.dma_start(lam_in[:, n, :], src.partition_broadcast(P)).then_inc(d_w, 16)

            def step(it):
                a, b, d, ln = it.plus(2), it.plus(1), it.plus(-1), it.plus(3)
                p = it.par()
                if it.k is None and it.off == 0:
                    sp.wait_ge(g_set, SETUP)
                    sp.dma_start(rows_dram.rearrange("(e n) d -> n e d", e=E)[CAP - P:CAP],
                                 zeros[:, :].unsqueeze(1).to_broadcast([P, E, D])).then_inc(d_zero, 16)
                    sp.dma_start(tags_dram.rearrange("(e n) d -> n e d", e=E)[CAP - P:CAP],
                                 no_tag[:, :].unsqueeze(1).to_broadcast([P, E, 2])).then_inc(d_zero, 16)
                if it.is_in(0, NS):
                    wait(sp, a_mT, 2, it, 2)
                    max_rows(it, 1)
                if d.is_in(0, NS):
                    wait(sp, g_x2, 4, d, 4)
                    sp.dma_start(x2_g[bass.ds(d.idx(), 1)].rearrange("g p u d -> (g p) u d"),
                                 x2[1 - p][:, :, :]).then_inc(d_x2[1 - p], 16)
                if b.is_in(0, NS):
                    wait(sp, g_x2, 4, it, 0)
                    sp.dma_start(x_res[1 - p][:, :, :],
                                 x_g[bass.ds(b.idx(), 1)].rearrange("g p u d -> (g p) u d")).then_inc(d_res[1 - p], 16)
                if ln.is_in(0, NS):
                    wait(sp, p_cT, 1, ln)
                    sp.dma_start(c_in[:, :, :],
                                 c_g[bass.ds(ln.idx(), 1)].rearrange("g p u d -> (g p) u d")).then_inc(d_c, 16)
                if a.is_in(0, NS):
                    for n, (done, buf, landed) in enumerate(((g_qs, qp, d_qw), (g_ks, kp, d_kw))):
                        wait(sp, done, 1, a, 1)
                        if n == 0:
                            wait(sp, d_stk, STK, a, -STK)
                        for h in range(2):
                            rows = stack_dram[p, n, h].rearrange("(r d) j t -> (d j) r t", d=HALF)
                            part = buf[:, :, h * SW:(h + 1) * SW]
                            for r, m in ((0, 3), (3, 2), (5, 1)):
                                if n == 0:
                                    src = part[:, 0:m, :]
                                else:
                                    src = part[:, 3 - m:4 - m, :].to_broadcast([P, m, SW])
                                sp.dma_start(rows[:, r:r + m, :], src).then_inc(landed, 16)
                nxt = it.plus(4)
                if nxt.is_in(1, NS):
                    wait(sp, v_xn, 2, nxt)
                    sp.dma_start(x_in[:, :, :],
                                 x_g[bass.ds(nxt.idx(), 1)].rearrange("g p u d -> (g p) u d")).then_inc(d_x, 16)
                if b.is_in(0, NS):
                    wait(sp, a_mT, 2, b, 1)
                    max_rows(b, 0)
                if a.is_in(0, NS):
                    wait(sp, p_st, NCH, it, NCH)
                    wait(sp, d_qw, PW, a, PW)
                    wait(sp, d_kw, PW, a, PW)
                    if a.k is None and a.off < 2:
                        sp.wait_ge(g_set, SETUP)
                    for h in range(2):
                        rows = slice(64 * h, 64 * h + ROWS)
                        sp.dma_start(q_st[p][rows, :, :], stack_dram[p, 0, h]).then_inc(d_stk, 16)
                        sp.dma_start(k_st[p][rows, :, :], stack_dram[p, 1, h]).then_inc(d_stk, 16)
                if it.k is None and 0 <= it.off < lo:
                    e = slice(it.off * E // lo, (it.off + 1) * E // lo)
                    sp.dma_start(w_gu_sb[:, e], w_gu[:, e]).then_inc(d_we, 16)
                    sp.dma_start(w_dn_sb[:, e, :], w_dn[:, e]).then_inc(d_we, 16)
                    if it.off == 0:
                        sp.dma_start(ws_gu_sb[:, :, :], ws_gu).then_inc(d_we, 16)
                        sp.dma_start(ws_dn_sb[:, :], ws_dn).then_inc(d_we, 16)

            def max_rows(s, u):
                p = s.par()
                wait(sp, d_m[u], MR, s, -MR)
                sp.dma_start(max_dram[p, u].rearrange("r h j t -> (r h j) t"), mxT[u][:, :]).then_inc(d_mw[u], 16)
                wait(sp, d_mw[u], 16, s, 16)
                for h in range(2):
                    row = 64 * h + ROWS
                    sp.dma_start(q_st[p][row:row + 2, :, u * P:(u + 1) * P], max_dram[p, u, :, h]
                                 ).then_inc(d_m[u], 16)

            steps(sp, step)
            for i in range(2):
                sp.wait_ge(d_x2[i], 16 * (NS // 2))

            pad_rows(sp, 0)
            sp.wait_ge(d_pad, 32 * E)
            for i in range(2):
                sp.wait_ge(d_scat[i], SCAT * (NS // 2))
            sp.wait_ge(v_row, 3)

            def expert_step(j):
                t = j.plus(6)
                if t.is_in(0, NT):
                    if t.off % 4 == 0:
                        wait(sp, p_tp[0], 1, t, -4)
                        wait(sp, v_res[0], 1, t, -8)
                    r = load(sp, row_tab[0:1, bass.ds(t.idx(), 1)], N_ROWS - P)
                    sp.dma_start(tok_in[t.off % 8][:, :], rows_dram[bass.ds(r, P), :]).then_inc(d_row[t.off % 8], 16)
                    sp.dma_start(row_tag[t.off % 16][:, :], tags_dram[bass.ds(r, P), :]
                                 ).then_inc(d_tag[t.off % 16], 16)

            expert_steps(sp, expert_step)

            sp.wait_ge(p_tp[0], NT)
            for i in range(4):
                sp.wait_ge(d_eo[i], 16 * (NT // 4))

            def token_step(j):
                t = j.plus(6)
                if t.is_in(0, NB):
                    wait(sp, g_a1, 1, t, -7)
                    wait(sp, v_h3, 1, t, -7)
                    sp.dma_start(tok_in[t.off % 8][:, :], x2_dram[bass.ds(t.idx(), 1)].rearrange("g p d -> (g p) d")
                                 ).then_inc(d_tok[t.off % 8], 16)
                t = j.plus(3)
                if t.is_in(0, NB):
                    wait(sp, g_a0, 1, t, -3)
                    sp.dma_start(got[t.off % 4][:, :, :],
                                 routed_t[bass.ds(t.idx(), 1)].rearrange("g p k d -> (g p) k d")
                                 ).then_inc(d_got[t.off % 4], 16)
                t = j.plus(-1)
                if t.is_in(0, NB):
                    wait(sp, v_res[1], 1, t, 1)
                    sp.dma_start(out[bass.ds(t.idx(), 1)].rearrange("g p d -> (g p) d"), res[t.off % 4][:, :]
                                 ).then_inc(d_out[t.off % 4], 16)

            token_steps(sp, token_step)
            for i in range(4):
                sp.wait_ge(d_out[i], 16 * (NB // 4))

        @block.tensor
        def _(pe):
            pe.wait_ge(d_w, 16 * N_W)
            pe.wait_ge(g_set, SETUP)
            M0, M1 = ms_ps

            def scores(s, k):
                u, c = divmod(k, NCH // 2)
                h, p = c // 4, s.par()
                if c == 0:
                    wait(pe, d_m[u], MR, s, MR)
                for i in range(CHUNK):
                    j = CHUNK * (c % 4) + i
                    mm = pe.matmul(st_ps[k % 2][:, i * P:(i + 1) * P],
                                   k_st[p][64 * h:64 * h + KROWS, j, u * P:(u + 1) * P],
                                   q_st[p][64 * h:64 * h + KROWS, j, u * P:(u + 1) * P], start=True, stop=True)
                mm.then_inc(p_st, 1)

            def attend(s, k):
                u, c = divmod(k, NCH // 2)
                if k == 0:
                    wait(pe, a_v, 1, s, 1)
                if c % 4 == 0:
                    wait(pe, v_cb, 4, s, k // 4 - 1)
                for i in range(CHUNK):
                    sub = CHUNK * c + i
                    at = (sub % SHH) * (DH + 1)
                    own = (u * HEADS + sub // 2) * (DH + 1)
                    mm = pe.matmul(o_ps[(k // 4) % 2][:, at:at + WIDE], prob[k % 4][:, i * P:(i + 1) * P],
                                   v_sb[s.par()][:, own:own + WIDE], start=True, stop=True)
                mm.then_inc(p_pv, 1)

            def maxima(s, k):
                u, c = divmod(k, NCH // 2)
                h, p = c // 4, s.par()
                if k == 0:
                    wait(pe, d_stk, STK, s, STK)
                wait(pe, v_red, NCH, s, k - 1)
                for i in range(CHUNK):
                    j = CHUNK * (c % 4) + i
                    mm = pe.matmul(mx_ps[k % 2][:, i * P:(i + 1) * P],
                                   q_st[p][64 * h:64 * h + ROWS, j, u * P:(u + 1) * P],
                                   k_st[p][64 * h:64 * h + ROWS, j, u * P:(u + 1) * P], start=True, stop=True)
                mm.then_inc(p_mx, 1)

            def turn_max(s, u, bank):
                wait(pe, v_mx, 2, s, u + 1, plain=True)
                pe.transpose(bank.bitcast(BF16)[0:2 * SUB, 0:P], mxp[:, u, :], identb[:, :]).then_inc(p_mT, 1)

            def turn(src, bank, done):
                for u in range(2):
                    for h in range(DK):
                        mm = pe.transpose(bank[:, h * SW + u * P:h * SW + (u + 1) * P], src[:, u, h * P:(h + 1) * P],
                                          ident[:, :])
                mm.then_inc(done, 1)

            def project(w, src, bank, done):
                for m in range(2):
                    for h in range(DK):
                        mm = pe.matmul(bank[:, m * SW:(m + 1) * SW], w[:, h, m * P:(m + 1) * P], src[:, h, :],
                                       start=(h == 0), stop=(h == DK - 1))
                mm.then_inc(done, 1)

            def side(it, k):
                a, b, d, r = it.plus(2), it.plus(1), it.plus(-1), it.plus(-2)
                do_a, do_b, do_d = a.is_in(0, NS), b.is_in(0, NS), d.is_in(0, NS)
                if k == 1 and it.is_in(0, NS):
                    turn_max(it, 1, M0)
                if k == 0 and do_a:
                    wait(pe, v_pf, 1, r)
                    wait(pe, a_mT, 2, it, 1, last=NS)
                    wait(pe, v_xn, 2, a, 2)
                    turn(xn, M1, p_xT)
                if k == 2 and do_a:
                    wait(pe, a_mT, 2, it, 2, last=NS)
                    wait(pe, d_c, 16, a, 16)
                    turn(c_in, M0, p_cT)
                if k == 3 and do_b:
                    if do_a:
                        wait(pe, a_x, 1, a, 1)
                    else:
                        wait(pe, a_mT, 2, it, 1, last=NS)
                    wait(pe, a_c, 1, b, 1)
                    for u in range(2):
                        for h in range(DK):
                            mm = pe.matmul(M1[:, u * SW:(u + 1) * SW], cT[b.par()][:, h, u * P:(u + 1) * P],
                                           wv_sb[:, h, :], start=(h == 0), stop=(h == DK - 1))
                    mm.then_inc(p_v, 1)
                if k == 4 and do_a:
                    wait(pe, a_x, 1, a, 1)
                    wait(pe, a_c, 1, a, 1)
                    project(wq_sb, xnT, M0, p_q)
                if k == 5 and do_a:
                    wait(pe, a_v, 1, b, 1)
                    wait(pe, a_c, 1, a, 1)
                    project(wk_sb, cT[a.par()], M1, p_k)
                if k == 6 and do_d:
                    if do_a:
                        wait(pe, v_q, 1, a, 1)
                    else:
                        wait(pe, a_mT, 2, it, 2, last=NS)
                    wait(pe, v_h2, 2, d, 2)
                    turn(h2[d.par()], M0, p_hT)
                if k == 7 and r.is_in(0, NS):
                    if not do_d:
                        wait(pe, a_e, 1, d)
                    if do_a:
                        wait(pe, v_k, 1, a, 1)
                    wait(pe, v_hot, 1, r, 1)
                    pe.matmul(M1[:, 2 * E:4 * E], upper[:, :], hots[:, :, :], start=True, stop=True)
                    pe.matmul(M1[:, 4 * E:6 * E], onesb[:, :], hots[:, :, :], start=True, stop=True).then_inc(p_pf, 1)
                if k == 7 and do_d:
                    if do_a:
                        wait(pe, v_k, 1, a, 1)
                    else:
                        wait(pe, a_v, 1, b, 1, last=NS)
                        wait(pe, a_mT, 2, it, 1, last=NS)
                    wait(pe, a_h, 1, d, 1)
                    for u in range(2):
                        for h in range(DK):
                            mm = pe.matmul(M1[:, u * E:(u + 1) * E], h2T[:, h, u * P:(u + 1) * P], gw_sb[:, h, :],
                                           start=(h == 0), stop=(h == DK - 1))
                    mm.then_inc(p_lg, 1)
                if k == 11 and do_b:
                    wait(pe, v_pf, 1, r, 1)
                    wait(pe, a_e, 1, d, 1, last=NS)
                    if d.k is None and d.off < 0 and do_a:
                        wait(pe, v_k, 1, a, 1)
                    turn_max(b, 0, M1)
                if do_b:
                    for n in MAX_SLOTS.get(k, ()):
                        maxima(b, n)

            def step(it):
                d = it.plus(-1)
                for k in range(NCH):
                    cur, prev = it.is_in(0, NS), k < 2 and d.is_in(0, NS)
                    if cur or prev or k >= 2:
                        if it.is_in(0, NS + (1 if k < 2 else 0)):
                            wait(pe, a_exp, NCH, it, k - 1)
                    if cur:
                        scores(it, k)
                    if prev:
                        attend(d, NCH + k - 2)
                    elif cur and k >= 2:
                        attend(it, k - 2)
                    side(it, k)

            steps(pe, step)

            pe.wait_ge(v_tab, 1)
            pe.wait_ge(a_e, NS)
            pe.wait_ge(v_pf, NS)
            pe.transpose(M0[0:E, 0:P], count[:, :], ident[:, :]).then_inc(p_tab, 1)
            pe.wait_ge(v_tab, 10)
            pe.matmul(M1[0:E, 0:1], upto[:, :], tiles_n[:, :], start=True, stop=True).then_inc(p_tab, 1)
            pe.wait_ge(v_tab, 13)
            pe.matmul(M0[0:1, 0:NT], one_skip[:, 0:1], past[:, :], start=True, stop=True)
            pe.matmul(M1[0:1, 0:NT], one_skip[:, 1:2], past[:, :], start=True, stop=True).then_inc(p_tab, 1)

            pe.wait_ge(a_exp, NCH * NS)
            pe.wait_ge(v_red, NCH * NS)
            pe.wait_ge(v_cb, 4 * NS)
            pe.wait_ge(v_row, 3)
            pe.wait_ge(v_wl, len(pieces))

            def product(out_ps, parts, high, low, start, stop):
                pe.matmul(out_ps, rnd(parts[:, 0, :]), rnd(high), start=start, stop=False)
                pe.matmul(out_ps, rnd(parts[:, 0, :]), rnd(low), start=False, stop=False)
                return pe.matmul(out_ps, rnd(parts[:, 1, :]), rnd(high), start=False, stop=stop)

            def ffn(ph, n, j, turned, free_in, w_up, w_down):
                up = w_up(j.plus(1)) if j.plus(1).is_in(0, n) else None
                down = w_down(j.plus(-1)) if j.plus(-1).is_in(0, n) else None
                t = j.plus(2)
                if t.is_in(0, n):
                    turned(t)
                    for h in range(DK):
                        mm = pe.transpose(tp_ps[t.off % 2][:, h * P:(h + 1) * P],
                                          free_in(t)[:, h * P:(h + 1) * P], ident[:, :])
                    mm.then_inc(p_tp[ph], 1)
                t = j.plus(1)
                if t.is_in(0, n):
                    wait(pe, v_tl[ph], 1, t, 1)
                    for h in range(DK):
                        high, low = up(h)
                        mm = product(gu_ps[t.off % 2][:, 0:2 * HID], rows_T[t.off % 2][:, :, h * P:(h + 1) * P],
                                     high, low, h == 0, h == DK - 1)
                    mm.then_inc(p_gu[ph], 1)
                t = j
                if t.is_in(0, n):
                    wait(pe, v_hid[ph], 1, t, 1)
                    pe.transpose(hp_ps[t.off % 2][:, 0:P], hid[t.off % 2][:, :], ident[:, :]).then_inc(p_hp[ph], 1)
                t = j.plus(-1)
                if t.is_in(0, n):
                    wait(pe, v_hl[ph], 1, t, 1)
                    wait(pe, v_res[ph], 1, t, -1)
                    product(eo_ps[t.off % 2][:, 0:D], hid_T[t.off % 2], down[0], down[1], True,
                            True).then_inc(p_eo[ph], 1)

            held = {}

            def expert_of(t):
                if (t.k is None, t.off) not in held:
                    held[t.k is None, t.off] = load(pe, expert_tab[0:1, bass.ds(t.idx(), 1)], E - 1)
                return held[t.k is None, t.off]

            def routed_up(t):
                e = expert_of(t)
                return lambda h: [w[:, bass.ds(e, 1), h, :].rearrange("p e n -> p (e n)") for w in (w_gu_hi, w_gu_lo)]

            def routed_down(t):
                e = expert_of(t)
                return [w[:, bass.ds(e, 1), :].rearrange("p e n -> p (e n)") for w in (w_dn_hi, w_dn_lo)]

            expert_steps(pe, lambda j: ffn(0, NT, j, lambda t: wait_par(pe, d_row, 16, t),
                                           lambda t: tok_in[t.off % 8], routed_up, routed_down))
            pe.wait_ge(v_res[0], NT)
            token_steps(pe, lambda j: ffn(1, NB, j, lambda t: wait(pe, v_h3, 1, t, 1), lambda t: h3[t.off % 2],
                                          lambda t: lambda h: (ws_gu_hi[:, h, :], ws_gu_lo[:, h, :]),
                                          lambda t: (ws_dn_hi[:, :], ws_dn_lo[:, :])))

        @block.scalar
        def _(act):
            M0, M1 = ms_ps
            act.wait_ge(v_lam, 2)
            nc.scalar.activation(lam_e[:, :], lam_s[:, :], ACT.Exp).then_inc(a_lam, 1)

            def copy_max(s, u, bank):
                wait(act, p_mT, 2, s, u + 1)
                wait(act, d_mw[u], 16, s)
                nc.scalar.activation(mxT[u][:, :], bank.bitcast(BF16)[0:2 * SUB, 0:P], ACT.Copy).then_inc(a_mT, 1)

            def step(it):
                a, b, d = it.plus(2), it.plus(1), it.plus(-1)
                do_a, do_b, do_c, do_d = a.is_in(0, NS), b.is_in(0, NS), it.is_in(0, NS), d.is_in(0, NS)
                for k in range(NCH):
                    if do_c:
                        wait(act, p_st, NCH, it, k + 1)
                        wait(act, p_pv, NCH, it, k - 3)
                        nc.scalar.activation(prob[k % 4][:, :], st_ps[k % 2][:, :], ACT.Exp,
                                             scale=float(HALF) ** -0.5).then_inc(a_exp, 1)
                    if k == 1 and do_c:
                        copy_max(it, 1, M0)
                    if k == 0 and do_a:
                        wait(act, p_xT, 1, a, 1)
                        wait(act, p_q, 1, a)
                        nc.scalar.activation(xnT[:, :, :], M1[:, :], ACT.Copy).then_inc(a_x, 1)
                    if k == 2 and do_a:
                        wait(act, p_cT, 1, a, 1)
                        wait(act, p_v, 1, it, 1)
                        wait(act, p_k, 1, it, 1)
                        nc.scalar.activation(cT[a.par()][:, :, :], M0[:, :], ACT.Copy).then_inc(a_c, 1)
                    if k == 3 and do_b:
                        wait(act, p_v, 1, b, 1)
                        wait(act, p_pv, NCH, it)
                        nc.scalar.activation(v_sb[b.par()][:, 0:VW].rearrange("p (u h d) -> p u h d", u=2,
                                                                              h=HEADS)[:, :, :, 0:DH],
                                             M1[:, :].rearrange("p (u h d) -> p u h d", u=2, h=HEADS),
                                             ACT.Copy).then_inc(a_v, 1)
                    if k == 4 and do_a:
                        wait(act, p_q, 1, a, 1)
                        wait(act, d_qw, PW, a)
                        nc.scalar.activation(qp[:, 0, :], M0[:, :], ACT.Copy).then_inc(a_q, 1)
                    if k == 5 and do_a:
                        wait(act, p_k, 1, a, 1)
                        wait(act, d_kw, PW, a)
                        nc.scalar.activation(kp[:, 0, :], M1[:, :], ACT.Copy).then_inc(a_k, 1)
                    if k == 6 and do_d:
                        wait(act, p_hT, 1, d, 1)
                        wait(act, p_lg, 1, d)
                        nc.scalar.activation(h2T[:, :, :], M0[:, :], ACT.Copy).then_inc(a_h, 1)
                    if k == 7 and do_d:
                        wait(act, p_lg, 1, d, 1)
                        wait(act, v_rt, RT, d)
                        nc.scalar.activation(ez[:, :], M1[:, 0:2 * E], ACT.Exp, scale=-1.0).then_inc(a_e, 1)
                    if k == 11 and do_b:
                        copy_max(b, 0, M1)

            steps(act, step)

            act.wait_ge(d_we, 16 * (2 * lo + 2))
            act.wait_ge(p_mx, NCH * NS)
            act.wait_ge(p_st, NCH * NS)
            act.wait_ge(d_stk, STK * NS)
            for i in range(2):
                act.wait_ge(d_m[i], MR * NS)
            act.wait_ge(p_pv, NCH * NS)
            act.wait_ge(g_qs, NS)
            act.wait_ge(g_ks, NS)
            act.wait_ge(d_qw, PW * NS)
            act.wait_ge(d_kw, PW * NS)
            for weights, _, high in pieces:
                nc.scalar.activation(rnd(high), weights, ACT.Copy).then_inc(a_wh, 1)
            pad_rows(act, 1)

            def ffn(ph, n, j):
                t = j.plus(2)
                if t.is_in(0, n):
                    wait(act, p_tp[ph], 1, t, 1)
                    nc.scalar.activation(rnd(rows_T[t.off % 2][:, 0, :]), tp_ps[t.off % 2][:, 0:D],
                                         ACT.Copy).then_inc(a_tp[ph], 1)
                t = j.plus(1)
                if t.is_in(0, n):
                    wait(act, p_gu[ph], 1, t, 1)
                    nc.scalar.activation(gate[t.off % 2][:, :], gu_ps[t.off % 2][:, 0:HID],
                                         ACT.Silu).then_inc(a_gate[ph], 1)
                t = j
                if t.is_in(0, n):
                    wait(act, p_hp[ph], 1, t, 1)
                    nc.scalar.activation(rnd(hid_T[t.off % 2][:, 0, :]), hp_ps[t.off % 2][:, 0:P],
                                         ACT.Copy).then_inc(a_hT[ph], 1)

            expert_steps(act, lambda j: ffn(0, NT, j))
            token_steps(act, lambda j: ffn(1, NB, j))

        @block.vector
        def _(dve):
            v = nc.vector
            M0, M1 = ms_ps
            dve.wait_ge(d_w, 16 * N_W)
            v.tensor_tensor(lam_p[:, :, :], lam_in[:, 0:2, :], lam_in[:, 2:4, :], ALU.mult).then_inc(v_lam, 1)
            dve.wait_ge(v_lam, 1)
            v.tensor_reduce(lam_s[:, :], lam_p[:, :, :], AX.X, ALU.add).then_inc(v_lam, 1)
            dve.wait_ge(a_lam, 1)
            dve.wait_ge(g_set, SETUP)
            cf = coef[:, :].rearrange("p (h two) -> p h two", two=2)
            v.tensor_scalar(lam_p[:, 0, 0:1], lam_e[:, 1:2], lam_e[:, 0:1], -LAMBDA_INIT, ALU.subtract,
                            ALU.add).then_inc(v_lam, 1)
            dve.wait_ge(v_lam, 3)
            v.tensor_copy(cf[:, :, 1], lam_p[:, 0, 0:1].to_broadcast([P, SHH // 2])).then_inc(v_lam, 1)
            dve.wait_ge(v_lam, 4)

            def rest(s, bank, a_done, part, tmp, g_done, v_done):
                wait(dve, a_done, 1, s, 1)
                wait(dve, g_done, 1, s)
                v.tensor_tensor(tmp[:, :], bank[:, :], part[:, 0, :], ALU.subtract).then_inc(v_done, 1)

            def reduce_max(s, k):
                u, c = divmod(k, NCH // 2)
                wait(dve, p_mx, NCH, s, k + 1)
                if c == 0:
                    wait(dve, v_mxa, 2, s, u - 1)
                v.tensor_reduce(mx[:, u, c * CHUNK:(c + 1) * CHUNK],
                                mx_ps[k % 2][:, :].rearrange("p (c n) -> p c n", c=CHUNK), AX.X,
                                ALU.max).then_inc(v_red, 1)
                if c == NCH // 2 - 1:
                    wait(dve, v_red, NCH, s, k + 1)
                    wait(dve, p_mT, 2, s, u - 1)
                    v.tensor_copy(mxp[:, u, 0:SUB], mx[:, u, :]).then_inc(v_mxa, 1)
                    wait(dve, v_mxa, 2, s, u + 1)
                    v.tensor_tensor(mxp[:, u, SUB:2 * SUB], mx[:, u, :], mxp[:, u, 0:SUB],
                                    ALU.subtract).then_inc(v_mx, 1)

            def combine(s, h):
                o = o_ps[h % 2][:, 0:SHH * (DH + 1)].rearrange("p (s d) -> p s d", s=SHH)
                wait(dve, p_pv, NCH, s, 4 * (h + 1))
                wait(dve, v_cb, 4, s, h)
                v.reciprocal(rl[:, :], o[:, :, DH]).then_inc(v_rl, 1)
                wait(dve, v_rl, 4, s, h + 1)
                v.tensor_tensor(rlc[:, :], rl[:, :], coef[:, :], ALU.mult).then_inc(v_rlc, 1)
                wait(dve, v_rlc, 4, s, h + 1)
                wait(dve, g_att, 4, s, h - 1)
                v.tensor_tensor(o_sc[h % 2][:, :, :], o[:, :, 0:DH],
                                rlc[:, :].unsqueeze(2).to_broadcast([P, SHH, DH]), ALU.mult).then_inc(v_cb, 1)

            def stats(s, src, st_b, mv, ve, v_b, v_s, v_done):
                wait(dve, v_done, 2, s)
                for u in range(2):
                    v.bn_stats(st_b[:, u, :], src[:, u, :]).then_inc(v_b, 1)
                for u in range(2):
                    wait(dve, v_b, 2, s, u + 1, plain=True)
                    v.bn_aggr(mv[:, u, :], st_b[:, u, :]).then_inc(v_s, 1)
                wait(dve, v_s, 3, s, 2)
                v.tensor_scalar(ve[:, :], mv[:, :, 1], EPS, None, ALU.add).then_inc(v_s, 1)

            def norm(s, src, mv, dst, g_r, v_done):
                wait(dve, g_r, 1, s, 1)
                for u in range(2):
                    v.tensor_scalar(dst[:, u, :], src[:, u, :], mv[:, u, 0:1], mv[:, u, 1:2], ALU.subtract,
                                    ALU.mult).then_inc(v_done, 1)

            def best_two(s):
                wait(dve, a_e, 1, s, 1)
                v.tensor_scalar(ez1[:, :], ez[:, :], 1.0, None, ALU.add).then_inc(v_rt, 1)
                wait(dve, v_rt, RT, s, 1)
                v.reciprocal(score[:, :, :], ez1[:, :].rearrange("p (u e) -> p u e", u=2)).then_inc(v_rt, 1)
                wait(dve, v_rt, RT, s, 2, plain=True)
                for u in range(2):
                    v.max(top[:, u, :], score[:, u, :]).then_inc(v_rt, 1)
                wait(dve, v_rt, RT, s, 4, plain=True)
                for u in range(2):
                    v.max_index(topi[:, u, :], top[:, u, :], score[:, u, :]).then_inc(v_rt, 1)
                v.tensor_tensor(den[:, :], top[:, :, 0], top[:, :, 1], ALU.add).then_inc(v_rt, 1)

            def choice(s):
                wait(dve, v_rt, RT, s, 7)
                v.tensor_copy(topf[:, :, :], topi[:, :, 0:TOPK]).then_inc(v_rt, 1)
                v.tensor_scalar(den1[:, :], den[:, :], 1e-20, None, ALU.add).then_inc(v_rt, 1)
                wait(dve, v_rt, RT, s, 9)
                v.tensor_tensor(hot[:, :, :, :].rearrange("p u k e -> p (u k) e"),
                                iota_e[:, :].unsqueeze(1).to_broadcast([P, 2 * TOPK, E]),
                                topf[:, :, :].rearrange("p u k -> p (u k)").unsqueeze(2)
                                .to_broadcast([P, 2 * TOPK, E]), ALU.is_equal).then_inc(v_rt, 1)
                v.reciprocal(rden[:, :], den1[:, :]).then_inc(v_rt, 1)
                wait(dve, v_rt, RT, s, 11)
                wait_par(dve, d_scat, SCAT, s.plus(-2))
                v.tensor_tensor(hots[:, :, :], hot[:, :, 0, :], hot[:, :, 1, :], ALU.add).then_inc(v_hot, 1)
                v.scalar_tensor_tensor(
                    tag[s.par()][:, :, 1].rearrange("p (u k) -> p u k", u=2), top[:, :, 0:TOPK],
                    ROUTE_SCALE, rden[:, :].unsqueeze(2).to_broadcast([P, 2, TOPK]), ALU.mult,
                    ALU.mult).then_inc(v_rt, 1)

            def places(s):
                tot = M1[:, 4 * E:6 * E].rearrange("p (u e) -> p u e", u=2)
                wait(dve, p_pf, 1, s, 1)
                wait(dve, a_e, 1, s.plus(1), 1, last=NS)
                v.tensor_tensor(base[:, 1, :], base[:, 0, :], tot[:, 0, :], ALU.add).then_inc(v_ps, 1)
                wait(dve, v_ps, 3, s, 1)
                v.tensor_tensor(pb[:, :, :], M1[:, 2 * E:4 * E].rearrange("p (u e) -> p u e", u=2), base[:, :, :],
                                ALU.add).then_inc(v_ps, 1)
                wait(dve, v_ps, 3, s, 2)
                v.tensor_tensor(base[:, 0, :], base[:, 1, :], tot[:, 1, :], ALU.add).then_inc(v_pf, 1)
                v.tensor_tensor(hotp[:, :, :, :], hot[:, :, :, :],
                                pb[:, :, :].unsqueeze(2).to_broadcast([P, 2, TOPK, E]), ALU.mult).then_inc(v_ps, 1)

            def positions(s):
                wait(dve, v_ps, 3, s, 3)
                v.tensor_reduce(posf[:, :], hotp[:, :, :, :].rearrange("p u k e -> p (u k) e"), AX.X,
                                ALU.add).then_inc(v_w, 1)
                wait(dve, v_w, 1, s, 1)
                wait(dve, v_pf, 1, s, 1)
                wait_par(dve, d_scat, SCAT, s.plus(-2))
                v.tensor_copy(posi[s.par()][:, :], posf[:, :]).then_inc(v_pos, 1)

            def step(it):
                a, b, d, ln, r = it.plus(2), it.plus(1), it.plus(-1), it.plus(3), it.plus(-2)
                do_a, do_b, do_d, do_ln, do_r = (a.is_in(0, NS), b.is_in(0, NS), d.is_in(0, NS), ln.is_in(0, NS),
                                                 r.is_in(0, NS))
                for k in range(NCH):
                    if k == 0 and do_r:
                        best_two(r)
                    if k == 1 and do_d:
                        combine(d, 3)
                    if k == 2 and do_r:
                        choice(r)
                    if k == 3 and do_d:
                        wait(dve, g_x2, 4, d, 4)
                        stats(d, x2[d.par()], bs2, mv2, ve2, v_b2, v_s2, v_h2)
                    if k == 4 and do_a:
                        rest(a, M0, a_q, qp, q_rest, g_qs, v_q)
                    if k == 5 and do_a:
                        rest(a, M1, a_k, kp, k_rest, g_ks, v_k)
                    if do_b:
                        for n in MAX_SLOTS.get(k, ()):
                            reduce_max(b, n)
                    if k == 4 and do_d:
                        wait_par(dve, d_scat, SCAT, d.plus(-2))
                        if d.k is not None or d.off >= 2:
                            wait(dve, p_hT, 1, d.plus(-1))
                        norm(d, x2[d.par()], mv2, h2[d.par()], g_r2, v_h2)
                        v.tensor_copy(mv_all[:, bass.ds(d.idx(), 1), :].rearrange("p g c -> p (g c)"),
                                      mv2[:, :, :].rearrange("p u c -> p (u c)")).then_inc(v_all, 1)
                    if k in (6, 11, 13) and it.is_in(0, NS):
                        combine(it, (6, 11, 13).index(k))
                    if k == 7 and do_ln:
                        wait(dve, d_x, 16, ln, 16)
                        stats(ln, x_in, bs1, mv1, ve1, v_b1, v_s1, v_xn)
                    if k == 8 and do_ln:
                        wait(dve, p_xT, 1, ln)
                        norm(ln, x_in, mv1, xn, g_r1, v_xn)
                    if k == 9 and do_r:
                        places(r)
                    if k == 10 and do_r:
                        positions(r)

            steps(dve, step)

            n_tab = [0]

            def tab(ins):
                ins.then_inc(v_tab, 1)
                n_tab[0] += 1
                dve.wait_ge(v_tab, n_tab[0])

            dve.wait_ge(v_pf, NS)
            tab(v.tensor_tensor(count[:, :], base[:, 0, :], cap_e[:, :], ALU.subtract))
            tab(v.tensor_scalar(full[:, :], count[0:1, :], float(CAP - P), None, ALU.is_gt))
            tab(v.scalar_tensor_tensor(room[:, :], full[:, :], float(1 << 20), base[0:1, 0, :], ALU.mult, ALU.add))
            tab(v.tensor_reduce(least[:, :], room[:, :], AX.X, ALU.min))
            tab(v.scalar_tensor_tensor(room[:, :], base[0:1, 0, :], least[:, 0:1], full[:, :], ALU.subtract,
                                       ALU.mult))
            tab(v.tensor_tensor(pad_f[:, :], base[0:1, 0, :], room[:, :], ALU.subtract))
            v.tensor_copy(pad_tab[:, :], pad_f[:, :]).then_inc(v_row, 1)
            dve.wait_ge(p_tab, 1)
            tab(v.tensor_scalar(tiles_n[:, :], M0[0:E, 0:1], float(P - 1), None, ALU.add))
            tab(v.tensor_copy(tiles_i[:, :], tiles_n[:, :]))
            tab(v.tensor_scalar(tiles_s[:, :], tiles_i[:, :], 7, None, ALU.logical_shift_right))
            tab(v.tensor_copy(tiles_n[:, :], tiles_s[:, :]))
            tab(v.tensor_scalar(one_skip[:, 1:2], tiles_n[:, :], float(-P), float(CAP), ALU.mult, ALU.add))
            dve.wait_ge(p_tab, 2)
            tab(v.tensor_copy(last_t[:, :], M1[0:E, 0:1]))
            tab(v.tensor_scalar(past[:, :], iota_t[:, :], last_t[:, 0:1], None, ALU.is_ge))
            dve.wait_ge(p_tab, 3)
            v.tensor_scalar(expert_tab[:, :], M0[0:1, 0:NT], float(E - 1), None, ALU.min).then_inc(v_row, 1)
            tab(v.scalar_tensor_tensor(row_f[:, :], iota_t[0:1, :], float(P), M1[0:1, 0:NT], ALU.mult, ALU.add))
            tab(v.tensor_scalar(past[0:1, :], row_f[:, :], float(E * CAP), None, ALU.is_ge))
            tab(v.scalar_tensor_tensor(row_d[:, :], row_f[:, :], pad_f[:, 0:1], past[0:1, :], ALU.subtract,
                                       ALU.mult))
            v.tensor_tensor(row_tab[:, :], row_f[:, :], row_d[:, :], ALU.subtract).then_inc(v_row, 1)

            for n, (weights, low, high) in enumerate(pieces):
                dve.wait_ge(a_wh, n + 1)
                v.tensor_tensor(rnd(low), weights, high, ALU.subtract).then_inc(v_wl, 1)

            def rows_low(ph, n, j):
                t = j.plus(2)
                if t.is_in(0, n):
                    wait(dve, a_tp[ph], 1, t, 1)
                    v.tensor_tensor(rnd(rows_T[t.off % 2][:, 1, :]), tp_ps[t.off % 2][:, 0:D],
                                    rows_T[t.off % 2][:, 0, :], ALU.subtract).then_inc(v_tl[ph], 1)

            def hidden_low(ph, n, j):
                t = j
                if t.is_in(0, n):
                    wait(dve, a_hT[ph], 1, t, 1)
                    v.tensor_tensor(rnd(hid_T[t.off % 2][:, 1, :]), hp_ps[t.off % 2][:, 0:P],
                                    hid_T[t.off % 2][:, 0, :], ALU.subtract).then_inc(v_hl[ph], 1)

            def hidden(ph, n, j):
                t = j.plus(1)
                if t.is_in(0, n):
                    wait(dve, a_gate[ph], 1, t, 1)
                    v.tensor_tensor(hid[t.off % 2][:, :], gate[t.off % 2][:, :], gu_ps[t.off % 2][:, HID:2 * HID],
                                    ALU.mult).then_inc(v_hid[ph], 1)

            def expert_step(j):
                rows_low(0, NT, j)
                hidden(0, NT, j)
                hidden_low(0, NT, j)
                t = j.plus(-1)
                if t.is_in(0, NT):
                    wait(dve, p_eo[0], 1, t, 1)
                    wait_par(dve, d_eo, 16, t.plus(-4))
                    wait_par(dve, d_tag, 16, t)
                    v.tensor_scalar(res[t.off % 4][:, :], eo_ps[t.off % 2][:, 0:D], row_tag[t.off % 16][:, 1:2],
                                    None, ALU.mult).then_inc(v_res[0], 1)

            expert_steps(dve, expert_step)
            for i in range(4):
                dve.wait_ge(d_eo[i], 16 * (NT // 4))

            dve.wait_ge(v_all, NS)

            def token_step(j):
                t = j.plus(4)
                if t.is_in(0, NB):
                    c = 2 * (t.off % 2)
                    grp = t.off // 2 if t.k is None else t.k * (t.unroll // 2) + t.off // 2
                    wait(dve, v_h3, 1, t, -1)
                    v.tensor_copy(mv3[t.off % 2][:, :],
                                  mv_all[:, bass.ds(grp, 1), c:c + 2].rearrange("p g c -> p (g c)")
                                  ).then_inc(v_s3, 1)
                t = j.plus(3)
                if t.is_in(0, NB):
                    wait_par(dve, d_tok, 16, t)
                    wait(dve, v_s3, 1, t, 1)
                    wait(dve, p_tp[1], 1, t, -1)
                    v.tensor_scalar(h3[t.off % 2][:, :], tok_in[t.off % 8][:, :], mv3[t.off % 2][:, 0:1],
                                    mv3[t.off % 2][:, 1:2], ALU.subtract, ALU.mult).then_inc(v_h3, 1)
                rows_low(1, NB, j)
                hidden(1, NB, j)
                hidden_low(1, NB, j)
                t = j.plus(-1)
                if t.is_in(0, NB):
                    wait(dve, g_a1, 1, t, 1)
                    wait(dve, p_eo[1], 1, t, 1)
                    wait_par(dve, d_out, 16, t.plus(-4))
                    v.tensor_tensor(res[t.off % 4][:, :], eo_ps[t.off % 2][:, 0:D], acc1[t.off % 2][:, :],
                                    ALU.add).then_inc(v_res[1], 1)

            token_steps(dve, token_step)

        @block.gpsimd
        def _(gp):
            g = nc.gpsimd
            n = 0
            for ins in ([g.memset(ident[:, :], 0.0), g.memset(identb[:, :], 0.0), g.memset(upper[:, :], 1.0),
                         g.memset(onesb[:, :], 1.0), g.memset(neghalf[:, :], -0.5), g.memset(coef[:, :], 1.0),
                         g.memset(zeros[:, :], 0.0), g.memset(no_tag[:, :], 0.0), g.memset(upto[:, :], 1.0), g.memset(one_skip[:, :], 1.0)]
                        + [g.memset(k_st[i][:, :, :], -1.0) for i in range(2)]
                        + [g.memset(v_sb[i][:, :], 1.0) for i in range(2)]):
                ins.then_inc(g_set, 1)
                n += 1
            gp.wait_ge(g_set, n)
            for m in (ident, identb):
                g.affine_select(out=m[:, :], in_=m[:, :], compare_op=ALU.not_equal, fill=1.0, base=0,
                                pattern=[[-1, P]], channel_multiplier=1)
            g.affine_select(out=upper[:, :], in_=upper[:, :], compare_op=ALU.is_gt, fill=0.0, base=0,
                            pattern=[[1, P]], channel_multiplier=-1).then_inc(g_set, 1)
            g.iota(iota_e[:, :], pattern=[[1, E]], base=0, channel_multiplier=0,
                   allow_small_or_imprecise_dtypes=True).then_inc(g_set, 1)
            g.iota(base[:, 0, :], pattern=[[CAP, E]], base=0, channel_multiplier=0,
                   allow_small_or_imprecise_dtypes=True).then_inc(g_set, 1)
            g.iota(cap_e[:, :], pattern=[[CAP, E]], base=0, channel_multiplier=0,
                   allow_small_or_imprecise_dtypes=True).then_inc(g_set, 1)
            g.iota(iota_t[:, :], pattern=[[1, NT]], base=0, channel_multiplier=0,
                   allow_small_or_imprecise_dtypes=True)
            g.iota(number[:, :].rearrange("p (u k) -> p u k", u=2), pattern=[[P * TOPK, 2], [1, TOPK]], base=0,
                   channel_multiplier=TOPK, allow_small_or_imprecise_dtypes=True).then_inc(g_set, 1)
            g.iota(no_tag.bitcast(U32)[:, 0:1], pattern=[[0, 1]], base=TOPK * T,
                   channel_multiplier=0).then_inc(g_set, 1)
            g.affine_select(out=upto[:, :], in_=upto[:, :], compare_op=ALU.is_ge, fill=0.0, base=0,
                            pattern=[[1, E]], channel_multiplier=-1).then_inc(g_set, 1)
            assert n + 7 == SETUP
            gp.wait_ge(g_set, SETUP)

            def deviation(s, ve, mv, v_s, g_r):
                wait(gp, v_s, 3, s, 3)
                g.tensor_tensor(mv[:, :, 1], ve[:, :], neghalf[:, :], ALU.pow).then_inc(g_r, 1)

            def split(s, tmp, part, v_done, g_b, g_done, landed):
                wait(gp, v_done, 1, s, 1)
                wait(gp, landed, PW, s)
                g.tensor_copy(part[:, 1, :], tmp[:, :]).then_inc(g_b, 1)
                wait(gp, g_b, 1, s, 1)
                g.tensor_tensor(part[:, 2, :], tmp[:, :], part[:, 1, :], ALU.subtract).then_inc(g_done, 1)

            def residual(s, h):
                u, m = divmod(h, 2)
                p = s.par()
                wait(gp, v_cb, 4, s, h + 1)
                wait(gp, g_x2, 4, s, h)
                two = o_sc[h % 2][:, :, :].rearrange("p (h two) d -> p h two d", two=2)
                g.tensor_tensor(att[:, :, :], two[:, :, 0, :], two[:, :, 1, :], ALU.add).then_inc(g_att, 1)
                wait(gp, g_att, 4, s, h + 1)
                if h == 0:
                    wait_par(gp, d_res, 16, s)
                    wait_par(gp, d_x2, 16, s.plus(-2))
                    wait(gp, v_h2, 2, s.plus(-1))
                g.tensor_tensor(x2[p][:, u, m * P:(m + 1) * P].rearrange("p (h d) -> p h d", d=DH), att[:, :, :],
                                x_res[p][:, u, m * P:(m + 1) * P].rearrange("p (h d) -> p h d", d=DH),
                                ALU.add).then_inc(g_x2, 1)

            def numbers(s):
                wait_par(gp, d_scat, SCAT, s.plus(-2))
                wait(gp, g_num, 1, s)
                g.tensor_copy(tag[s.par()].bitcast(U32)[:, :, 0], number[:, :]).then_inc(g_tag, 1)
                wait(gp, g_tag, 1, s, 1)
                g.tensor_scalar(number[:, :], number[:, :], float(TOPK * SW), None, ALU.add).then_inc(g_num, 1)

            def scatter(s, u):
                p = s.par()
                if s.k is None and s.off == 0:
                    gp.wait_ge(d_zero, 32)
                wait(gp, v_pos, 1, s, 1)
                wait(gp, v_h2, 2, s, 2)
                wait(gp, v_rt, RT, s, RT)
                wait(gp, g_tag, 1, s, 1)
                for k in range(TOPK):
                    c = TOPK * u + k
                    g.indirect_dma_start(
                        rows_dram[:, :], bass.IndirectOffsetOnAxis(ap=posi[p][:, c:c + 1], axis=0),
                        h2[p][:, u, :], None).then_inc(d_scat[p], 16)
                    g.indirect_dma_start(
                        tags_dram[:, :], bass.IndirectOffsetOnAxis(ap=posi[p][:, c:c + 1], axis=0),
                        tag[p][:, c, :], None).then_inc(d_scat[p], 16)

            def step(it):
                a, d, ln, r = it.plus(2), it.plus(-1), it.plus(3), it.plus(-2)
                do_c = it.is_in(0, NS)
                if d.is_in(0, NS):
                    residual(d, 3)
                    deviation(d, ve2, mv2, v_s2, g_r2)
                if a.is_in(0, NS):
                    split(a, q_rest, qp, v_q, g_qb, g_qs, d_qw)
                    split(a, k_rest, kp, v_k, g_kb, g_ks, d_kw)
                if do_c:
                    residual(it, 0)
                if ln.is_in(0, NS):
                    deviation(ln, ve1, mv1, v_s1, g_r1)
                if do_c:
                    residual(it, 1)
                if r.is_in(0, NS):
                    numbers(r)
                if r.is_in(0, NS):
                    scatter(r, 0)
                if do_c:
                    residual(it, 2)
                if r.is_in(0, NS):
                    scatter(r, 1)

            steps(gp, step)

            def expert_step(j):
                t = j.plus(-1)
                if t.is_in(0, NT):
                    wait_par(gp, d_tag, 16, t)
                    wait(gp, v_res[0], 1, t, 1)
                    g.indirect_dma_start(routed_dram[:, :], bass.IndirectOffsetOnAxis(
                        ap=row_tag[t.off % 16].bitcast(U32)[:, 0:1], axis=0), res[t.off % 4][:, :], None,
                        bounds_check=TOPK * T - 1, oob_is_err=False).then_inc(d_eo[t.off % 4], 16)

            expert_steps(gp, expert_step)

            def token_step(j):
                t = j
                if t.is_in(0, NB):
                    p = t.off % 2
                    wait_par(gp, d_got, 16, t)
                    wait(gp, g_a1, 1, t, -1)
                    g.tensor_tensor(acc0[p][:, :], got[t.off % 4][:, 0, :], got[t.off % 4][:, 1, :],
                                    ALU.add).then_inc(g_a0, 1)
                    wait_par(gp, d_tok, 16, t)
                    wait(gp, v_res[1], 1, t, -1)
                    wait(gp, g_a0, 1, t, 1)
                    g.tensor_tensor(acc1[p][:, :], acc0[p][:, :], tok_in[t.off % 8][:, :],
                                    ALU.add).then_inc(g_a1, 1)

            token_steps(gp, token_step)


def kernel(x, ctx_1024, L0_xattn_Wq, L0_xattn_Wk, L0_xattn_Wv, L0_xattn_lambda_q1, L0_xattn_lambda_q2,
           L0_xattn_lambda_k1, L0_xattn_lambda_k2, L0_ffn_gate_w, L0_ffn_w_gate, L0_ffn_w_up, L0_ffn_w_down,
           L0_ffn_ws_gate, L0_ffn_ws_up, L0_ffn_ws_down):
    import numpy as np
    import concourse.bacc as bacc
    from concourse.bass_utils import run_bass_kernel_spmd

    def contract_rows(w):
        w = np.asarray(w)
        return w.reshape(w.shape[0] // P, P, w.shape[1]).transpose(1, 0, 2)

    def dims_first(w):
        w = np.asarray(w).T
        return w.reshape(w.shape[0], 2, SUB // 2, -1).transpose(0, 1, 3, 2).reshape(w.shape)

    wg, wu = np.asarray(L0_ffn_w_gate), np.asarray(L0_ffn_w_up)
    n_e, dim, hid = wg.shape
    gate_up = np.concatenate([wg, wu], axis=2).reshape(n_e, dim // P, P, 2 * hid).transpose(2, 0, 1, 3)
    down = np.asarray(L0_ffn_w_down).transpose(1, 0, 2)
    laid = {
        "x": x, "ctx": ctx_1024, "lq1": L0_xattn_lambda_q1, "lk1": L0_xattn_lambda_k1, "lq2": L0_xattn_lambda_q2,
        "lk2": L0_xattn_lambda_k2, "wqT": contract_rows(dims_first(L0_xattn_Wq)),
        "wkT": contract_rows(dims_first(L0_xattn_Wk)), "wvT": contract_rows(np.asarray(L0_xattn_Wv).T),
        "gate_wT": contract_rows(np.asarray(L0_ffn_gate_w).T), "w_gu": gate_up, "w_dn": down,
        "ws_gu": contract_rows(np.concatenate([np.asarray(L0_ffn_ws_gate), np.asarray(L0_ffn_ws_up)], axis=1)),
        "ws_dn": L0_ffn_ws_down,
    }
    nc = bacc.Bacc("TRN2", target_bir_lowering=False, num_devices=1)
    arrays, args = {}, {}
    for name, a in laid.items():
        a = np.ascontiguousarray(a)
        arrays["in_" + name] = a
        args[name] = nc.dram_tensor("in_" + name, a.shape, mybir.dt.from_np(a.dtype), kind="ExternalInput").ap()
    out = nc.dram_tensor("out", x.shape, F32, kind="ExternalOutput").ap()
    program(nc, out=out, **args)
    r = run_bass_kernel_spmd(nc, [arrays], core_ids=[0])
    return r.results[0]["out"]
```

```python
from contextlib import ExitStack

import concourse.bass as bass
from concourse import mybir

ALU = mybir.AluOpType
ACT = mybir.ActivationFunctionType
AX = mybir.AxisListType
F32 = mybir.dt.float32
BF16 = mybir.dt.bfloat16
F32R = mybir.dt.float32r
U32 = mybir.dt.uint32
I32 = mybir.dt.int32

P = 128
HEADS = 16
SUB = 2 * HEADS
PARTS = 3
ROWS = 48
KROWS = ROWS + 2
CHUNK = 4
NCH = 2 * SUB // CHUNK
WIDE_HEADS = 7
LAMBDA_INIT = 0.8
EPS = 1e-5
ROUTE_SCALE = 2.5
TOPK = 2

MAX_SLOTS = {4: [0, 1], 5: [2, 3], 6: [4], 7: [5], 8: [6], 9: [7], 10: [8], 11: [9], 12: [10, 11], 13: [12],
             14: [13, 14], 15: [15]}


class Step:

    def __init__(self, k, off, unroll=2):
        self.k, self.off, self.unroll = k, off, unroll

    def plus(self, n):
        return Step(self.k, self.off + n, self.unroll)

    def idx(self):
        return self.off if self.k is None else self.k * self.unroll + self.off

    def par(self):
        return self.off % 2

    def pair(self):
        return Step(self.k, self.off // 2, self.unroll // 2)

    def is_in(self, lo, hi):
        return self.k is not None or lo <= self.off < hi


def program(nc, x, ctxT, lq1, lk1, lq2, lk2, wqT, wkT, wvT, gate_wT, w_gu, w_dn, ws_gu, ws_dn, out):
    NB, _, D = x.shape
    NS = NB // 2
    T = NB * P
    NT = TOPK * T // P + gate_wT.shape[-1]
    E = gate_wT.shape[-1]
    CAP = T
    DK = D // P
    SHH = SUB // 2
    DH = D // HEADS
    HALF = DH // 2
    SW = 2 * P
    HID = w_dn.shape[0]
    VW = 2 * HEADS * (DH + 1)
    WIDE = WIDE_HEADS * (DH + 1)
    assert NS % 2 == 0 and NB >= 28 and E % 4 == 0 and NT % 8 == 0 and CAP < 32768 and DK == 2 and HALF * SHH == P and HID == P and NT <= 512

    x_g = x.rearrange("(g u) p d -> g p u d", u=2)
    x2_dram = nc.dram_tensor("x2_dram", (NB, P, D), F32, kind="Internal").ap()
    x2_g = x2_dram.rearrange("(g u) p d -> g p u d", u=2)
    stack_dram = nc.dram_tensor("stack_dram", (2, 2, 2, ROWS, SHH, SW), BF16, kind="Internal").ap()
    max_dram = nc.dram_tensor("max_dram", (2, 2, 2, 2, SHH, P), BF16, kind="Internal").ap()
    N_ROWS = E * CAP
    rows_dram = nc.dram_tensor("rows_dram", (N_ROWS, D), F32, kind="Internal").ap()
    tags_dram = nc.dram_tensor("tags_dram", (N_ROWS, 2), F32, kind="Internal").ap()
    routed_dram = nc.dram_tensor("routed_dram", (T * TOPK, D), F32, kind="Internal").ap()

    routed_g = routed_dram.rearrange("(g u p k) d -> g p u (k d)", u=2, p=P, k=TOPK)
    out_g = out.rearrange("(g u) p d -> g p u d", u=2)

    with ExitStack() as st:
        def sb(name, shape, dt=F32):
            return st.enter_context(nc.sbuf_tensor(name, shape, dt))

        def ps(name):
            return st.enter_context(nc.psum_tensor(name, [P, 512], F32))

        def sem(name):
            return st.enter_context(nc.semaphore(name))

        st_ps = [ps(f"st_ps{i}") for i in range(2)]
        mx_ps = [ps(f"mx_ps{i}") for i in range(2)]
        o_ps = [ps(f"o_ps{i}") for i in range(2)]
        ms_ps = [ps(f"ms_ps{i}") for i in range(2)]
        tp_ps, gu_ps, hp_ps, eo_ps = st_ps, mx_ps, o_ps, ms_ps

        with ExitStack() as first_st:
            def first_sb(name, shape):
                return first_st.enter_context(nc.sbuf_tensor(name, shape, F32))

            w_gu_sb = first_sb("w_gu_sb", [P, E, DK, 2 * HID])
            w_dn_sb = first_sb("w_dn_sb", [P, E, D])
            ws_gu_sb = first_sb("ws_gu_sb", [P, DK, 2 * HID])
            ws_dn_sb = first_sb("ws_dn_sb", [P, D])
            stacks = first_sb("stacks", [P, 4 * SHH * SW // 2])
            spare = first_sb("spare", [P, E * D + DK * 2 * HID + D])
            x_in = first_sb("x_in", [P, 2, D])
            c_in = first_sb("c_in", [P, DK, SW])
            x_res = [first_sb(f"x_res{i}", [P, 2, D]) for i in range(2)]
            xn = first_sb("xn", [P, 2, D])
            xnT = first_sb("xnT", [P, 2, DK, SW])
            cT = [first_sb(f"cT{i}", [P, 2, DK, SW]) for i in range(2)]
            w_in = first_sb("w_in", [P, 3, DK * D])
            w_hi = first_sb("w_hi", [P, 3, DK, D])
            w_lo = first_sb("w_lo", [P, 3, DK, D])
        w_gu_lo = sb("w_gu_lo", [P, E, DK, 2 * HID])
        w_dn_lo = sb("w_dn_lo", [P, E, D])
        ws_gu_lo = sb("ws_gu_lo", [P, DK, 2 * HID])
        ws_dn_lo = sb("ws_dn_lo", [P, D])
        w_gu_hi = sb("w_gu_hi", [P, E, DK, 2 * HID])
        w_dn_hi = sb("w_dn_hi", [P, E, D])
        ws_gu_hi = sb("ws_gu_hi", [P, DK, 2 * HID])
        ws_dn_hi = sb("ws_dn_hi", [P, D])
        got_pair = [sb(f"got_pair{i}", [P, 2, TOPK * D]) for i in range(4)]
        tok_pair = [sb(f"tok_pair{i}", [P, 2, D]) for i in range(4)]
        tok_in = [tok_pair[i // 2][:, i % 2, :] for i in range(8)]
        rows_T = [sb(f"rows_T{i}", [P, 2, DK * P]) for i in range(2)]
        gate = [sb(f"gate{i}", [P, HID]) for i in range(2)]
        hid = [sb(f"hid{i}", [P, HID]) for i in range(2)]
        hid_T = [sb(f"hid_T{i}", [P, 2, P]) for i in range(2)]
        res_pair = [sb(f"res_pair{i}", [P, 2, D]) for i in range(2)]
        res = [res_pair[i // 2][:, i % 2, :] for i in range(4)]
        h3 = [sb(f"h3_{i}", [P, D]) for i in range(2)]
        acc_pair = [sb(f"acc_pair{i}", [P, 2, D]) for i in range(2)]

        gw_sb = sb("gw_sb", [P, DK, E])
        lam_in = sb("lam_in", [P, 4, HALF])
        lam_p = sb("lam_p", [P, 2, HALF])
        lam_s = sb("lam_s", [P, 2])
        lam_e = sb("lam_e", [P, 2])
        coef = sb("coef", [P, SHH])
        ident = sb("ident", [P, P])
        identb = sb("identb", [P, P], BF16)
        upper = sb("upper", [P, P], BF16)
        onesb = sb("onesb", [P, P], BF16)
        iota_e = sb("iota_e", [P, E])
        neghalf = sb("neghalf", [P, 2])

        taken = [0]

        def carve(words, pattern, **sizes):
            taken[0] += words
            return spare[:, taken[0] - words:taken[0]].rearrange(pattern, **sizes)

        def carve_parts():
            taken[0] += PARTS * 256
            return spare.bitcast(BF16)[:, 2 * taken[0] - PARTS * 512:2 * taken[0]].rearrange("p (r n) -> p r n", r=PARTS)

        def stack(n):
            return stacks.bitcast(BF16)[:, n * SHH * SW:(n + 1) * SHH * SW].rearrange("p (j t) -> p j t", j=SHH)

        q_st, k_st = [stack(0), stack(1)], [stack(2), stack(3)]
        prob = [carve(512, "p n -> p n") for _ in range(4)]
        qp, kp = carve_parts(), carve_parts()
        q_rest, k_rest = carve(512, "p n -> p n"), carve(512, "p n -> p n")
        assert taken[0] <= E * D + DK * 2 * HID + D
        v_sb = [sb(f"v_sb{i}", [P, VW + WIDE]) for i in range(2)]
        mx = sb("mx", [P, 2, SUB])
        mxp = sb("mxp", [P, 2, 2 * SUB], BF16)
        mxT = [sb(f"mxT{i}", [2 * SUB, P], BF16) for i in range(2)]
        rl = sb("rl", [P, SHH])
        rlc = sb("rlc", [P, SHH])
        o_sc = [sb(f"o_sc{i}", [P, SHH, DH]) for i in range(2)]
        att = sb("att", [P, SHH // 2, DH])
        x2 = [sb(f"x2_{i}", [P, 2, D]) for i in range(2)]
        h2 = [sb(f"h2_{i}", [P, 2, D]) for i in range(2)]
        h2T = sb("h2T", [P, DK, SW])
        bs1 = sb("bs1", [P, 2, 6])
        mv1 = sb("mv1", [P, 2, 2])
        ve1 = sb("ve1", [P, 2])
        bs2 = sb("bs2", [P, 2, 6])
        mv2 = sb("mv2", [P, 2, 2])
        ve2 = sb("ve2", [P, 2])
        mv_all = sb("mv_all", [P, NS, 4])
        ez = sb("ez", [P, 2 * E])
        ez1 = sb("ez1", [P, 2 * E])
        score = sb("score", [P, 2, E])
        top = sb("top", [P, 2, 8])
        topi = sb("topi", [P, 2, 8], U32)
        topf = sb("topf", [P, 2, TOPK])
        hot = sb("hot", [P, 2, TOPK, E])
        hots = sb("hots", [P, 2, E], BF16)
        den = sb("den", [P, 2])
        den1 = sb("den1", [P, 2])
        rden = sb("rden", [P, 2])
        number = sb("number", [P, 2 * TOPK])
        tag = [sb(f"tag{i}", [P, 2 * TOPK, 2]) for i in range(2)]
        no_tag = sb("no_tag", [P, 2])
        base = sb("base", [P, 2, E])
        pb = sb("pb", [P, 2, E])
        hotp = sb("hotp", [P, 2, TOPK, E])
        posf = sb("posf", [P, 2 * TOPK])
        posi = [sb(f"posi{i}", [P, 2 * TOPK], U32) for i in range(2)]

        zeros = sb("zeros", [P, D])
        cap_e = sb("cap_e", [P, E])
        count = sb("count", [P, E])
        upto = sb("upto", [E, E])
        tiles_i = sb("tiles_i", [E, 1], I32)
        tiles_s = sb("tiles_s", [E, 1], I32)
        tiles_n = sb("tiles_n", [E, 1])
        last_t = sb("last_t", [E, 1])
        one_skip = sb("one_skip", [E, 2])
        iota_t = sb("iota_t", [E, NT])
        past = sb("past", [E, NT])
        expert_tab = sb("expert_tab", [1, NT], I32)
        full = sb("full", [1, E])
        room = sb("room", [1, E])
        least = sb("least", [1, 1])
        row_f = sb("row_f", [1, NT])
        row_d = sb("row_d", [1, NT])
        row_tab = sb("row_tab", [1, NT], I32)
        pad_f = sb("pad_f", [1, E])
        pad_tab = sb("pad_tab", [1, E], I32)
        row_tag = [sb(f"row_tag{i}", [P, 2]) for i in range(16)]
        mv3 = [sb(f"mv3_{i}", [P, 4]) for i in range(2)]

        d_w, d_x, d_c = sem("d_w"), sem("d_x"), sem("d_c")
        d_res = [sem(f"d_res{i}") for i in range(2)]
        d_qw, d_kw, d_stk = sem("d_qw"), sem("d_kw"), sem("d_stk")
        d_m = [sem(f"d_m{i}") for i in range(2)]
        d_mw = [sem(f"d_mw{i}") for i in range(2)]
        d_x2 = [sem(f"d_x2_{i}") for i in range(2)]
        d_scat = [sem(f"d_scat{i}") for i in range(2)]
        d_we, d_zero, d_pad = sem("d_we"), sem("d_zero"), sem("d_pad")
        d_row = [sem(f"d_row{i}") for i in range(8)]
        d_tag = [sem(f"d_tag{i}") for i in range(16)]
        d_eo = [sem(f"d_eo{i}") for i in range(4)]
        d_tok = [sem(f"d_tok{i}") for i in range(4)]
        d_got = [sem(f"d_got{i}") for i in range(4)]
        d_out = [sem(f"d_out{i}") for i in range(2)]
        v_tab, p_tab, v_row = sem("v_tab"), sem("p_tab"), sem("v_row")
        p_tp, a_tp = [sem("p_tp2"), sem("p_tp3")], [sem("a_tp2"), sem("a_tp3")]
        p_gu, a_gate = [sem("p_gu2"), sem("p_gu3")], [sem("a_gate2"), sem("a_gate3")]
        v_hid, p_hp = [sem("v_hid2"), sem("v_hid3")], [sem("p_hp2"), sem("p_hp3")]
        a_hT, p_eo = [sem("a_hT2"), sem("a_hT3")], [sem("p_eo2"), sem("p_eo3")]
        g_ones = sem("g_ones")
        a_w1, v_w1, v_xl, v_cl = sem("a_w1"), sem("v_w1"), sem("v_xl"), sem("v_cl")
        v_tl, v_hl = [sem("v_tl2"), sem("v_tl3")], [sem("v_hl2"), sem("v_hl3")]
        a_wh, v_wl = sem("a_wh"), sem("v_wl")
        v_res = [sem("v_res2"), sem("v_res3")]
        v_s3, v_h3, g_a0, g_a1, v_all = sem("v_s3"), sem("v_h3"), sem("g_a0"), sem("g_a1"), sem("v_all")
        g_num, g_tag = sem("g_num"), sem("g_tag")
        p_xT, p_v, p_q, p_k = sem("p_xT"), sem("p_v"), sem("p_q"), sem("p_k")
        p_hT, p_lg, p_pf, p_mT = sem("p_hT"), sem("p_lg"), sem("p_pf"), sem("p_mT")
        p_st, p_pv, p_mx = sem("p_st"), sem("p_pv"), sem("p_mx")
        a_x, a_c, a_v, a_q, a_k = sem("a_x"), sem("a_c"), sem("a_v"), sem("a_q"), sem("a_k")
        a_h, a_e, a_mT, a_exp, a_lam = sem("a_h"), sem("a_e"), sem("a_mT"), sem("a_exp"), sem("a_lam")
        v_q, v_k, v_red, v_mx, v_s1, v_s2 = (sem("v_q"), sem("v_k"), sem("v_red"), sem("v_mx"), sem("v_s1"),
                                             sem("v_s2"))
        v_mxa, v_ps = sem("v_mxa"), sem("v_ps")
        v_rl, v_rlc, v_cb, v_b1, v_b2, v_lam = (sem("v_rl"), sem("v_rlc"), sem("v_cb"), sem("v_b1"), sem("v_b2"),
                                                sem("v_lam"))
        v_rt, v_hot, v_pf, v_pos, v_w = sem("v_rt"), sem("v_hot"), sem("v_pf"), sem("v_pos"), sem("v_w")
        g_set, v_xn, g_qb, g_qs, g_kb, g_ks = (sem("g_set"), sem("v_xn"), sem("g_qb"), sem("g_qs"),
                                               sem("g_kb"), sem("g_ks"))
        g_att, g_x2, v_h2, g_r1, g_r2 = sem("g_att"), sem("g_x2"), sem("v_h2"), sem("g_r1"), sem("g_r2")
        passed = sem("passed")
        SETUP = 17
        N_W = 8
        PW = 2 * 3 * 16
        STK = 4 * 16
        MR = 2 * 16
        SCAT = 2 * 2 * TOPK * 16
        RT = 12

        first, lo, hi, end = -3, 4, NS - 4, NS + 2

        def wait(eng, sem, inc, s, j=0, last=None, plain=False):
            if s.k is None:
                v = inc * s.off + j
                if last is not None:
                    v = min(v, inc * last)
                if v > 0:
                    eng.wait_ge(sem, v)
            else:
                eng.wait_ge(sem, s.k * (s.unroll * inc) + (inc * s.off + j))
                if plain or eng.engine in (mybir.EngineType.SP, mybir.EngineType.Pool):
                    eng.sem_inc(passed, 1)

        def wait_par(eng, sems, inc, s):
            ring = len(sems)
            v = inc * (s.off // ring + 1)
            if s.k is None:
                if v > 0:
                    eng.wait_ge(sems[s.off % ring], v)
            else:
                eng.wait_ge(sems[s.off % ring], s.k * (inc * s.unroll // ring) + v)
                if eng.engine in (mybir.EngineType.SP, mybir.EngineType.Pool):
                    eng.sem_inc(passed, 1)

        def pipeline(eng, body, first, lo, hi, end, unroll):
            for it in range(first, lo):
                body(Step(None, it))
            with eng.Fori(0, (hi - lo) // unroll) as k:
                for off in range(unroll):
                    body(Step(k, lo + off, unroll))
            for it in range(hi, end):
                body(Step(None, it))

        def steps(eng, body):
            pipeline(eng, body, first, lo, hi, end, 2)

        NT_HI = 16 + (NT - 23) // 16 * 16
        TT_HI = (NB - 7) // 8 * 8

        def expert_steps(eng, body):
            pipeline(eng, body, -6, 16, NT_HI, NT + 2, 16)

        def token_steps(eng, body):
            pipeline(eng, body, -6, 8, TT_HI, NB + 2, 8)

        def load(eng, entry, most):
            return nc.values_load(entry, engines=(eng.engine,), min_val=0, max_val=most,
                                  skip_runtime_bounds_check_because="VectorE clamps the tables' entries")

        def pad_rows(eng, i):
            eng.wait_ge(v_row, 1)
            for e in range(i, E, 2):
                r = load(eng, pad_tab[0:1, e:e + 1], E * CAP - P)
                eng.dma_start(rows_dram[bass.ds(r, P), :], zeros[:, :]).then_inc(d_pad, 16)
                eng.dma_start(tags_dram[bass.ds(r, P), :], no_tag[:, :]).then_inc(d_pad, 16)

        def rnd(ap):
            return ap.bitcast(F32R)

        def by_expert(w, e):
            return w[:, e:e + E // 4].rearrange("p e k n -> p (e k n)" if len(w.shape) == 4 else "p e n -> p (e n)")

        pieces = [tuple(by_expert(w, e) for w in ws) for e in range(0, E, E // 4)
                  for ws in ((w_gu_sb, w_gu_lo, w_gu_hi), (w_dn_sb, w_dn_lo, w_dn_hi))]
        pieces += [tuple(w[:, :, :].rearrange("p k n -> p (k n)") for w in (ws_gu_sb, ws_gu_lo, ws_gu_hi)),
                   tuple(w[:, :] for w in (ws_dn_sb, ws_dn_lo, ws_dn_hi))]

        block = st.enter_context(nc.Block())

        @block.sync
        def _(sp):
            sp.dma_start(x_in[:, :, :], x_g[0]).then_inc(d_x, 16)
            for n, src in enumerate((wqT, wkT, wvT)):
                sp.dma_start(w_in[:, n, :], src.rearrange("p k n -> p (k n)")).then_inc(d_w, 16)
            sp.dma_start(gw_sb[:, :, :], gate_wT).then_inc(d_w, 16)
            for n, src in enumerate((lq1, lq2, lk1, lk2)):
                sp.dma_start(lam_in[:, n, :], src.partition_broadcast(P)).then_inc(d_w, 16)

            def step(it):
                a, b, d, ln = it.plus(2), it.plus(1), it.plus(-1), it.plus(3)
                p = it.par()
                if it.k is None and it.off == 0:
                    sp.wait_ge(g_set, SETUP)
                    sp.dma_start(rows_dram.rearrange("(e n) d -> n e d", e=E)[CAP - P:CAP],
                                 zeros[:, :].unsqueeze(1).to_broadcast([P, E, D])).then_inc(d_zero, 16)
                    sp.dma_start(tags_dram.rearrange("(e n) d -> n e d", e=E)[CAP - P:CAP],
                                 no_tag[:, :].unsqueeze(1).to_broadcast([P, E, 2])).then_inc(d_zero, 16)
                if it.is_in(0, NS):
                    wait(sp, a_mT, 2, it, 2)
                    max_rows(it, 1)
                if d.is_in(0, NS):
                    wait(sp, g_x2, 4, d, 4)
                    sp.dma_start(x2_g[bass.ds(d.idx(), 1)].rearrange("g p u d -> (g p) u d"),
                                 x2[1 - p][:, :, :]).then_inc(d_x2[1 - p], 16)
                if b.is_in(0, NS):
                    wait(sp, g_x2, 4, it, 0)
                    sp.dma_start(x_res[1 - p][:, :, :],
                                 x_g[bass.ds(b.idx(), 1)].rearrange("g p u d -> (g p) u d")).then_inc(d_res[1 - p], 16)
                if ln.is_in(0, NS):
                    wait(sp, v_cl, 1, ln)
                    sp.dma_start(c_in[:, :, :],
                                 ctxT[bass.ds(ln.idx(), 1)].rearrange("g p k t -> (g p) k t")).then_inc(d_c, 16)
                if a.is_in(0, NS):
                    for n, (done, buf, landed) in enumerate(((g_qs, qp, d_qw), (g_ks, kp, d_kw))):
                        wait(sp, done, 1, a, 1)
                        if n == 0:
                            wait(sp, d_stk, STK, a, -STK)
                        for h in range(2):
                            rows = stack_dram[p, n, h].rearrange("(r d) j t -> (d j) r t", d=HALF)
                            part = buf[:, :, h * SW:(h + 1) * SW]
                            for r, m in ((0, 3), (3, 2), (5, 1)):
                                if n == 0:
                                    src = part[:, 0:m, :]
                                else:
                                    src = part[:, 3 - m:4 - m, :].to_broadcast([P, m, SW])
                                sp.dma_start(rows[:, r:r + m, :], src).then_inc(landed, 16)
                nxt = it.plus(4)
                if nxt.is_in(1, NS):
                    wait(sp, v_xn, 2, nxt)
                    sp.dma_start(x_in[:, :, :],
                                 x_g[bass.ds(nxt.idx(), 1)].rearrange("g p u d -> (g p) u d")).then_inc(d_x, 16)
                if b.is_in(0, NS):
                    wait(sp, a_mT, 2, b, 1)
                    max_rows(b, 0)
                if a.is_in(0, NS):
                    wait(sp, p_st, NCH, it, NCH)
                    wait(sp, d_qw, PW, a, PW)
                    wait(sp, d_kw, PW, a, PW)
                    if a.k is None and a.off < 2:
                        sp.wait_ge(g_ones, a.off + 1)
                    for h in range(2):
                        rows = slice(64 * h, 64 * h + ROWS)
                        sp.dma_start(q_st[p][rows, :, :], stack_dram[p, 0, h]).then_inc(d_stk, 16)
                        sp.dma_start(k_st[p][rows, :, :], stack_dram[p, 1, h]).then_inc(d_stk, 16)
                if it.k is None and 0 <= it.off < lo:
                    e = slice(it.off * E // lo, (it.off + 1) * E // lo)
                    sp.dma_start(w_gu_sb[:, e], w_gu[:, e]).then_inc(d_we, 16)
                    sp.dma_start(w_dn_sb[:, e, :], w_dn[:, e]).then_inc(d_we, 16)
                    if it.off == 0:
                        sp.dma_start(ws_gu_sb[:, :, :], ws_gu).then_inc(d_we, 16)
                        sp.dma_start(ws_dn_sb[:, :], ws_dn).then_inc(d_we, 16)

            def max_rows(s, u):
                p = s.par()
                wait(sp, d_m[u], MR, s, -MR)
                sp.dma_start(max_dram[p, u].rearrange("r h j t -> (r h j) t"), mxT[u][:, :]).then_inc(d_mw[u], 16)
                wait(sp, d_mw[u], 16, s, 16)
                for h in range(2):
                    row = 64 * h + ROWS
                    sp.dma_start(q_st[p][row:row + 2, :, u * P:(u + 1) * P], max_dram[p, u, :, h]
                                 ).then_inc(d_m[u], 16)

            steps(sp, step)
            for i in range(2):
                sp.wait_ge(d_x2[i], 16 * (NS // 2))

            pad_rows(sp, 0)
            sp.wait_ge(d_pad, 32 * E)
            for i in range(2):
                sp.wait_ge(d_scat[i], SCAT * (NS // 2))
            sp.wait_ge(v_row, 3)

            def expert_step(j):
                t = j.plus(6)
                if t.is_in(0, NT):
                    if t.off % 4 == 0:
                        wait(sp, p_tp[0], 1, t, -4)
                        wait(sp, v_res[0], 1, t, -8)
                    r = load(sp, row_tab[0:1, bass.ds(t.idx(), 1)], N_ROWS - P)
                    sp.dma_start(tok_in[t.off % 8][:, :], rows_dram[bass.ds(r, P), :]).then_inc(d_row[t.off % 8], 16)
                    sp.dma_start(row_tag[t.off % 16][:, :], tags_dram[bass.ds(r, P), :]
                                 ).then_inc(d_tag[t.off % 16], 16)

            expert_steps(sp, expert_step)

            def token_step(j):
                if j.off % 2:
                    return
                t = j.plus(6)
                if t.k is None and t.off < 8:
                    sp.wait_ge(p_tp[0], NT - 6 + t.off)
                if t.is_in(0, NB):
                    wait(sp, g_a1, 1, t, -6)
                    wait(sp, v_h3, 1, t, -6)
                    sp.dma_start(tok_pair[t.off // 2 % 4][:, :, :],
                                 x2_g[bass.ds(t.pair().idx(), 1)].rearrange("g p u d -> (g p) u d")
                                 ).then_inc(d_tok[t.off // 2 % 4], 16)
                if j.k is None and j.off == -4:
                    for i in range(4):
                        sp.wait_ge(d_eo[i], 16 * (NT // 4))
                t = j.plus(4)
                if t.is_in(0, NB):
                    sp.dma_start(got_pair[t.off // 2 % 4][:, :, :],
                                 routed_g[bass.ds(t.pair().idx(), 1)].rearrange("g p u n -> (g p) u n")
                                 ).then_inc(d_got[t.off // 2 % 4], 16)
                t = j.plus(-2)
                if t.is_in(0, NB):
                    wait(sp, v_res[1], 1, t, 2)
                    sp.dma_start(out_g[bass.ds(t.pair().idx(), 1)].rearrange("g p u d -> (g p) u d"),
                                 res_pair[t.off // 2 % 2][:, :, :]).then_inc(d_out[t.off // 2 % 2], 16)

            token_steps(sp, token_step)
            for i in range(2):
                sp.wait_ge(d_out[i], 16 * (NB // 4))

        @block.tensor
        def _(pe):
            pe.wait_ge(d_w, 16 * N_W)
            pe.wait_ge(g_set, SETUP)
            pe.wait_ge(v_w1, 1)
            M0, M1 = ms_ps

            def product(out_ps, still, moving, start, stop):
                pe.matmul(out_ps, rnd(still[0]), rnd(moving[0]), start=start, stop=False)
                pe.matmul(out_ps, rnd(still[0]), rnd(moving[1]), start=False, stop=False)
                return pe.matmul(out_ps, rnd(still[1]), rnd(moving[0]), start=False, stop=stop)

            def scores(s, k):
                u, c = divmod(k, NCH // 2)
                h, p = c // 4, s.par()
                if c == 0:
                    wait(pe, d_m[u], MR, s, MR)
                for i in range(CHUNK):
                    j = CHUNK * (c % 4) + i
                    mm = pe.matmul(st_ps[k % 2][:, i * P:(i + 1) * P],
                                   k_st[p][64 * h:64 * h + KROWS, j, u * P:(u + 1) * P],
                                   q_st[p][64 * h:64 * h + KROWS, j, u * P:(u + 1) * P], start=True, stop=True)
                mm.then_inc(p_st, 1)

            def attend(s, k):
                u, c = divmod(k, NCH // 2)
                if k == 0:
                    wait(pe, a_v, 1, s, 1)
                if c % 4 == 0:
                    wait(pe, v_cb, 4, s, k // 4 - 1)
                for i in range(CHUNK):
                    sub = CHUNK * c + i
                    at = (sub % SHH) * (DH + 1)
                    own = (u * HEADS + sub // 2) * (DH + 1)
                    mm = pe.matmul(o_ps[(k // 4) % 2][:, at:at + WIDE], prob[k % 4][:, i * P:(i + 1) * P],
                                   v_sb[s.par()][:, own:own + WIDE], start=True, stop=True)
                mm.then_inc(p_pv, 1)

            def maxima(s, k):
                u, c = divmod(k, NCH // 2)
                h, p = c // 4, s.par()
                if k == 0:
                    wait(pe, d_stk, STK, s, STK)
                wait(pe, v_red, NCH, s, k - 1)
                for i in range(CHUNK):
                    j = CHUNK * (c % 4) + i
                    mm = pe.matmul(mx_ps[k % 2][:, i * P:(i + 1) * P],
                                   q_st[p][64 * h:64 * h + ROWS, j, u * P:(u + 1) * P],
                                   k_st[p][64 * h:64 * h + ROWS, j, u * P:(u + 1) * P], start=True, stop=True)
                mm.then_inc(p_mx, 1)

            def turn_max(s, u, bank):
                wait(pe, v_mx, 2, s, u + 1, plain=True)
                pe.transpose(bank.bitcast(BF16)[0:2 * SUB, 0:P], mxp[:, u, :], identb[:, :]).then_inc(p_mT, 1)

            def turn(src, bank, done):
                for u in range(2):
                    for h in range(DK):
                        mm = pe.transpose(bank[:, h * SW + u * P:h * SW + (u + 1) * P], src[:, u, h * P:(h + 1) * P],
                                          ident[:, :])
                mm.then_inc(done, 1)

            def project(n, src, bank, done):
                for m in range(2):
                    for h in range(DK):
                        mm = product(bank[:, m * SW:(m + 1) * SW],
                                     [w[:, n, h, m * P:(m + 1) * P] for w in (w_hi, w_lo)],
                                     [src[:, i, h, :] for i in range(2)], h == 0, h == DK - 1)
                mm.then_inc(done, 1)

            def side(it, k):
                a, b, d, r = it.plus(2), it.plus(1), it.plus(-1), it.plus(-2)
                do_a, do_b, do_d = a.is_in(0, NS), b.is_in(0, NS), d.is_in(0, NS)
                if k == 1 and it.is_in(0, NS):
                    turn_max(it, 1, M0)
                if k == 0 and do_a:
                    wait(pe, v_pf, 1, r)
                    wait(pe, a_mT, 2, it, 1, last=NS)
                    wait(pe, v_xn, 2, a, 2)
                    turn(xn, M1, p_xT)
                if k == 3 and do_b:
                    if do_a:
                        wait(pe, v_xl, 1, a, 1)
                    else:
                        wait(pe, a_mT, 2, it, 1, last=NS)
                    wait(pe, v_cl, 1, b, 1)
                    for u in range(2):
                        for h in range(DK):
                            mm = product(M1[:, u * SW:(u + 1) * SW],
                                         [cT[b.par()][:, i, h, u * P:(u + 1) * P] for i in range(2)],
                                         [w[:, 2, h, :] for w in (w_hi, w_lo)], h == 0, h == DK - 1)
                    mm.then_inc(p_v, 1)
                if k == 4 and do_a:
                    wait(pe, v_xl, 1, a, 1)
                    wait(pe, a_mT, 2, it, 2, last=NS)
                    project(0, xnT, M0, p_q)
                if k == 5 and do_a:
                    wait(pe, a_v, 1, b, 1)
                    wait(pe, v_cl, 1, a, 1)
                    project(1, cT[a.par()], M1, p_k)
                if k == 6 and do_d:
                    if do_a:
                        wait(pe, v_q, 1, a, 1)
                    else:
                        wait(pe, a_mT, 2, it, 2, last=NS)
                    wait(pe, v_h2, 2, d, 2)
                    turn(h2[d.par()], M0, p_hT)
                if k == 7 and r.is_in(0, NS):
                    if not do_d:
                        wait(pe, a_e, 1, d)
                    if do_a:
                        wait(pe, v_k, 1, a, 1)
                    wait(pe, v_hot, 1, r, 1)
                    pe.matmul(M1[:, 2 * E:4 * E], upper[:, :], hots[:, :, :], start=True, stop=True)
                    pe.matmul(M1[:, 4 * E:6 * E], onesb[:, :], hots[:, :, :], start=True, stop=True).then_inc(p_pf, 1)
                if k == 7 and do_d:
                    if do_a:
                        wait(pe, v_k, 1, a, 1)
                    else:
                        wait(pe, a_v, 1, b, 1, last=NS)
                        wait(pe, a_mT, 2, it, 1, last=NS)
                    wait(pe, a_h, 1, d, 1)
                    for u in range(2):
                        for h in range(DK):
                            mm = pe.matmul(M1[:, u * E:(u + 1) * E], h2T[:, h, u * P:(u + 1) * P], gw_sb[:, h, :],
                                           start=(h == 0), stop=(h == DK - 1))
                    mm.then_inc(p_lg, 1)
                if k == 11 and do_b:
                    wait(pe, v_pf, 1, r, 1)
                    wait(pe, a_e, 1, d, 1, last=NS)
                    if d.k is None and d.off < 0 and do_a:
                        wait(pe, v_k, 1, a, 1)
                    turn_max(b, 0, M1)
                if do_b:
                    for n in MAX_SLOTS.get(k, ()):
                        maxima(b, n)

            def step(it):
                d = it.plus(-1)
                for k in range(NCH):
                    cur, prev = it.is_in(0, NS), k < 2 and d.is_in(0, NS)
                    if cur or prev or k >= 2:
                        if it.is_in(0, NS + (1 if k < 2 else 0)):
                            wait(pe, a_exp, NCH, it, k - 1)
                    if cur:
                        scores(it, k)
                    if prev:
                        attend(d, NCH + k - 2)
                    elif cur and k >= 2:
                        attend(it, k - 2)
                    side(it, k)

            steps(pe, step)

            pe.wait_ge(v_tab, 1)
            pe.wait_ge(a_e, NS)
            pe.wait_ge(v_pf, NS)
            pe.transpose(M0[0:E, 0:P], count[:, :], ident[:, :]).then_inc(p_tab, 1)
            pe.wait_ge(v_tab, 10)
            pe.matmul(M1[0:E, 0:1], upto[:, :], tiles_n[:, :], start=True, stop=True).then_inc(p_tab, 1)
            pe.wait_ge(v_tab, 13)
            pe.matmul(M0[0:1, 0:NT], one_skip[:, 0:1], past[:, :], start=True, stop=True)
            pe.matmul(M1[0:1, 0:NT], one_skip[:, 1:2], past[:, :], start=True, stop=True).then_inc(p_tab, 1)

            pe.wait_ge(a_exp, NCH * NS)
            pe.wait_ge(v_red, NCH * NS)
            pe.wait_ge(v_cb, 4 * NS)
            pe.wait_ge(v_row, 3)
            pe.wait_ge(v_wl, len(pieces))

            def ffn(ph, n, j, turned, free_in, w_up, w_down):
                up = w_up(j.plus(1)) if j.plus(1).is_in(0, n) else None
                down = w_down(j.plus(-1)) if j.plus(-1).is_in(0, n) else None
                t = j.plus(2)
                if t.is_in(0, n):
                    turned(t)
                    for h in range(DK):
                        mm = pe.transpose(tp_ps[t.off % 2][:, h * P:(h + 1) * P],
                                          free_in(t)[:, h * P:(h + 1) * P], ident[:, :])
                    mm.then_inc(p_tp[ph], 1)
                t = j.plus(1)
                if t.is_in(0, n):
                    wait(pe, v_tl[ph], 1, t, 1)
                    for h in range(DK):
                        mm = product(gu_ps[t.off % 2][:, 0:2 * HID],
                                     [rows_T[t.off % 2][:, i, h * P:(h + 1) * P] for i in range(2)],
                                     up(h), h == 0, h == DK - 1)
                    mm.then_inc(p_gu[ph], 1)
                t = j
                if t.is_in(0, n):
                    wait(pe, v_hid[ph], 1, t, 1)
                    pe.transpose(hp_ps[t.off % 2][:, 0:P], hid[t.off % 2][:, :], ident[:, :]).then_inc(p_hp[ph], 1)
                t = j.plus(-1)
                if t.is_in(0, n):
                    wait(pe, v_hl[ph], 1, t, 1)
                    wait(pe, v_res[ph], 1, t, -1)
                    if ph == 1 and t.k is None and t.off < 2:
                        pe.wait_ge(v_res[0], NT - 1 + t.off)
                    product(eo_ps[t.off % 2][:, 0:D], [hid_T[t.off % 2][:, i, :] for i in range(2)], down, True,
                            True).then_inc(p_eo[ph], 1)

            held = {}

            def expert_of(t):
                if (t.k is None, t.off) not in held:
                    held[t.k is None, t.off] = load(pe, expert_tab[0:1, bass.ds(t.idx(), 1)], E - 1)
                return held[t.k is None, t.off]

            def routed_up(t):
                e = expert_of(t)
                return lambda h: [w[:, bass.ds(e, 1), h, :].rearrange("p e n -> p (e n)") for w in (w_gu_hi, w_gu_lo)]

            def routed_down(t):
                e = expert_of(t)
                return [w[:, bass.ds(e, 1), :].rearrange("p e n -> p (e n)") for w in (w_dn_hi, w_dn_lo)]

            expert_steps(pe, lambda j: ffn(0, NT, j, lambda t: wait_par(pe, d_row, 16, t),
                                           lambda t: tok_in[t.off % 8], routed_up, routed_down))
            token_steps(pe, lambda j: ffn(1, NB, j, lambda t: wait(pe, v_h3, 1, t, 1), lambda t: h3[t.off % 2],
                                          lambda t: lambda h: (ws_gu_hi[:, h, :], ws_gu_lo[:, h, :]),
                                          lambda t: (ws_dn_hi[:, :], ws_dn_lo[:, :])))

        @block.scalar
        def _(act):
            M0, M1 = ms_ps
            act.wait_ge(d_w, 16 * N_W)
            nc.scalar.activation(rnd(w_hi[:, :, :, :].rearrange("p w k n -> p (w k n)")),
                                 w_in[:, :, :].rearrange("p w n -> p (w n)"), ACT.Copy).then_inc(a_w1, 1)
            act.wait_ge(v_lam, 2)
            nc.scalar.activation(lam_e[:, :], lam_s[:, :], ACT.Exp).then_inc(a_lam, 1)

            def copy_max(s, u, bank):
                wait(act, p_mT, 2, s, u + 1)
                wait(act, d_mw[u], 16, s)
                nc.scalar.activation(mxT[u][:, :], bank.bitcast(BF16)[0:2 * SUB, 0:P], ACT.Copy).then_inc(a_mT, 1)

            def step(it):
                a, b, d = it.plus(2), it.plus(1), it.plus(-1)
                do_a, do_b, do_c, do_d = a.is_in(0, NS), b.is_in(0, NS), it.is_in(0, NS), d.is_in(0, NS)
                for k in range(NCH):
                    if do_c:
                        wait(act, p_st, NCH, it, k + 1)
                        wait(act, p_pv, NCH, it, k - 3)
                        nc.scalar.activation(prob[k % 4][:, :], st_ps[k % 2][:, :], ACT.Exp,
                                             scale=float(HALF) ** -0.5).then_inc(a_exp, 1)
                    if k == 1 and do_c:
                        copy_max(it, 1, M0)
                    if k == 0 and do_a:
                        wait(act, p_xT, 1, a, 1)
                        wait(act, p_q, 1, a)
                        nc.scalar.activation(rnd(xnT[:, 0, :, :]), M1[:, :], ACT.Copy).then_inc(a_x, 1)
                    if k == 2 and do_a:
                        wait(act, d_c, 16, a, 16)
                        wait(act, p_v, 1, it, 1)
                        wait(act, p_k, 1, it, 1)
                        nc.scalar.activation(rnd(cT[a.par()][:, 0, :, :]), c_in[:, :, :], ACT.Copy).then_inc(a_c, 1)
                    if k == 3 and do_b:
                        wait(act, p_v, 1, b, 1)
                        wait(act, p_pv, NCH, it)
                        nc.scalar.activation(v_sb[b.par()][:, 0:VW].rearrange("p (u h d) -> p u h d", u=2,
                                                                              h=HEADS)[:, :, :, 0:DH],
                                             M1[:, :].rearrange("p (u h d) -> p u h d", u=2, h=HEADS),
                                             ACT.Copy).then_inc(a_v, 1)
                    if k == 4 and do_a:
                        wait(act, p_q, 1, a, 1)
                        wait(act, d_qw, PW, a)
                        nc.scalar.activation(qp[:, 0, :], M0[:, :], ACT.Copy).then_inc(a_q, 1)
                    if k == 5 and do_a:
                        wait(act, p_k, 1, a, 1)
                        wait(act, d_kw, PW, a)
                        nc.scalar.activation(kp[:, 0, :], M1[:, :], ACT.Copy).then_inc(a_k, 1)
                    if k == 6 and do_d:
                        wait(act, p_hT, 1, d, 1)
                        wait(act, p_lg, 1, d)
                        nc.scalar.activation(h2T[:, :, :], M0[:, :], ACT.Copy).then_inc(a_h, 1)
                    if k == 7 and do_d:
                        wait(act, p_lg, 1, d, 1)
                        wait(act, v_rt, RT, d)
                        nc.scalar.activation(ez[:, :], M1[:, 0:2 * E], ACT.Exp, scale=-1.0).then_inc(a_e, 1)
                    if k == 11 and do_b:
                        copy_max(b, 0, M1)

            steps(act, step)

            act.wait_ge(d_we, 16 * (2 * lo + 2))
            act.wait_ge(p_mx, NCH * NS)
            act.wait_ge(p_st, NCH * NS)
            act.wait_ge(d_stk, STK * NS)
            for i in range(2):
                act.wait_ge(d_m[i], MR * NS)
            act.wait_ge(p_pv, NCH * NS)
            act.wait_ge(g_qs, NS)
            act.wait_ge(g_ks, NS)
            act.wait_ge(d_qw, PW * NS)
            act.wait_ge(d_kw, PW * NS)
            for weights, _, high in pieces:
                nc.scalar.activation(rnd(high), weights, ACT.Copy).then_inc(a_wh, 1)
            pad_rows(act, 1)

            def ffn(ph, n, j):
                t = j.plus(2)
                if t.is_in(0, n):
                    wait(act, p_tp[ph], 1, t, 1)
                    nc.scalar.activation(rnd(rows_T[t.off % 2][:, 0, :]), tp_ps[t.off % 2][:, 0:D],
                                         ACT.Copy).then_inc(a_tp[ph], 1)
                t = j.plus(1)
                if t.is_in(0, n):
                    wait(act, p_gu[ph], 1, t, 1)
                    nc.scalar.activation(gate[t.off % 2][:, :], gu_ps[t.off % 2][:, 0:HID],
                                         ACT.Silu).then_inc(a_gate[ph], 1)
                t = j
                if t.is_in(0, n):
                    wait(act, p_hp[ph], 1, t, 1)
                    nc.scalar.activation(rnd(hid_T[t.off % 2][:, 0, :]), hp_ps[t.off % 2][:, 0:P],
                                         ACT.Copy).then_inc(a_hT[ph], 1)

            expert_steps(act, lambda j: ffn(0, NT, j))
            token_steps(act, lambda j: ffn(1, NB, j))

        @block.vector
        def _(dve):
            v = nc.vector
            M0, M1 = ms_ps
            for i in range(2):
                v.memset(v_sb[i][:, :], 1.0)
            dve.wait_ge(d_w, 16 * N_W)
            v.tensor_tensor(lam_p[:, :, :], lam_in[:, 0:2, :], lam_in[:, 2:4, :], ALU.mult).then_inc(v_lam, 1)
            dve.wait_ge(v_lam, 1)
            v.tensor_reduce(lam_s[:, :], lam_p[:, :, :], AX.X, ALU.add).then_inc(v_lam, 1)
            dve.wait_ge(a_lam, 1)
            dve.wait_ge(g_set, SETUP)
            cf = coef[:, :].rearrange("p (h two) -> p h two", two=2)
            v.tensor_scalar(lam_p[:, 0, 0:1], lam_e[:, 1:2], lam_e[:, 0:1], -LAMBDA_INIT, ALU.subtract,
                            ALU.add).then_inc(v_lam, 1)
            dve.wait_ge(v_lam, 3)
            v.tensor_copy(cf[:, :, 1], lam_p[:, 0, 0:1].to_broadcast([P, SHH // 2])).then_inc(v_lam, 1)
            dve.wait_ge(v_lam, 4)

            dve.wait_ge(a_w1, 1)
            v.tensor_tensor(rnd(w_lo[:, :, :, :].rearrange("p w k n -> p (w k n)")),
                            w_in[:, :, :].rearrange("p w n -> p (w n)"),
                            w_hi[:, :, :, :].rearrange("p w k n -> p (w k n)"), ALU.subtract).then_inc(v_w1, 1)

            def turned_low(s, whole, a_done, parts, v_done):
                wait(dve, a_done, 1, s, 1)
                v.tensor_tensor(rnd(parts[:, 1, :, :].rearrange("p h t -> p (h t)")), whole,
                                parts[:, 0, :, :].rearrange("p h t -> p (h t)"), ALU.subtract).then_inc(v_done, 1)

            def rest(s, bank, a_done, part, tmp, g_done, v_done):
                wait(dve, a_done, 1, s, 1)
                wait(dve, g_done, 1, s)
                v.tensor_tensor(tmp[:, :], bank[:, :], part[:, 0, :], ALU.subtract).then_inc(v_done, 1)

            def reduce_max(s, k):
                u, c = divmod(k, NCH // 2)
                wait(dve, p_mx, NCH, s, k + 1)
                if c == 0:
                    wait(dve, v_mxa, 2, s, u - 1)
                v.tensor_reduce(mx[:, u, c * CHUNK:(c + 1) * CHUNK],
                                mx_ps[k % 2][:, :].rearrange("p (c n) -> p c n", c=CHUNK), AX.X,
                                ALU.max).then_inc(v_red, 1)
                if c == NCH // 2 - 1:
                    wait(dve, v_red, NCH, s, k + 1)
                    wait(dve, p_mT, 2, s, u - 1)
                    v.tensor_copy(mxp[:, u, 0:SUB], mx[:, u, :]).then_inc(v_mxa, 1)
                    wait(dve, v_mxa, 2, s, u + 1)
                    v.tensor_tensor(mxp[:, u, SUB:2 * SUB], mx[:, u, :], mxp[:, u, 0:SUB],
                                    ALU.subtract).then_inc(v_mx, 1)

            def combine(s, h):
                o = o_ps[h % 2][:, 0:SHH * (DH + 1)].rearrange("p (s d) -> p s d", s=SHH)
                wait(dve, p_pv, NCH, s, 4 * (h + 1))
                wait(dve, v_cb, 4, s, h)
                v.reciprocal(rl[:, :], o[:, :, DH]).then_inc(v_rl, 1)
                wait(dve, v_rl, 4, s, h + 1)
                v.tensor_tensor(rlc[:, :], rl[:, :], coef[:, :], ALU.mult).then_inc(v_rlc, 1)
                wait(dve, v_rlc, 4, s, h + 1)
                wait(dve, g_att, 4, s, h - 1)
                v.tensor_tensor(o_sc[h % 2][:, :, :], o[:, :, 0:DH],
                                rlc[:, :].unsqueeze(2).to_broadcast([P, SHH, DH]), ALU.mult).then_inc(v_cb, 1)

            def stats(s, src, st_b, mv, ve, v_b, v_s, v_done):
                wait(dve, v_done, 2, s)
                for u in range(2):
                    v.bn_stats(st_b[:, u, :], src[:, u, :]).then_inc(v_b, 1)
                for u in range(2):
                    wait(dve, v_b, 2, s, u + 1, plain=True)
                    v.bn_aggr(mv[:, u, :], st_b[:, u, :]).then_inc(v_s, 1)
                wait(dve, v_s, 3, s, 2)
                v.tensor_scalar(ve[:, :], mv[:, :, 1], EPS, None, ALU.add).then_inc(v_s, 1)

            def norm(s, src, mv, dst, g_r, v_done):
                wait(dve, g_r, 1, s, 1)
                for u in range(2):
                    v.tensor_scalar(dst[:, u, :], src[:, u, :], mv[:, u, 0:1], mv[:, u, 1:2], ALU.subtract,
                                    ALU.mult).then_inc(v_done, 1)

            def best_two(s):
                wait(dve, a_e, 1, s, 1)
                v.tensor_scalar(ez1[:, :], ez[:, :], 1.0, None, ALU.add).then_inc(v_rt, 1)
                wait(dve, v_rt, RT, s, 1)
                v.reciprocal(score[:, :, :], ez1[:, :].rearrange("p (u e) -> p u e", u=2)).then_inc(v_rt, 1)
                wait(dve, v_rt, RT, s, 2, plain=True)
                for u in range(2):
                    v.max(top[:, u, :], score[:, u, :]).then_inc(v_rt, 1)
                wait(dve, v_rt, RT, s, 4, plain=True)
                for u in range(2):
                    v.max_index(topi[:, u, :], top[:, u, :], score[:, u, :]).then_inc(v_rt, 1)
                v.tensor_tensor(den[:, :], top[:, :, 0], top[:, :, 1], ALU.add).then_inc(v_rt, 1)

            def choice(s):
                wait(dve, v_rt, RT, s, 7)
                v.tensor_copy(topf[:, :, :], topi[:, :, 0:TOPK]).then_inc(v_rt, 1)
                v.tensor_scalar(den1[:, :], den[:, :], 1e-20, None, ALU.add).then_inc(v_rt, 1)
                wait(dve, v_rt, RT, s, 9)
                v.tensor_tensor(hot[:, :, :, :].rearrange("p u k e -> p (u k) e"),
                                iota_e[:, :].unsqueeze(1).to_broadcast([P, 2 * TOPK, E]),
                                topf[:, :, :].rearrange("p u k -> p (u k)").unsqueeze(2)
                                .to_broadcast([P, 2 * TOPK, E]), ALU.is_equal).then_inc(v_rt, 1)
                v.reciprocal(rden[:, :], den1[:, :]).then_inc(v_rt, 1)
                wait(dve, v_rt, RT, s, 11)
                wait_par(dve, d_scat, SCAT, s.plus(-2))
                v.tensor_tensor(hots[:, :, :], hot[:, :, 0, :], hot[:, :, 1, :], ALU.add).then_inc(v_hot, 1)
                v.scalar_tensor_tensor(
                    tag[s.par()][:, :, 1].rearrange("p (u k) -> p u k", u=2), top[:, :, 0:TOPK],
                    ROUTE_SCALE, rden[:, :].unsqueeze(2).to_broadcast([P, 2, TOPK]), ALU.mult,
                    ALU.mult).then_inc(v_rt, 1)

            def places(s):
                tot = M1[:, 4 * E:6 * E].rearrange("p (u e) -> p u e", u=2)
                wait(dve, p_pf, 1, s, 1)
                wait(dve, a_e, 1, s.plus(1), 1, last=NS)
                v.tensor_tensor(base[:, 1, :], base[:, 0, :], tot[:, 0, :], ALU.add).then_inc(v_ps, 1)
                wait(dve, v_ps, 3, s, 1)
                v.tensor_tensor(pb[:, :, :], M1[:, 2 * E:4 * E].rearrange("p (u e) -> p u e", u=2), base[:, :, :],
                                ALU.add).then_inc(v_ps, 1)
                wait(dve, v_ps, 3, s, 2)
                v.tensor_tensor(base[:, 0, :], base[:, 1, :], tot[:, 1, :], ALU.add).then_inc(v_pf, 1)
                v.tensor_tensor(hotp[:, :, :, :], hot[:, :, :, :],
                                pb[:, :, :].unsqueeze(2).to_broadcast([P, 2, TOPK, E]), ALU.mult).then_inc(v_ps, 1)

            def positions(s):
                wait(dve, v_ps, 3, s, 3)
                v.tensor_reduce(posf[:, :], hotp[:, :, :, :].rearrange("p u k e -> p (u k) e"), AX.X,
                                ALU.add).then_inc(v_w, 1)
                wait(dve, v_w, 1, s, 1)
                wait(dve, v_pf, 1, s, 1)
                wait_par(dve, d_scat, SCAT, s.plus(-2))
                v.tensor_copy(posi[s.par()][:, :], posf[:, :]).then_inc(v_pos, 1)

            def step(it):
                a, b, d, ln, r = it.plus(2), it.plus(1), it.plus(-1), it.plus(3), it.plus(-2)
                do_a, do_b, do_d, do_ln, do_r = (a.is_in(0, NS), b.is_in(0, NS), d.is_in(0, NS), ln.is_in(0, NS),
                                                 r.is_in(0, NS))
                for k in range(NCH):
                    if k == 0 and do_r:
                        best_two(r)
                    if k == 1 and do_a:
                        turned_low(a, M1[:, :], a_x, xnT, v_xl)
                    if k == 3 and do_a:
                        turned_low(a, c_in[:, :, :].rearrange("p k t -> p (k t)"), a_c, cT[a.par()], v_cl)
                    if k == 1 and do_d:
                        combine(d, 3)
                    if k == 2 and do_r:
                        choice(r)
                    if k == 3 and do_d:
                        wait(dve, g_x2, 4, d, 4)
                        stats(d, x2[d.par()], bs2, mv2, ve2, v_b2, v_s2, v_h2)
                    if k == 4 and do_a:
                        rest(a, M0, a_q, qp, q_rest, g_qs, v_q)
                    if k == 5 and do_a:
                        rest(a, M1, a_k, kp, k_rest, g_ks, v_k)
                    if do_b:
                        for n in MAX_SLOTS.get(k, ()):
                            reduce_max(b, n)
                    if k == 4 and do_d:
                        wait_par(dve, d_scat, SCAT, d.plus(-2))
                        if d.k is not None or d.off >= 2:
                            wait(dve, p_hT, 1, d.plus(-1))
                        norm(d, x2[d.par()], mv2, h2[d.par()], g_r2, v_h2)
                        v.tensor_copy(mv_all[:, bass.ds(d.idx(), 1), :].rearrange("p g c -> p (g c)"),
                                      mv2[:, :, :].rearrange("p u c -> p (u c)")).then_inc(v_all, 1)
                    if k in (6, 11, 13) and it.is_in(0, NS):
                        combine(it, (6, 11, 13).index(k))
                    if k == 7 and do_ln:
                        wait(dve, d_x, 16, ln, 16)
                        stats(ln, x_in, bs1, mv1, ve1, v_b1, v_s1, v_xn)
                    if k == 8 and do_ln:
                        wait(dve, p_xT, 1, ln)
                        norm(ln, x_in, mv1, xn, g_r1, v_xn)
                    if k == 9 and do_r:
                        places(r)
                    if k == 10 and do_r:
                        positions(r)

            steps(dve, step)

            n_tab = [0]

            def tab(ins):
                ins.then_inc(v_tab, 1)
                n_tab[0] += 1
                dve.wait_ge(v_tab, n_tab[0])

            dve.wait_ge(v_pf, NS)
            tab(v.tensor_tensor(count[:, :], base[:, 0, :], cap_e[:, :], ALU.subtract))
            tab(v.tensor_scalar(full[:, :], count[0:1, :], float(CAP - P), None, ALU.is_gt))
            tab(v.scalar_tensor_tensor(room[:, :], full[:, :], float(1 << 20), base[0:1, 0, :], ALU.mult, ALU.add))
            tab(v.tensor_reduce(least[:, :], room[:, :], AX.X, ALU.min))
            tab(v.scalar_tensor_tensor(room[:, :], base[0:1, 0, :], least[:, 0:1], full[:, :], ALU.subtract,
                                       ALU.mult))
            tab(v.tensor_tensor(pad_f[:, :], base[0:1, 0, :], room[:, :], ALU.subtract))
            v.tensor_copy(pad_tab[:, :], pad_f[:, :]).then_inc(v_row, 1)
            dve.wait_ge(p_tab, 1)
            tab(v.tensor_scalar(tiles_n[:, :], M0[0:E, 0:1], float(P - 1), None, ALU.add))
            tab(v.tensor_copy(tiles_i[:, :], tiles_n[:, :]))
            tab(v.tensor_scalar(tiles_s[:, :], tiles_i[:, :], 7, None, ALU.logical_shift_right))
            tab(v.tensor_copy(tiles_n[:, :], tiles_s[:, :]))
            tab(v.tensor_scalar(one_skip[:, 1:2], tiles_n[:, :], float(-P), float(CAP), ALU.mult, ALU.add))
            dve.wait_ge(p_tab, 2)
            tab(v.tensor_copy(last_t[:, :], M1[0:E, 0:1]))
            tab(v.tensor_scalar(past[:, :], iota_t[:, :], last_t[:, 0:1], None, ALU.is_ge))
            dve.wait_ge(p_tab, 3)
            v.tensor_scalar(expert_tab[:, :], M0[0:1, 0:NT], float(E - 1), None, ALU.min).then_inc(v_row, 1)
            tab(v.scalar_tensor_tensor(row_f[:, :], iota_t[0:1, :], float(P), M1[0:1, 0:NT], ALU.mult, ALU.add))
            tab(v.tensor_scalar(past[0:1, :], row_f[:, :], float(E * CAP), None, ALU.is_ge))
            tab(v.scalar_tensor_tensor(row_d[:, :], row_f[:, :], pad_f[:, 0:1], past[0:1, :], ALU.subtract,
                                       ALU.mult))
            v.tensor_tensor(row_tab[:, :], row_f[:, :], row_d[:, :], ALU.subtract).then_inc(v_row, 1)

            for n, (weights, low, high) in enumerate(pieces):
                dve.wait_ge(a_wh, n + 1)
                v.tensor_tensor(rnd(low), weights, high, ALU.subtract).then_inc(v_wl, 1)

            def rows_low(ph, n, j):
                t = j.plus(2)
                if t.is_in(0, n):
                    wait(dve, a_tp[ph], 1, t, 1)
                    v.tensor_tensor(rnd(rows_T[t.off % 2][:, 1, :]), tp_ps[t.off % 2][:, 0:D],
                                    rows_T[t.off % 2][:, 0, :], ALU.subtract).then_inc(v_tl[ph], 1)

            def hidden_low(ph, n, j):
                t = j
                if t.is_in(0, n):
                    wait(dve, a_hT[ph], 1, t, 1)
                    v.tensor_tensor(rnd(hid_T[t.off % 2][:, 1, :]), hp_ps[t.off % 2][:, 0:P],
                                    hid_T[t.off % 2][:, 0, :], ALU.subtract).then_inc(v_hl[ph], 1)

            def hidden(ph, n, j):
                t = j.plus(1)
                if t.is_in(0, n):
                    wait(dve, a_gate[ph], 1, t, 1)
                    v.tensor_tensor(hid[t.off % 2][:, :], gate[t.off % 2][:, :], gu_ps[t.off % 2][:, HID:2 * HID],
                                    ALU.mult).then_inc(v_hid[ph], 1)

            def expert_step(j):
                rows_low(0, NT, j)
                hidden(0, NT, j)
                hidden_low(0, NT, j)
                t = j.plus(-1)
                if t.is_in(0, NT):
                    wait(dve, p_eo[0], 1, t, 1)
                    wait_par(dve, d_eo, 16, t.plus(-4))
                    wait_par(dve, d_tag, 16, t)
                    v.tensor_scalar(res[t.off % 4][:, :], eo_ps[t.off % 2][:, 0:D], row_tag[t.off % 16][:, 1:2],
                                    None, ALU.mult).then_inc(v_res[0], 1)

            expert_steps(dve, expert_step)

            dve.wait_ge(v_all, NS)

            def token_step(j):
                t = j.plus(4)
                if t.is_in(0, NB) and t.off % 2 == 0:
                    grp = t.off // 2 if t.k is None else t.k * (t.unroll // 2) + t.off // 2
                    v.tensor_copy(mv3[t.off // 2 % 2][:, :],
                                  mv_all[:, bass.ds(grp, 1), :].rearrange("p g c -> p (g c)")).then_inc(v_s3, 2)
                t = j.plus(3)
                if t.is_in(0, NB):
                    wait_par(dve, d_tok, 16, t.pair())
                    wait(dve, v_s3, 1, t, 1)
                    mv, c = mv3[t.off // 2 % 2], 2 * (t.off % 2)
                    v.tensor_scalar(h3[t.off % 2][:, :], tok_in[t.off % 8][:, :], mv[:, c:c + 1], mv[:, c + 1:c + 2],
                                    ALU.subtract, ALU.mult).then_inc(v_h3, 1)
                rows_low(1, NB, j)
                hidden(1, NB, j)
                hidden_low(1, NB, j)
                t = j.plus(-1)
                if t.is_in(0, NB):
                    wait(dve, g_a1, 1, t, 2 - t.off % 2)
                    wait(dve, p_eo[1], 1, t, 1)
                    wait_par(dve, d_out, 16, t.plus(-4).pair())
                    if t.k is None and t.off < 4:
                        dve.wait_ge(d_eo[t.off], 16 * (NT // 4))
                    v.tensor_tensor(res[t.off % 4][:, :], eo_ps[t.off % 2][:, 0:D], acc_pair[t.off // 2 % 2][:, t.off % 2, :],
                                    ALU.add).then_inc(v_res[1], 1)

            token_steps(dve, token_step)

        @block.gpsimd
        def _(gp):
            g = nc.gpsimd
            n = 0
            for ins in ([g.memset(ident[:, :], 0.0), g.memset(identb[:, :], 0.0), g.memset(upper[:, :], 1.0),
                         g.memset(onesb[:, :], 1.0), g.memset(neghalf[:, :], -0.5), g.memset(coef[:, :], 1.0),
                         g.memset(zeros[:, :], 0.0), g.memset(no_tag[:, :], 0.0), g.memset(upto[:, :], 1.0),
                         g.memset(one_skip[:, :], 1.0)]):
                ins.then_inc(g_set, 1)
                n += 1
            gp.wait_ge(g_set, n)
            for m in (ident, identb):
                g.affine_select(out=m[:, :], in_=m[:, :], compare_op=ALU.not_equal, fill=1.0, base=0,
                                pattern=[[-1, P]], channel_multiplier=1)
            g.affine_select(out=upper[:, :], in_=upper[:, :], compare_op=ALU.is_gt, fill=0.0, base=0,
                            pattern=[[1, P]], channel_multiplier=-1).then_inc(g_set, 1)
            g.iota(iota_e[:, :], pattern=[[1, E]], base=0, channel_multiplier=0,
                   allow_small_or_imprecise_dtypes=True).then_inc(g_set, 1)
            g.iota(base[:, 0, :], pattern=[[CAP, E]], base=0, channel_multiplier=0,
                   allow_small_or_imprecise_dtypes=True).then_inc(g_set, 1)
            g.iota(cap_e[:, :], pattern=[[CAP, E]], base=0, channel_multiplier=0,
                   allow_small_or_imprecise_dtypes=True).then_inc(g_set, 1)
            g.iota(iota_t[:, :], pattern=[[1, NT]], base=0, channel_multiplier=0,
                   allow_small_or_imprecise_dtypes=True)
            g.iota(number[:, :].rearrange("p (u k) -> p u k", u=2), pattern=[[P * TOPK, 2], [1, TOPK]], base=0,
                   channel_multiplier=TOPK, allow_small_or_imprecise_dtypes=True).then_inc(g_set, 1)
            g.iota(no_tag.bitcast(U32)[:, 0:1], pattern=[[0, 1]], base=TOPK * T,
                   channel_multiplier=0).then_inc(g_set, 1)
            g.affine_select(out=upto[:, :], in_=upto[:, :], compare_op=ALU.is_ge, fill=0.0, base=0,
                            pattern=[[1, E]], channel_multiplier=-1).then_inc(g_set, 1)
            assert n + 7 == SETUP
            for i in range(2):
                g.memset(k_st[i][:, :, :], -1.0).then_inc(g_ones, 1)
            gp.wait_ge(g_set, SETUP)

            def deviation(s, ve, mv, v_s, g_r):
                wait(gp, v_s, 3, s, 3)
                g.tensor_tensor(mv[:, :, 1], ve[:, :], neghalf[:, :], ALU.pow).then_inc(g_r, 1)

            def split(s, tmp, part, v_done, g_b, g_done, landed):
                wait(gp, v_done, 1, s, 1)
                wait(gp, landed, PW, s)
                g.tensor_copy(part[:, 1, :], tmp[:, :]).then_inc(g_b, 1)
                wait(gp, g_b, 1, s, 1)
                g.tensor_tensor(part[:, 2, :], tmp[:, :], part[:, 1, :], ALU.subtract).then_inc(g_done, 1)

            def residual(s, h):
                u, m = divmod(h, 2)
                p = s.par()
                wait(gp, v_cb, 4, s, h + 1)
                wait(gp, g_x2, 4, s, h)
                two = o_sc[h % 2][:, :, :].rearrange("p (h two) d -> p h two d", two=2)
                g.tensor_tensor(att[:, :, :], two[:, :, 0, :], two[:, :, 1, :], ALU.add).then_inc(g_att, 1)
                wait(gp, g_att, 4, s, h + 1)
                if h == 0:
                    wait_par(gp, d_res, 16, s)
                    wait_par(gp, d_x2, 16, s.plus(-2))
                    wait(gp, v_h2, 2, s.plus(-1))
                g.tensor_tensor(x2[p][:, u, m * P:(m + 1) * P].rearrange("p (h d) -> p h d", d=DH), att[:, :, :],
                                x_res[p][:, u, m * P:(m + 1) * P].rearrange("p (h d) -> p h d", d=DH),
                                ALU.add).then_inc(g_x2, 1)

            def numbers(s):
                wait_par(gp, d_scat, SCAT, s.plus(-2))
                wait(gp, g_num, 1, s)
                g.tensor_copy(tag[s.par()].bitcast(U32)[:, :, 0], number[:, :]).then_inc(g_tag, 1)
                wait(gp, g_tag, 1, s, 1)
                g.tensor_scalar(number[:, :], number[:, :], float(TOPK * SW), None, ALU.add).then_inc(g_num, 1)

            def scatter(s, u):
                p = s.par()
                if s.k is None and s.off == 0:
                    gp.wait_ge(d_zero, 32)
                wait(gp, v_pos, 1, s, 1)
                wait(gp, v_h2, 2, s, 2)
                wait(gp, v_rt, RT, s, RT)
                wait(gp, g_tag, 1, s, 1)
                for k in range(TOPK):
                    c = TOPK * u + k
                    g.indirect_dma_start(
                        rows_dram[:, :], bass.IndirectOffsetOnAxis(ap=posi[p][:, c:c + 1], axis=0),
                        h2[p][:, u, :], None).then_inc(d_scat[p], 16)
                    g.indirect_dma_start(
                        tags_dram[:, :], bass.IndirectOffsetOnAxis(ap=posi[p][:, c:c + 1], axis=0),
                        tag[p][:, c, :], None).then_inc(d_scat[p], 16)

            def step(it):
                a, d, ln, r = it.plus(2), it.plus(-1), it.plus(3), it.plus(-2)
                do_c = it.is_in(0, NS)
                if d.is_in(0, NS):
                    residual(d, 3)
                    deviation(d, ve2, mv2, v_s2, g_r2)
                if a.is_in(0, NS):
                    split(a, q_rest, qp, v_q, g_qb, g_qs, d_qw)
                    split(a, k_rest, kp, v_k, g_kb, g_ks, d_kw)
                if do_c:
                    residual(it, 0)
                if ln.is_in(0, NS):
                    deviation(ln, ve1, mv1, v_s1, g_r1)
                if do_c:
                    residual(it, 1)
                if r.is_in(0, NS):
                    numbers(r)
                if r.is_in(0, NS):
                    scatter(r, 0)
                if do_c:
                    residual(it, 2)
                if r.is_in(0, NS):
                    scatter(r, 1)

            steps(gp, step)

            def expert_step(j):
                t = j.plus(-1)
                if t.is_in(0, NT):
                    wait_par(gp, d_tag, 16, t)
                    wait(gp, v_res[0], 1, t, 1)
                    g.indirect_dma_start(routed_dram[:, :], bass.IndirectOffsetOnAxis(
                        ap=row_tag[t.off % 16].bitcast(U32)[:, 0:1], axis=0), res[t.off % 4][:, :], None,
                        bounds_check=TOPK * T - 1, oob_is_err=False).then_inc(d_eo[t.off % 4], 16)

            expert_steps(gp, expert_step)

            def token_step(j):
                t = j
                if t.is_in(0, NB) and t.off % 2 == 0:
                    two = got_pair[t.off // 2 % 4]
                    wait_par(gp, d_got, 16, t.pair())
                    g.tensor_tensor(two[:, :, 0:D], two[:, :, 0:D], two[:, :, D:2 * D], ALU.add).then_inc(g_a0, 2)
                    wait_par(gp, d_tok, 16, t.pair())
                    wait(gp, v_res[1], 1, t, -2)
                    wait(gp, g_a0, 1, t, 2)
                    g.tensor_tensor(acc_pair[t.off // 2 % 2][:, :, :], two[:, :, 0:D],
                                    tok_pair[t.off // 2 % 4][:, :, :], ALU.add).then_inc(g_a1, 2)

            token_steps(gp, token_step)


def kernel(x, ctx_1024, L0_xattn_Wq, L0_xattn_Wk, L0_xattn_Wv, L0_xattn_lambda_q1, L0_xattn_lambda_q2,
           L0_xattn_lambda_k1, L0_xattn_lambda_k2, L0_ffn_gate_w, L0_ffn_w_gate, L0_ffn_w_up, L0_ffn_w_down,
           L0_ffn_ws_gate, L0_ffn_ws_up, L0_ffn_ws_down):
    import numpy as np
    import concourse.bacc as bacc
    from concourse.bass_utils import run_bass_kernel_spmd

    def contract_rows(w):
        w = np.asarray(w)
        return w.reshape(w.shape[0] // P, P, w.shape[1]).transpose(1, 0, 2)

    def dims_first(w):
        w = np.asarray(w).T
        return w.reshape(w.shape[0], 2, SUB // 2, -1).transpose(0, 1, 3, 2).reshape(w.shape)

    def features_first(c):
        b, t, f = np.asarray(c).shape
        return np.asarray(c).reshape(b // 2, 2, t, f // P, P).transpose(0, 4, 3, 1, 2).reshape(b // 2, P, f // P, 2 * t)

    wg, wu = np.asarray(L0_ffn_w_gate), np.asarray(L0_ffn_w_up)
    n_e, dim, hid = wg.shape
    gate_up = np.concatenate([wg, wu], axis=2).reshape(n_e, dim // P, P, 2 * hid).transpose(2, 0, 1, 3)
    down = np.asarray(L0_ffn_w_down).transpose(1, 0, 2)
    laid = {
        "x": x, "ctxT": features_first(ctx_1024), "lq1": L0_xattn_lambda_q1, "lk1": L0_xattn_lambda_k1, "lq2": L0_xattn_lambda_q2,
        "lk2": L0_xattn_lambda_k2, "wqT": contract_rows(dims_first(L0_xattn_Wq)),
        "wkT": contract_rows(dims_first(L0_xattn_Wk)), "wvT": contract_rows(np.asarray(L0_xattn_Wv).T),
        "gate_wT": contract_rows(np.asarray(L0_ffn_gate_w).T), "w_gu": gate_up, "w_dn": down,
        "ws_gu": contract_rows(np.concatenate([np.asarray(L0_ffn_ws_gate), np.asarray(L0_ffn_ws_up)], axis=1)),
        "ws_dn": L0_ffn_ws_down,
    }
    nc = bacc.Bacc("TRN2", target_bir_lowering=False, num_devices=1)
    arrays, args = {}, {}
    for name, a in laid.items():
        a = np.ascontiguousarray(a)
        arrays["in_" + name] = a
        args[name] = nc.dram_tensor("in_" + name, a.shape, mybir.dt.from_np(a.dtype), kind="ExternalInput").ap()
    out = nc.dram_tensor("out", x.shape, F32, kind="ExternalOutput").ap()
    program(nc, out=out, **args)
    r = run_bass_kernel_spmd(nc, [arrays], core_ids=[0])
    return r.results[0]["out"]
```
